# Optimizing a Trainium2 kernel written in Bass

```python
import numpy as np
import jax
import jax.numpy as jnp

def _softmax(x, axis=-1):
    return jax.nn.softmax(x, axis=axis)

def _gelu(x):
    return jax.nn.gelu(x, approximate=True)

def _silu(x):
    return jax.nn.silu(x)

def _sigmoid(x):
    return jax.nn.sigmoid(x)

def _layernorm(x, axis=-1, eps=1e-05):
    m = jnp.mean(x, axis=axis, keepdims=True)
    v = jnp.var(x, axis=axis, keepdims=True)
    return (x - m) / jnp.sqrt(v + eps)

def _scatter_add(tgt, idx, src, axis=0):
    return tgt.at[idx].add(src)

def _segment_sum(src, seg, n):
    return jax.ops.segment_sum(src, seg, n)
kernel_name = 'mk_gnn_preln_d4_gnn_r32_730640'

def setup_inputs(seed: int=0):
    np.random.seed(seed)
    _w = jnp.asarray

    def _rec_inputs():
        import jax
        import jax.numpy as jnp
        _gk = jax.random.key(seed)
        x = -0.000202 + 1 * jax.random.normal(jax.random.fold_in(_gk, 1), (3125, 160), jnp.float32)
        _s = jax.random.randint(jax.random.fold_in(_gk, 2), (50000,), 0, 3125, jnp.int32)
        _d = jax.random.randint(jax.random.fold_in(_gk, 3), (50000,), 0, 3125, jnp.int32)
        _loop = jnp.arange(3125, dtype=jnp.int32)
        src = jnp.concatenate([_s, _d, _loop])
        dst = jnp.concatenate([_d, _s, _loop])
        _o = jnp.argsort(dst, stable=True)
        src = src[_o]
        dst = dst[_o]
        edge_attr_4 = 0.0012443 + 1.0001 * jax.random.normal(jax.random.fold_in(_gk, 12), (103125, 4), jnp.float32)
        edge_attr_64 = 0.000127647 + 1.00004 * jax.random.normal(jax.random.fold_in(_gk, 13), (103125, 64), jnp.float32)
        edge_attr_8 = jax.random.uniform(jax.random.fold_in(_gk, 14), (103125, 8), jnp.float32, 0.0, 1)
        node_vec1 = jax.random.uniform(jax.random.fold_in(_gk, 16), (3125, 1), jnp.float32, 0.0, 1)
        return (x, src, dst, edge_attr_4, edge_attr_64, edge_attr_8, node_vec1)
    x, src, dst, edge_attr_4, edge_attr_64, edge_attr_8, node_vec1 = _rec_inputs()

    def _L0_gnn_setup():
        import jax, jax.numpy as jnp
        import numpy as np
        N, E = (1250, 20000)
        S_IN, V_IN = (64, 32)
        S_MID, V_MID = (96, 128)
        S_OUT, V_OUT = (96, 32)
        R = 64
        FC_HID = 64
        W_NUMEL = 64 + 64 + 32 + 32 + 32
        NUM_NEIGHBORS = 16.0

        def _inv(d):
            return 1.0 / jnp.sqrt(jnp.float32(d))

        def _forward(node_features, node_attr, edge_attr, edge_scalars, lin1_ws, lin1_wv, fc_w1, fc_w2, sc_ws, sc_wv, lin2_ws, lin2_wv, edge_src, edge_dst):
            n = node_features.shape[0]
            s = node_features[:, :S_IN]
            v = node_features[:, S_IN:].reshape(n, V_IN, 3)
            a = node_attr
            sc_s = s @ sc_ws * a * _inv(S_IN)
            sc_v = jnp.einsum('nci,cd->ndi', v, sc_wv) * a[:, :, None] * _inv(V_IN)
            h_s = s @ lin1_ws * a * _inv(S_IN)
            h_v = jnp.einsum('nci,cd->ndi', v, lin1_wv) * a[:, :, None] * _inv(V_IN)
            hid = jax.nn.silu(edge_scalars @ fc_w1 * _inv(R))
            w = hid @ fc_w2 * _inv(FC_HID)
            w1, w2, w3, w4, w5 = jnp.split(w, [64, 128, 160, 192], axis=-1)
            es = h_s[edge_src]
            ev = h_v[edge_src]
            e0 = edge_attr[:, :1]
            e1 = edge_attr[:, 1:4]
            m_s1 = w1 * es * e0
            m_s2 = w4 * jnp.einsum('eci,ei->ec', ev, e1) * _inv(3)
            m_v1 = (w2 * es)[:, :, None] * e1[:, None, :]
            m_v2 = w3[:, :, None] * ev * e0[:, :, None]
            m_v3 = w5[:, :, None] * jnp.cross(ev, e1[:, None, :]) * _inv(2)
            mid_s = jnp.concatenate([m_s1, m_s2], axis=-1)
            mid_v = jnp.concatenate([m_v1, m_v2, m_v3], axis=1)
            inv_nn = 1.0 / jnp.sqrt(jnp.float32(NUM_NEIGHBORS))
            agg_s = jax.ops.segment_sum(mid_s, edge_dst, num_segments=n) * inv_nn
            agg_v = jax.ops.segment_sum(mid_v, edge_dst, num_segments=n) * inv_nn
            o_s = agg_s @ lin2_ws * a * _inv(S_MID)
            o_v = jnp.einsum('nci,cd->ndi', agg_v, lin2_wv) * a[:, :, None] * _inv(V_MID)
            pre_s = sc_s + o_s
            pre_v = sc_v + o_v
            scalars = jax.nn.silu(pre_s[:, :64])
            gates = jax.nn.sigmoid(pre_s[:, 64:96])
            gated = gates[:, :, None] * pre_v
            return jnp.concatenate([scalars, gated.reshape(n, 3 * V_OUT)], axis=-1)
        key = jax.random.key(seed)
        ks = jax.random.split(key, 13)
        return {'node_features': jax.random.normal(ks[0], (N, S_IN + 3 * V_IN), jnp.float32), 'node_attr': jnp.ones((N, 1), jnp.float32), 'edge_src': jax.random.randint(ks[1], (E,), 0, N), 'edge_dst': jax.random.randint(ks[2], (E,), 0, N), 'edge_attr': jax.random.normal(ks[3], (E, 4), jnp.float32), 'edge_scalars': jax.random.normal(ks[4], (E, R), jnp.float32), 'lin1_ws': jax.random.normal(ks[5], (S_IN, S_IN), jnp.float32), 'lin1_wv': jax.random.normal(ks[6], (V_IN, V_IN), jnp.float32), 'fc_w1': jax.random.normal(ks[7], (R, FC_HID), jnp.float32), 'fc_w2': jax.random.normal(ks[8], (FC_HID, W_NUMEL), jnp.float32), 'sc_ws': jax.random.normal(ks[9], (S_IN, S_OUT), jnp.float32), 'sc_wv': jax.random.normal(ks[10], (V_IN, V_OUT), jnp.float32), 'lin2_ws': jax.random.normal(ks[11], (S_MID, S_OUT), jnp.float32), 'lin2_wv': jax.random.normal(ks[12], (V_MID, V_OUT), jnp.float32)}
    _L0_gnn_all = _L0_gnn_setup()
    _L0_gnn_in = {k: v for k, v in _L0_gnn_all.items() if k in ('lin1_ws', 'lin1_wv', 'fc_w1', 'fc_w2', 'sc_ws', 'sc_wv', 'lin2_ws', 'lin2_wv')}
    del _L0_gnn_all

    def _L1_gnn_setup():
        import jax, jax.numpy as jnp
        import numpy as np
        N, E = (50000, 25000)
        MUL0, MUL1 = (64, 32)
        D = MUL0 + 3 * MUL1
        INV3 = float(1.0 / np.sqrt(3.0))
        INV6 = float(1.0 / np.sqrt(6.0))
        C0 = float(1.0 / np.sqrt(MUL0 + MUL1))
        C1 = float(np.sqrt(3.0 / (MUL0 + 2 * MUL1)))
        LIN_S = float(1.0 / np.sqrt(MUL0))
        LIN_V = float(1.0 / np.sqrt(MUL1))
        key = jax.random.key(seed)
        ks = jax.random.split(key, 10)
        x = jax.random.normal(ks[0], (N, D), dtype=jnp.float32)
        sh = jax.random.normal(ks[1], (E, 4), dtype=jnp.float32)
        edge_index = jax.random.randint(ks[2], (2, E), 0, N, dtype=jnp.int64)
        W1 = jax.random.normal(ks[3], (MUL0, MUL0), dtype=jnp.float32)
        W2 = jax.random.normal(ks[4], (MUL1, MUL0), dtype=jnp.float32)
        W3 = jax.random.normal(ks[5], (MUL0, MUL1), dtype=jnp.float32)
        W4 = jax.random.normal(ks[6], (MUL1, MUL1), dtype=jnp.float32)
        W5 = jax.random.normal(ks[7], (MUL1, MUL1), dtype=jnp.float32)
        Ws = jax.random.normal(ks[8], (MUL0, MUL0), dtype=jnp.float32)
        Wv = jax.random.normal(ks[9], (MUL1, MUL1), dtype=jnp.float32)
        return {'x': x, 'sh': sh, 'W1': W1, 'W2': W2, 'W3': W3, 'W4': W4, 'W5': W5, 'Ws': Ws, 'Wv': Wv, 'edge_index': edge_index}
    _L1_gnn_all = _L1_gnn_setup()
    _L1_gnn_in = {k: v for k, v in _L1_gnn_all.items() if k in ('W1', 'W2', 'W3', 'W4', 'W5', 'Ws', 'Wv')}
    del _L1_gnn_all

    def _L2_gnn_setup():
        import jax, jax.numpy as jnp
        import numpy as np
        N = 1250
        E = 12500
        MUL0, MUL1 = (64, 32)
        RAD, HID = (8, 64)
        WNUM = 192
        NUM_NEIGHBORS = 10.0
        INV3 = 1.0 / np.sqrt(3.0)

        def _lin(s, v, Ws, Wv, attr):
            out_s = s @ Ws * attr * (1.0 / np.sqrt(Ws.shape[0]))
            out_v = jnp.einsum('nud,uv->nvd', v, Wv) * attr[..., None] * (1.0 / np.sqrt(Wv.shape[0]))
            return (out_s, out_v)
        key = jax.random.key(seed)
        ks = jax.random.split(key, 16)
        return {'node_input': jax.random.normal(ks[0], (N, MUL0 + 3 * MUL1), jnp.float32), 'node_attr': jnp.ones((N, 1), jnp.float32), 'edge_attr': jax.random.normal(ks[1], (E, 4), jnp.float32), 'edge_scalars': jax.random.uniform(ks[2], (E, RAD), jnp.float32), 'W_sc_s': jax.random.normal(ks[3], (MUL0, MUL0), jnp.float32), 'W_sc_v': jax.random.normal(ks[4], (MUL1, MUL1), jnp.float32), 'W1_s': jax.random.normal(ks[5], (MUL0, MUL0), jnp.float32), 'W1_v': jax.random.normal(ks[6], (MUL1, MUL1), jnp.float32), 'W2_s': jax.random.normal(ks[7], (MUL0 + MUL1, MUL0), jnp.float32), 'W2_v': jax.random.normal(ks[8], (MUL0 + MUL1, MUL1), jnp.float32), 'W3': jax.random.normal(ks[9], (MUL0 + MUL1, 1), jnp.float32), 'fcW1': jax.random.normal(ks[10], (RAD, HID), jnp.float32), 'fcW2': jax.random.normal(ks[11], (HID, WNUM), jnp.float32), 'edge_src': jax.random.randint(ks[12], (E,), 0, N, jnp.int32), 'edge_dst': jax.random.randint(ks[13], (E,), 0, N, jnp.int32)}
    _L2_gnn_all = _L2_gnn_setup()
    _L2_gnn_in = {k: v for k, v in _L2_gnn_all.items() if k in ('W_sc_s', 'W_sc_v', 'W1_s', 'W1_v', 'W2_s', 'W2_v', 'W3', 'fcW1', 'fcW2')}
    del _L2_gnn_all

    def _L3_gnn_setup():
        import jax, jax.numpy as jnp
        import numpy as np
        N_NODES, N_EDGES = (50000, 12500)
        D, SPLIT, EA, H = (128, 32, 64, 256)
        IN = D + EA
        EPS = 1e-05
        SLOPE = 0.01

        def _ln(x, g, b):
            m = x.mean(-1, keepdims=True)
            v = ((x - m) ** 2).mean(-1, keepdims=True)
            return (x - m) * jax.lax.rsqrt(v + EPS) * g + b

        def _block(x, w, b, g, be):
            return jax.nn.relu(_ln(x @ w + b, g, be))

        def _masked_softmax(logits, mask):
            z = jnp.where(mask, logits, -jnp.inf)
            z = z - jnp.max(z, axis=0, keepdims=True)
            e = jnp.where(mask, jnp.exp(z), 0.0)
            return e / jnp.sum(e, axis=0, keepdims=True)

        def _forward(x, edge_index, edge_attr, w_att, b_att, d2t_w1, d2t_b1, d2t_g1, d2t_be1, d2t_w2, d2t_b2, d2t_g2, d2t_be2, t2d_w1, t2d_b1, t2d_g1, t2d_be1, t2d_w2, t2d_b2, t2d_g2, t2d_be2, node_w, node_b, node_g, node_be, self_w, self_b, self_g, self_be):
            x_split = x[:, D:]
            xn = x[:, :D]
            row, col = (edge_index[0], edge_index[1])
            n = xn.shape[0]
            concat = jnp.concatenate([xn[col], xn[row]], axis=-1)
            logits = jax.nn.leaky_relu(concat @ w_att + b_att, SLOPE)
            flow_in = jnp.concatenate([xn[col], edge_attr], axis=-1)

            def direction(mask, w1, b1, g1, be1, w2, b2, g2, be2):
                attn = _masked_softmax(logits, mask[:, None])
                h = attn * flow_in
                h = _block(h, w1, b1, g1, be1)
                h = _block(h, w2, b2, g2, be2)
                h = jnp.where(mask[:, None], h, 0.0)
                return jax.ops.segment_sum(h, row, num_segments=n)
            flow_d2t = direction(row < col, d2t_w1, d2t_b1, d2t_g1, d2t_be1, d2t_w2, d2t_b2, d2t_g2, d2t_be2)
            flow_t2d = direction(row > col, t2d_w1, t2d_b1, t2d_g1, t2d_be1, t2d_w2, t2d_b2, t2d_g2, t2d_be2)
            flow_total = jnp.concatenate([flow_t2d, flow_d2t], axis=1)
            upd = _block(flow_total, node_w, node_b, node_g, node_be)
            upd = upd + _block(xn, self_w, self_b, self_g, self_be)
            return jnp.concatenate([upd, x_split], axis=1)
        key = jax.random.key(seed)
        ks = jax.random.split(key, 24)

        def lin(k, fi, fo):
            kw, kb = jax.random.split(k)
            return (jax.random.normal(kw, (fi, fo), jnp.float32) / np.float32(np.sqrt(fi)), jax.random.normal(kb, (fo,), jnp.float32) * 0.02)

        def lnp(k, d):
            kg, kb = jax.random.split(k)
            return (1.0 + 0.05 * jax.random.normal(kg, (d,), jnp.float32), 0.05 * jax.random.normal(kb, (d,), jnp.float32))
        inp = {}
        inp['x'] = jax.random.normal(ks[0], (N_NODES, D + SPLIT), jnp.float32)
        inp['edge_index'] = jax.random.randint(ks[1], (2, N_EDGES), 0, N_NODES)
        inp['edge_attr'] = jax.random.normal(ks[2], (N_EDGES, EA), jnp.float32)
        inp['w_att'], inp['b_att'] = lin(ks[3], 2 * D, 1)
        for pre, off in (('d2t', 4), ('t2d', 10)):
            inp[pre + '_w1'], inp[pre + '_b1'] = lin(ks[off], IN, H)
            inp[pre + '_g1'], inp[pre + '_be1'] = lnp(ks[off + 1], H)
            inp[pre + '_w2'], inp[pre + '_b2'] = lin(ks[off + 2], H, D)
            inp[pre + '_g2'], inp[pre + '_be2'] = lnp(ks[off + 3], D)
        inp['node_w'], inp['node_b'] = lin(ks[16], 2 * D, D)
        inp['node_g'], inp['node_be'] = lnp(ks[17], D)
        inp['self_w'], inp['self_b'] = lin(ks[18], D, D)
        inp['self_g'], inp['self_be'] = lnp(ks[19], D)
        return inp
    _L3_gnn_all = _L3_gnn_setup()
    _L3_gnn_in = {k: v for k, v in _L3_gnn_all.items() if k in ('w_att', 'b_att', 'd2t_w1', 'd2t_b1', 'd2t_g1', 'd2t_be1', 'd2t_w2', 'd2t_b2', 'd2t_g2', 'd2t_be2', 't2d_w1', 't2d_b1', 't2d_g1', 't2d_be1', 't2d_w2', 't2d_b2', 't2d_g2', 't2d_be2', 'node_w', 'node_b', 'node_g', 'node_be', 'self_w', 'self_b', 'self_g', 'self_be')}
    del _L3_gnn_all
    return {'x': x, 'src': src, 'dst': dst, 'edge_attr_4': edge_attr_4, 'edge_attr_64': edge_attr_64, 'edge_attr_8': edge_attr_8, 'node_vec1': node_vec1, 'L0_gnn_lin1_ws': _L0_gnn_in['lin1_ws'], 'L0_gnn_lin1_wv': _L0_gnn_in['lin1_wv'], 'L0_gnn_fc_w1': _L0_gnn_in['fc_w1'], 'L0_gnn_fc_w2': _L0_gnn_in['fc_w2'], 'L0_gnn_sc_ws': _L0_gnn_in['sc_ws'], 'L0_gnn_sc_wv': _L0_gnn_in['sc_wv'], 'L0_gnn_lin2_ws': _L0_gnn_in['lin2_ws'], 'L0_gnn_lin2_wv': _L0_gnn_in['lin2_wv'], 'L1_gnn_W1': _L1_gnn_in['W1'], 'L1_gnn_W2': _L1_gnn_in['W2'], 'L1_gnn_W3': _L1_gnn_in['W3'], 'L1_gnn_W4': _L1_gnn_in['W4'], 'L1_gnn_W5': _L1_gnn_in['W5'], 'L1_gnn_Ws': _L1_gnn_in['Ws'], 'L1_gnn_Wv': _L1_gnn_in['Wv'], 'L2_gnn_W_sc_s': _L2_gnn_in['W_sc_s'], 'L2_gnn_W_sc_v': _L2_gnn_in['W_sc_v'], 'L2_gnn_W1_s': _L2_gnn_in['W1_s'], 'L2_gnn_W1_v': _L2_gnn_in['W1_v'], 'L2_gnn_W2_s': _L2_gnn_in['W2_s'], 'L2_gnn_W2_v': _L2_gnn_in['W2_v'], 'L2_gnn_W3': _L2_gnn_in['W3'], 'L2_gnn_fcW1': _L2_gnn_in['fcW1'], 'L2_gnn_fcW2': _L2_gnn_in['fcW2'], 'L3_gnn_w_att': _L3_gnn_in['w_att'], 'L3_gnn_b_att': _L3_gnn_in['b_att'], 'L3_gnn_d2t_w1': _L3_gnn_in['d2t_w1'], 'L3_gnn_d2t_b1': _L3_gnn_in['d2t_b1'], 'L3_gnn_d2t_g1': _L3_gnn_in['d2t_g1'], 'L3_gnn_d2t_be1': _L3_gnn_in['d2t_be1'], 'L3_gnn_d2t_w2': _L3_gnn_in['d2t_w2'], 'L3_gnn_d2t_b2': _L3_gnn_in['d2t_b2'], 'L3_gnn_d2t_g2': _L3_gnn_in['d2t_g2'], 'L3_gnn_d2t_be2': _L3_gnn_in['d2t_be2'], 'L3_gnn_t2d_w1': _L3_gnn_in['t2d_w1'], 'L3_gnn_t2d_b1': _L3_gnn_in['t2d_b1'], 'L3_gnn_t2d_g1': _L3_gnn_in['t2d_g1'], 'L3_gnn_t2d_be1': _L3_gnn_in['t2d_be1'], 'L3_gnn_t2d_w2': _L3_gnn_in['t2d_w2'], 'L3_gnn_t2d_b2': _L3_gnn_in['t2d_b2'], 'L3_gnn_t2d_g2': _L3_gnn_in['t2d_g2'], 'L3_gnn_t2d_be2': _L3_gnn_in['t2d_be2'], 'L3_gnn_node_w': _L3_gnn_in['node_w'], 'L3_gnn_node_b': _L3_gnn_in['node_b'], 'L3_gnn_node_g': _L3_gnn_in['node_g'], 'L3_gnn_node_be': _L3_gnn_in['node_be'], 'L3_gnn_self_w': _L3_gnn_in['self_w'], 'L3_gnn_self_b': _L3_gnn_in['self_b'], 'L3_gnn_self_g': _L3_gnn_in['self_g'], 'L3_gnn_self_be': _L3_gnn_in['self_be']}

def reference(x, src, dst, edge_attr_4, edge_attr_64, edge_attr_8, node_vec1, L0_gnn_lin1_ws, L0_gnn_lin1_wv, L0_gnn_fc_w1, L0_gnn_fc_w2, L0_gnn_sc_ws, L0_gnn_sc_wv, L0_gnn_lin2_ws, L0_gnn_lin2_wv, L1_gnn_W1, L1_gnn_W2, L1_gnn_W3, L1_gnn_W4, L1_gnn_W5, L1_gnn_Ws, L1_gnn_Wv, L2_gnn_W_sc_s, L2_gnn_W_sc_v, L2_gnn_W1_s, L2_gnn_W1_v, L2_gnn_W2_s, L2_gnn_W2_v, L2_gnn_W3, L2_gnn_fcW1, L2_gnn_fcW2, L3_gnn_w_att, L3_gnn_b_att, L3_gnn_d2t_w1, L3_gnn_d2t_b1, L3_gnn_d2t_g1, L3_gnn_d2t_be1, L3_gnn_d2t_w2, L3_gnn_d2t_b2, L3_gnn_d2t_g2, L3_gnn_d2t_be2, L3_gnn_t2d_w1, L3_gnn_t2d_b1, L3_gnn_t2d_g1, L3_gnn_t2d_be1, L3_gnn_t2d_w2, L3_gnn_t2d_b2, L3_gnn_t2d_g2, L3_gnn_t2d_be2, L3_gnn_node_w, L3_gnn_node_b, L3_gnn_node_g, L3_gnn_node_be, L3_gnn_self_w, L3_gnn_self_b, L3_gnn_self_g, L3_gnn_self_be):
    import jax
    import jax.numpy as jnp

    def _L0_gnn_ref(node_features, node_attr, edge_src, edge_dst, edge_attr, edge_scalars, lin1_ws, lin1_wv, fc_w1, fc_w2, sc_ws, sc_wv, lin2_ws, lin2_wv):
        import jax, jax.numpy as jnp
        import numpy as np
        N, E = (1250, 20000)
        S_IN, V_IN = (64, 32)
        S_MID, V_MID = (96, 128)
        S_OUT, V_OUT = (96, 32)
        R = 64
        FC_HID = 64
        W_NUMEL = 64 + 64 + 32 + 32 + 32
        NUM_NEIGHBORS = 16.0

        def _inv(d):
            return 1.0 / jnp.sqrt(jnp.float32(d))

        def _forward(node_features, node_attr, edge_attr, edge_scalars, lin1_ws, lin1_wv, fc_w1, fc_w2, sc_ws, sc_wv, lin2_ws, lin2_wv, edge_src, edge_dst):
            n = node_features.shape[0]
            s = node_features[:, :S_IN]
            v = node_features[:, S_IN:].reshape(n, V_IN, 3)
            a = node_attr
            sc_s = s @ sc_ws * a * _inv(S_IN)
            sc_v = jnp.einsum('nci,cd->ndi', v, sc_wv) * a[:, :, None] * _inv(V_IN)
            h_s = s @ lin1_ws * a * _inv(S_IN)
            h_v = jnp.einsum('nci,cd->ndi', v, lin1_wv) * a[:, :, None] * _inv(V_IN)
            hid = jax.nn.silu(edge_scalars @ fc_w1 * _inv(R))
            w = hid @ fc_w2 * _inv(FC_HID)
            w1, w2, w3, w4, w5 = jnp.split(w, [64, 128, 160, 192], axis=-1)
            es = h_s[edge_src]
            ev = h_v[edge_src]
            e0 = edge_attr[:, :1]
            e1 = edge_attr[:, 1:4]
            m_s1 = w1 * es * e0
            m_s2 = w4 * jnp.einsum('eci,ei->ec', ev, e1) * _inv(3)
            m_v1 = (w2 * es)[:, :, None] * e1[:, None, :]
            m_v2 = w3[:, :, None] * ev * e0[:, :, None]
            m_v3 = w5[:, :, None] * jnp.cross(ev, e1[:, None, :]) * _inv(2)
            mid_s = jnp.concatenate([m_s1, m_s2], axis=-1)
            mid_v = jnp.concatenate([m_v1, m_v2, m_v3], axis=1)
            inv_nn = 1.0 / jnp.sqrt(jnp.float32(NUM_NEIGHBORS))
            agg_s = jax.ops.segment_sum(mid_s, edge_dst, num_segments=n) * inv_nn
            agg_v = jax.ops.segment_sum(mid_v, edge_dst, num_segments=n) * inv_nn
            o_s = agg_s @ lin2_ws * a * _inv(S_MID)
            o_v = jnp.einsum('nci,cd->ndi', agg_v, lin2_wv) * a[:, :, None] * _inv(V_MID)
            pre_s = sc_s + o_s
            pre_v = sc_v + o_v
            scalars = jax.nn.silu(pre_s[:, :64])
            gates = jax.nn.sigmoid(pre_s[:, 64:96])
            gated = gates[:, :, None] * pre_v
            return jnp.concatenate([scalars, gated.reshape(n, 3 * V_OUT)], axis=-1)
        return _forward(node_features, node_attr, edge_attr, edge_scalars, lin1_ws, lin1_wv, fc_w1, fc_w2, sc_ws, sc_wv, lin2_ws, lin2_wv, edge_src, edge_dst)

    def _L1_gnn_ref(x, sh, W1, W2, W3, W4, W5, Ws, Wv, edge_index):
        import jax, jax.numpy as jnp
        import numpy as np
        N, E = (50000, 25000)
        MUL0, MUL1 = (64, 32)
        D = MUL0 + 3 * MUL1
        INV3 = float(1.0 / np.sqrt(3.0))
        INV6 = float(1.0 / np.sqrt(6.0))
        C0 = float(1.0 / np.sqrt(MUL0 + MUL1))
        C1 = float(np.sqrt(3.0 / (MUL0 + 2 * MUL1)))
        LIN_S = float(1.0 / np.sqrt(MUL0))
        LIN_V = float(1.0 / np.sqrt(MUL1))
        n = x.shape[0]
        src, dst = (edge_index[0], edge_index[1])
        s = x[:, :MUL0]
        v = x[:, MUL0:].reshape(n, MUL1, 3)
        ss, vv = (s[src], v[src])
        e0 = sh[:, 0:1]
        e1 = sh[:, 1:4]
        dot = jnp.einsum('eui,ei->eu', vv, e1)
        out0 = C0 * (ss * e0 @ W1 + dot * INV3 @ W2)
        p3 = (ss @ W3)[:, :, None] * e1[:, None, :] * INV3
        p4 = jnp.einsum('eui,uw->ewi', vv * e0[:, :, None], W4) * INV3
        p5 = jnp.einsum('eui,uw->ewi', jnp.cross(vv, e1[:, None, :]), W5) * INV6
        out1 = C1 * (p3 + p4 + p5)
        m = jnp.concatenate([out0, out1.reshape(-1, 3 * MUL1)], axis=1)
        m_agg = jax.ops.segment_sum(m, dst, num_segments=n)
        hs = m_agg[:, :MUL0] @ Ws * LIN_S
        hv = jnp.einsum('nui,uw->nwi', m_agg[:, MUL0:].reshape(n, MUL1, 3), Wv) * LIN_V
        h = jnp.concatenate([hs, hv.reshape(n, 3 * MUL1)], axis=1)
        return x + jax.nn.relu(h)

    def _L2_gnn_ref(node_input, node_attr, edge_attr, edge_scalars, W_sc_s, W_sc_v, W1_s, W1_v, W2_s, W2_v, W3, fcW1, fcW2, edge_src, edge_dst):
        import jax, jax.numpy as jnp
        import numpy as np
        N = 1250
        E = 12500
        MUL0, MUL1 = (64, 32)
        RAD, HID = (8, 64)
        WNUM = 192
        NUM_NEIGHBORS = 10.0
        INV3 = 1.0 / np.sqrt(3.0)

        def _lin(s, v, Ws, Wv, attr):
            out_s = s @ Ws * attr * (1.0 / np.sqrt(Ws.shape[0]))
            out_v = jnp.einsum('nud,uv->nvd', v, Wv) * attr[..., None] * (1.0 / np.sqrt(Wv.shape[0]))
            return (out_s, out_v)
        n = node_input.shape[0]
        s_in = node_input[:, :MUL0]
        v_in = node_input[:, MUL0:].reshape(n, MUL1, 3)
        sc_s, sc_v = _lin(s_in, v_in, W_sc_s, W_sc_v, node_attr)
        f_s, f_v = _lin(s_in, v_in, W1_s, W1_v, node_attr)
        h = jax.nn.silu(edge_scalars @ fcW1 * (1.0 / np.sqrt(RAD)))
        w = h @ fcW2 * (1.0 / np.sqrt(HID))
        wA, wB, wC, wD = (w[:, :64], w[:, 64:128], w[:, 128:160], w[:, 160:192])
        xs = f_s[edge_src]
        xv = f_v[edge_src]
        y0 = edge_attr[:, :1]
        y1 = edge_attr[:, 1:4]
        outA = wA * xs * y0
        outD = wD * jnp.einsum('eud,ed->eu', xv, y1) * INV3
        outB = wB[:, :, None] * xs[:, :, None] * y1[:, None, :]
        outC = wC[:, :, None] * xv * y0[:, :, None]
        edge_feat = jnp.concatenate([outA, outD, outB.reshape(-1, MUL0 * 3), outC.reshape(-1, MUL1 * 3)], axis=1)
        agg = jax.ops.segment_sum(edge_feat, edge_dst, num_segments=n)
        agg = agg * (1.0 / np.sqrt(NUM_NEIGHBORS))
        ms = agg[:, :MUL0 + MUL1]
        mv = agg[:, MUL0 + MUL1:].reshape(n, MUL0 + MUL1, 3)
        c_s, c_v = _lin(ms, mv, W2_s, W2_v, node_attr)
        conv = jnp.concatenate([c_s, c_v.reshape(n, -1)], axis=1)
        sc = jnp.concatenate([sc_s, sc_v.reshape(n, -1)], axis=1)
        angle = 0.1 * (ms @ W3) * node_attr * (1.0 / np.sqrt(MUL0 + MUL1))
        cos, sin = (jnp.cos(angle), jnp.sin(angle))
        return cos * sc + sin * conv

    def _L3_gnn_ref(x, edge_index, edge_attr, w_att, b_att, d2t_w1, d2t_b1, d2t_g1, d2t_be1, d2t_w2, d2t_b2, d2t_g2, d2t_be2, t2d_w1, t2d_b1, t2d_g1, t2d_be1, t2d_w2, t2d_b2, t2d_g2, t2d_be2, node_w, node_b, node_g, node_be, self_w, self_b, self_g, self_be):
        import jax, jax.numpy as jnp
        import numpy as np
        N_NODES, N_EDGES = (50000, 12500)
        D, SPLIT, EA, H = (128, 32, 64, 256)
        IN = D + EA
        EPS = 1e-05
        SLOPE = 0.01

        def _ln(x, g, b):
            m = x.mean(-1, keepdims=True)
            v = ((x - m) ** 2).mean(-1, keepdims=True)
            return (x - m) * jax.lax.rsqrt(v + EPS) * g + b

        def _block(x, w, b, g, be):
            return jax.nn.relu(_ln(x @ w + b, g, be))

        def _masked_softmax(logits, mask):
            z = jnp.where(mask, logits, -jnp.inf)
            z = z - jnp.max(z, axis=0, keepdims=True)
            e = jnp.where(mask, jnp.exp(z), 0.0)
            return e / jnp.sum(e, axis=0, keepdims=True)

        def _forward(x, edge_index, edge_attr, w_att, b_att, d2t_w1, d2t_b1, d2t_g1, d2t_be1, d2t_w2, d2t_b2, d2t_g2, d2t_be2, t2d_w1, t2d_b1, t2d_g1, t2d_be1, t2d_w2, t2d_b2, t2d_g2, t2d_be2, node_w, node_b, node_g, node_be, self_w, self_b, self_g, self_be):
            x_split = x[:, D:]
            xn = x[:, :D]
            row, col = (edge_index[0], edge_index[1])
            n = xn.shape[0]
            concat = jnp.concatenate([xn[col], xn[row]], axis=-1)
            logits = jax.nn.leaky_relu(concat @ w_att + b_att, SLOPE)
            flow_in = jnp.concatenate([xn[col], edge_attr], axis=-1)

            def direction(mask, w1, b1, g1, be1, w2, b2, g2, be2):
                attn = _masked_softmax(logits, mask[:, None])
                h = attn * flow_in
                h = _block(h, w1, b1, g1, be1)
                h = _block(h, w2, b2, g2, be2)
                h = jnp.where(mask[:, None], h, 0.0)
                return jax.ops.segment_sum(h, row, num_segments=n)
            flow_d2t = direction(row < col, d2t_w1, d2t_b1, d2t_g1, d2t_be1, d2t_w2, d2t_b2, d2t_g2, d2t_be2)
            flow_t2d = direction(row > col, t2d_w1, t2d_b1, t2d_g1, t2d_be1, t2d_w2, t2d_b2, t2d_g2, t2d_be2)
            flow_total = jnp.concatenate([flow_t2d, flow_d2t], axis=1)
            upd = _block(flow_total, node_w, node_b, node_g, node_be)
            upd = upd + _block(xn, self_w, self_b, self_g, self_be)
            return jnp.concatenate([upd, x_split], axis=1)
        return _forward(x, edge_index, edge_attr, w_att, b_att, d2t_w1, d2t_b1, d2t_g1, d2t_be1, d2t_w2, d2t_b2, d2t_g2, d2t_be2, t2d_w1, t2d_b1, t2d_g1, t2d_be1, t2d_w2, t2d_b2, t2d_g2, t2d_be2, node_w, node_b, node_g, node_be, self_w, self_b, self_g, self_be)
    edge_index = jnp.stack([src, dst])
    h = jnp.maximum(_layernorm(x, axis=-1), 0.0)
    x = x + _L0_gnn_ref(h, node_vec1, src, dst, edge_attr_4, edge_attr_64, L0_gnn_lin1_ws, L0_gnn_lin1_wv, L0_gnn_fc_w1, L0_gnn_fc_w2, L0_gnn_sc_ws, L0_gnn_sc_wv, L0_gnn_lin2_ws, L0_gnn_lin2_wv)
    h = jnp.maximum(_layernorm(x, axis=-1), 0.0)
    x = x + _L1_gnn_ref(h, edge_attr_4, L1_gnn_W1, L1_gnn_W2, L1_gnn_W3, L1_gnn_W4, L1_gnn_W5, L1_gnn_Ws, L1_gnn_Wv, edge_index)
    h = jnp.maximum(_layernorm(x, axis=-1), 0.0)
    x = x + _L2_gnn_ref(h, node_vec1, edge_attr_4, edge_attr_8, L2_gnn_W_sc_s, L2_gnn_W_sc_v, L2_gnn_W1_s, L2_gnn_W1_v, L2_gnn_W2_s, L2_gnn_W2_v, L2_gnn_W3, L2_gnn_fcW1, L2_gnn_fcW2, src, dst)
    h = jnp.maximum(_layernorm(x, axis=-1), 0.0)
    x = x + _L3_gnn_ref(h, edge_index, edge_attr_64, L3_gnn_w_att, L3_gnn_b_att, L3_gnn_d2t_w1, L3_gnn_d2t_b1, L3_gnn_d2t_g1, L3_gnn_d2t_be1, L3_gnn_d2t_w2, L3_gnn_d2t_b2, L3_gnn_d2t_g2, L3_gnn_d2t_be2, L3_gnn_t2d_w1, L3_gnn_t2d_b1, L3_gnn_t2d_g1, L3_gnn_t2d_be1, L3_gnn_t2d_w2, L3_gnn_t2d_b2, L3_gnn_t2d_g2, L3_gnn_t2d_be2, L3_gnn_node_w, L3_gnn_node_b, L3_gnn_node_g, L3_gnn_node_be, L3_gnn_self_w, L3_gnn_self_b, L3_gnn_self_g, L3_gnn_self_be)
    return x

_drawn_inputs = setup_inputs


def setup_inputs(seed=0):
    import zlib

    import numpy as np

    out = dict(_drawn_inputs(seed))
    spreads = {}
    factors = {}
    for name, (base, spread) in spreads.items():
        noise = np.random.default_rng([zlib.crc32(name.encode()), seed]).standard_normal(out[name].shape)
        drawn = base * np.exp(spread * noise) if base else spread * noise
        out[name] = jnp.asarray(drawn.astype(out[name].dtype))
    for name, factor in factors.items():
        out[name] = (out[name] * factor).astype(out[name].dtype)
    return out
```

```python
import math
from contextlib import ExitStack, contextmanager


import numpy as np
import concourse.bass as bass
from concourse import mybir

F32 = mybir.dt.float32
BF16 = mybir.dt.bfloat16
I32 = mybir.dt.int32
ALU = mybir.AluOpType
ACT = mybir.ActivationFunctionType
AX = mybir.AxisListType
ds = bass.ds

P = 128
N, D = 3125, 160
E = 103125
NT = 25
NP = NT * P
GE = 512
TG = GE // P
NG = 202
IT = NG // 2
EP = NG * GE
ET = EP // P
WIN = 32
NB = 5
NI = NT // NB
EPS = 1e-5
ROW = 132
NBIN = 98
AWIN = 64
INV2, INV3, INV6 = 1 / math.sqrt(2), 1 / math.sqrt(3), 1 / math.sqrt(6)
CROSS = {(0, 1, 2): 1.0, (1, 2, 0): 1.0, (2, 0, 1): 1.0, (0, 2, 1): -1.0, (1, 0, 2): -1.0, (2, 1, 0): -1.0}


class Bundle:
    pass


class Core:

    def __init__(self, nc, ctx):
        self.nc, self.ctx = nc, ctx
        self.bank = [ctx.enter_context(nc.psum_tensor(f"bank{i}", [P, 512], F32)) for i in range(8)]

    def sb(self, name, shape, dt=F32, ctx=None):
        return (ctx or self.ctx).enter_context(self.nc.sbuf_tensor(name, shape, dt))

    def sem(self, name):
        s = self.sem_ctx.enter_context(self.nc.semaphore(name))
        self.sems.append(s)
        return s

    def gpsimd_dma_sem(self, name):
        return self.ctx.enter_context(self.nc.semaphore(name))

    @contextmanager
    def semaphores(self, again=True):
        with ExitStack() as self.sem_ctx:
            self.sems = []
            yield
            if again:
                with self.nc.Block() as block:
                    @block.gpsimd
                    def _(pool):
                        for s in self.sems:
                            pool.sem_clear(s)


def linker(eng, sem):
    count = [0]

    def link(ins):
        count[0] += 1
        ins.then_inc(sem, 1)
        eng.wait_ge(sem, count[0])

    return link


CREDIT = 2


def group_counts(eng, n):
    v = [eng.snap(2 * n + k) for k in range(1, 5)]
    return [v[2], v[3]], [v[0], v[1]], [v[1], v[2]]


def load_weights(core, w, ins):
    nc = core.nc
    loads, scales = [], []

    def put(tile, slot, r, c, src, scale=1.0):
        rows, cols = src.shape
        dst = tile[r:r + rows, slot, c:c + cols]
        loads.append((dst, src))
        if scale != 1.0:
            scales.append((dst, scale))

    w.post0 = core.sb("w_post0", [P, 9, 96])
    w.post1 = core.sb("w_post1", [P, 13, 96])
    w.post2 = core.sb("w_post2", [P, 6, 96])
    w.pre0 = core.sb("w_pre0", [P, 2, 192])
    w.pre2 = core.sb("w_pre2", [P, 2, 192])
    w.fc0 = core.sb("w_fc0", [64, 1, 64 + 224])
    w.fc2 = core.sb("w_fc2", [64, 1, 64 + 192])
    tiles = [w.post0, w.post1, w.post2, w.pre0, w.pre2]

    for pre, lin_s, sc_s, lin_v, sc_v in ((w.pre0, ins["L0_gnn_lin1_ws"], ins["L0_gnn_sc_ws"], ins["L0_gnn_lin1_wv"],
                                           ins["L0_gnn_sc_wv"]),
                                          (w.pre2, ins["L2_gnn_W1_s"], ins["L2_gnn_W_sc_s"], ins["L2_gnn_W1_v"],
                                           ins["L2_gnn_W_sc_v"])):
        put(pre, 0, 0, 0, lin_s, 1 / 8)
        put(pre, 0, 0, 64, sc_s, 1 / 8)
        for d in range(3):
            put(pre, 1, 32 * d, 32 * d, lin_v, 1 / math.sqrt(32))
            put(pre, 1, 32 * d, 96 + 32 * d, sc_v, 1 / math.sqrt(32))
    put(w.fc0, 0, 0, 0, ins["L0_gnn_fc_w1"])
    put(w.fc0, 0, 0, 64, ins["L0_gnn_fc_w2"])
    put(w.fc2, 0, 0, 0, ins["L2_gnn_fcW1"])
    put(w.fc2, 0, 0, 64, ins["L2_gnn_fcW2"])

    ls, lv = ins["L0_gnn_lin2_ws"], ins["L0_gnn_lin2_wv"]
    cs, cv = 1 / 32 / math.sqrt(96), 1 / 32 / math.sqrt(128)
    put(w.post0, 0, 0, 0, ls[0:64, :], cs)
    for d in range(3):
        put(w.post0, 1, 32 * d, 0, ls[64:96, :], cs * INV3)
        put(w.post0, 2 + d, 64, 32 * d, lv[0:64, :], cv)
        put(w.post0, 5, 32 * d, 32 * d, lv[64:96, :], cv)
    for (d, j, k), sign in CROSS.items():
        put(w.post0, 6 + k, 32 * j, 32 * d, lv[96:128, :], cv * INV2 * sign)

    c0, c1 = 1 / math.sqrt(96), math.sqrt(3 / 128)
    put(w.post1, 0, 0, 0, ins["L1_gnn_W1"], c0)
    for d in range(3):
        put(w.post1, 1 + d, 0, 32 * d, ins["L1_gnn_W3"], c1 * INV3)
        put(w.post1, 4, 32 * d, 32 * d, ins["L1_gnn_W4"], c1 * INV3)
        put(w.post1, 5 + d, 32 * d, 0, ins["L1_gnn_W2"], c0 * INV3)
        put(w.post1, 12, 32 * d, 32 * d, ins["L1_gnn_Wv"], 1 / math.sqrt(32))
    for (d, j, k), sign in CROSS.items():
        put(w.post1, 8 + k, 32 * j, 32 * d, ins["L1_gnn_W5"], c1 * INV6 * sign)
    put(w.post1, 11, 0, 0, ins["L1_gnn_Ws"], 1 / 8)

    ls, lv, la = ins["L2_gnn_W2_s"], ins["L2_gnn_W2_v"], ins["L2_gnn_W3"]
    cs = 1 / 8 / math.sqrt(10) / math.sqrt(96)
    put(w.post2, 0, 0, 0, ls[0:64, :], cs)
    put(w.post2, 0, 0, 64, la[0:64, :], cs * 0.1)
    for d in range(3):
        put(w.post2, 1, 32 * d, 0, ls[64:96, :], cs * INV3)
        put(w.post2, 1, 32 * d, 64, la[64:96, :], cs * INV3 * 0.1)
        put(w.post2, 2 + d, 64, 32 * d, lv[0:64, :], cs)
        put(w.post2, 5, 32 * d, 32 * d, lv[64:96, :], cs)
    return tiles, loads, scales


def prepare(core, t, ins):
    nc = core.nc
    t.x = core.sb("x_res", [P, NT, D])
    t.attr = core.sb("node_attr", [P, NT])
    t.e4 = core.sb("edge_vec", [P, ET, 4])
    t.srcI = core.sb("src_idx", [P, ET], I32)
    t.dstrel = core.sb("dst_in_window", [P, ET])
    t.ident = core.sb("ident", [P, P])
    t.iotaW = core.sb("iota_window", [P, WIN])
    t.win0 = core.sb("window_base", [1, NG], I32)
    t.passes = core.sb("passes", [1, 1], I32)
    t.w = Bundle()
    zero_tiles, loads, scales = load_weights(core, t.w, ins)
    t.base_dram = nc.dram_tensor("base_dram", [NG], F32).ap()
    s_zero, s_w, s_in, s_base, s_baseload = (core.sem(n) for n in (
        "w_zeroed", "w_loaded", "prep_loaded", "bases_stored", "bases_loaded"))
    s_iota, s_ident, s_red, s_span, s_bases, s_dve = (core.sem(n) for n in (
        "iota_made", "ident_made", "span_reduced", "span_ready", "bases_ready", "prep_dve"))
    with ExitStack() as ctx:
        sb = lambda n, s, d=F32: core.sb(n, s, d, ctx)
        dstI = sb("dst_idx", [P, ET], I32)
        rows = sb("dst_rows", [IT, 2, GE], I32)
        rowsF = sb("dst_rows_f", [IT, 2, GE])
        lo = sb("row_min", [IT, 2])
        hi = sb("row_max", [IT, 2])
        span = sb("span", [P, 1])
        spanR = sb("span_all", [P, 1])
        spanI = sb("span_int", [P, 1], I32)
        iotaI = sb("iota_int", [P, WIN], I32)
        baseB = sb("base_all", [P, NG])
        block = ctx.enter_context(nc.Block())

        @block.sync
        def _(sp):
            sp.dma_start(rows[:], ins["dst_rows"].rearrange("(i h) e -> i h e", h=2)).then_inc(s_in, 16)
            sp.dma_start(dstI[:], ins["dst_pt"]).then_inc(s_in, 16)
            sp.dma_start(t.srcI[:], ins["src_pt"]).then_inc(s_in, 16)
            sp.dma_start(t.attr[:], ins["attr_pt"]).then_inc(s_in, 16)
            sp.dma_start(t.x[:], ins["x_pad"].rearrange("(t p) d -> p t d", p=P)).then_inc(s_in, 16)
            sp.dma_start(t.e4[:], ins["e4_pt"].rearrange("p (t k) -> p t k", k=4)).then_inc(s_in, 16)
            sp.wait_ge(s_zero, len(zero_tiles))
            for dst, src in loads:
                sp.dma_start(dst, src).then_inc(s_w, 16)
            sp.wait_ge(s_bases, 1)
            sp.dma_start(t.base_dram.rearrange("(i h) -> i h", h=2), lo[:]).then_inc(s_base, 16)
            sp.wait_ge(s_base, 16)
            sp.dma_start(baseB[:], t.base_dram.rearrange("(a g) -> a g", a=1).broadcast_to([P, NG])).then_inc(
                s_baseload, 16)
            sp.wait_ge(s_baseload, 16)

        @block.gpsimd
        def _(pool):
            nc.gpsimd.iota(iotaI[:], pattern=[[1, WIN]], base=0, channel_multiplier=0).then_inc(s_iota, 1)
            nc.gpsimd.memset(t.ident[:], 0.0).then_inc(s_ident, 1)
            pool.wait_ge(s_ident, 1)
            nc.gpsimd.affine_select(out=t.ident[:], in_=t.ident[:], compare_op=ALU.not_equal, fill=1.0, base=0,
                                    pattern=[[-1, P]], channel_multiplier=1).then_inc(s_ident, 1)
            pool.wait_ge(s_span, 1)
            nc.gpsimd.partition_all_reduce(spanR[:], span[:], P, bass.bass_isa.ReduceOp.max).then_inc(s_red, 1)

        @block.vector
        def _(dve):
            link = linker(dve, s_dve)
            for z in zero_tiles:
                nc.vector.memset(z[:], 0.0).then_inc(s_zero, 1)
            link(nc.vector.memset(span[:], 0.0))
            dve.wait_ge(s_iota, 1)
            nc.vector.tensor_copy(t.iotaW[:], iotaI[:])
            dve.wait_ge(s_in, 96)
            link(nc.vector.tensor_copy(rowsF[:], rows[:]))
            nc.vector.tensor_reduce(lo[:], rowsF[:], AX.X, ALU.min).then_inc(s_bases, 1)
            link(nc.vector.tensor_reduce(hi[:], rowsF[:], AX.X, ALU.max))
            dve.wait_ge(s_bases, 1)
            link(nc.vector.tensor_tensor(hi[:], hi[:], lo[:], ALU.subtract))
            nc.vector.tensor_reduce(span[0:IT, :], hi[:], AX.X, ALU.max).then_inc(s_span, 1)
            dve.wait_ge(s_red, 1)
            link(nc.vector.tensor_copy(spanI[:], spanR[:]))
            link(nc.vector.tensor_scalar(spanI[:], spanI[:], int(math.log2(WIN)), None, ALU.logical_shift_right))
            link(nc.vector.tensor_scalar(t.passes[:], spanI[0:1, :], 1, None, ALU.add))
            link(nc.vector.tensor_copy(t.dstrel[:], dstI[:]))
            dve.wait_ge(s_baseload, 16)
            nc.vector.tensor_copy(t.win0[:], baseB[0:1, :])
            rel = t.dstrel[:].rearrange("p (g j) -> p g j", j=TG)
            link(nc.vector.tensor_tensor(rel, rel, baseB[:].unsqueeze(2).broadcast_to([P, NG, TG]), ALU.subtract))
            dve.wait_ge(s_w, 16 * len(loads))
            for dst, scale in scales:
                nc.vector.tensor_scalar(dst, dst, scale, None, ALU.mult)


def center(core, t, name, xm, rstd):
    nc = core.nc
    s_dve, s_var, s_std = (core.sem(f"{name}_{n}") for n in ("stat_dve", "var_ready", "std_ready"))
    with ExitStack() as ctx:
        sq = core.sb(f"{name}_sq", [P, NT, D], F32, ctx)
        m = core.sb(f"{name}_mean", [P, NT], F32, ctx)
        v = core.sb(f"{name}_var", [P, NT], F32, ctx)
        std = core.sb(f"{name}_std", [P, NT], F32, ctx)
        block = ctx.enter_context(nc.Block())

        @block.vector
        def _(dve):
            link = linker(dve, s_dve)
            link(nc.vector.tensor_reduce(m[:], t.x[:], AX.X, ALU.add))
            link(nc.vector.tensor_scalar(m[:], m[:], 1.0 / D, None, ALU.mult))
            link(nc.vector.tensor_tensor(xm[:], t.x[:], m[:].unsqueeze(2).broadcast_to([P, NT, D]), ALU.subtract))
            link(nc.vector.tensor_tensor(sq[:], xm[:], xm[:], ALU.mult))
            link(nc.vector.tensor_reduce(v[:], sq[:], AX.X, ALU.add))
            nc.vector.tensor_scalar(v[:], v[:], 1.0 / D, EPS, ALU.mult, ALU.add).then_inc(s_var, 1)
            dve.wait_ge(s_std, 1)
            link(nc.vector.reciprocal(rstd[:], std[:]))

        @block.scalar
        def _(act):
            act.wait_ge(s_var, 1)
            nc.scalar.activation(std[:], v[:], ACT.Sqrt).then_inc(s_std, 1)



def node_tables(core, t, name, weights, n_sc):
    nc = core.nc
    S = {n: core.sem(f"{name}_{n}") for n in ("h_ready", "turned", "turned_copied", "lin", "lin_copied", "stored")}
    width = 64 + n_sc
    with ExitStack() as ctx:
        xm = core.sb(f"{name}_xm", [P, NT, D], F32, ctx)
        rstd = core.sb(f"{name}_rstd", [P, NT], F32, ctx)
        center(core, t, name, xm, rstd)
        h = core.sb(f"{name}_h", [P, NB, D], F32, ctx)
        hT = core.sb(f"{name}_hT", [96, NB, 2, P], F32, ctx)
        tab = core.sb(f"{name}_tab", [P, NB, D], F32, ctx)
        block = ctx.enter_context(nc.Block())
        turned = [core.bank[u // 2][:, 256 * (u % 2):256 * (u % 2) + 256] for u in range(NB)]
        lin = [core.bank[3 + u] for u in range(NB)]

        @block.scalar
        def _(act):
            with act.Fori(0, NI) as i:
                act.wait_ge(S["turned"], i + 1)
                for u in range(NB):
                    tile = i * NB + u
                    nc.scalar.activation(h[:, u, 0:64], xm[:, ds(tile, 1), 0:64], ACT.Relu, scale=rstd[:, ds(tile, 1)])
                    last = nc.scalar.activation(
                        h[:, u, 64:D].rearrange("p (i c) -> p c i", i=3),
                        xm[:, ds(tile, 1), 64:D].rearrange("p a (c i) -> p (a c) i", i=3), ACT.Relu,
                        scale=rstd[:, ds(tile, 1)])
                last.then_inc(S["h_ready"], 1)

        @block.tensor
        def _(pe):
            pe.sem_inc(S["turned"], 1)
            pe.sem_inc(S["lin"], 1)
            with pe.Fori(0, NI) as i:
                pe.wait_ge(S["h_ready"], i + 1)
                pe.wait_ge(S["turned_copied"], i + 1)
                for u in range(NB):
                    nc.tensor.transpose(turned[u][0:96, P:2 * P], h[:, u, 64:D], t.ident[:])
                    last = nc.tensor.transpose(turned[u][0:64, 0:P], h[:, u, 0:64], t.ident[:])
                last.then_inc(S["turned"], 1)
                pe.wait_ge(S["turned_copied"], i + 2)
                pe.wait_ge(S["lin_copied"], i + 1)
                for u in range(NB):
                    nc.tensor.matmul(lin[u][:, 0:width], hT[0:64, u, 0, :], weights[0:64, 0, 0:width], start=True,
                                     stop=False, skip_group_check=True)
                    last = nc.tensor.matmul(lin[u][:, width:width + 192], hT[0:96, u, 1, :], weights[0:96, 1, 0:192],
                                            start=False, stop=True, skip_group_check=True)
                last.then_inc(S["lin"], 1)

        @block.vector
        def _(dve):
            dve.sem_inc(S["turned_copied"], 1)
            dve.sem_inc(S["lin_copied"], 1)
            with dve.Fori(0, NI) as i:
                dve.wait_ge(S["turned"], i + 2)
                dve.wait_ge(S["lin"], i + 1)
                for u in range(NB):
                    nc.vector.tensor_copy(hT[0:64, u, 0, :], turned[u][0:64, 0:P])
                    last = nc.vector.tensor_copy(hT[0:96, u, 1, :], turned[u][0:96, P:2 * P])
                last.then_inc(S["turned_copied"], 1)
                dve.wait_ge(S["lin"], i + 2)
                dve.wait_ge(S["stored"], i * 16 + 16)
                for u in range(NB):
                    tile = i * NB + u
                    a = t.attr[:, ds(tile, 1)]
                    nc.vector.tensor_scalar(tab[:, u, 0:64], lin[u][:, 0:64], a, None, ALU.mult)
                    nc.vector.tensor_scalar(tab[:, u, 64:D], lin[u][:, width:width + 96], a, None, ALU.mult)
                    nc.vector.tensor_scalar(t.sc[:, ds(tile, 1), 0:n_sc].rearrange("p a c -> p (a c)"),
                                            lin[u][:, 64:width], a, None, ALU.mult)
                    last = nc.vector.tensor_scalar(t.sc[:, ds(tile, 1), n_sc:n_sc + 96].rearrange("p a c -> p (a c)"),
                                                   lin[u][:, width + 96:width + 192], a, None, ALU.mult)
                last.then_inc(S["lin_copied"], 1)

        @block.sync
        def _(sp):
            sp.sem_inc(S["stored"], 16)
            table = t.table.rearrange("(i u p) d -> i p u d", u=NB, p=P)
            with sp.Fori(0, NI) as i:
                sp.wait_ge(S["lin_copied"], i + 2)
                sp.dma_start(table[ds(i, 1)].rearrange("a p u d -> (a p) u d"), tab[:]).then_inc(S["stored"], 16)
            sp.wait_ge(S["stored"], NI * 16 + 16)


def table_plain(core, t, name, hR):
    nc = core.nc
    s_h, s_out = core.sem(f"{name}_h_ready"), core.sem(f"{name}_stored")
    with ExitStack() as ctx:
        xm = core.sb(f"{name}_xm", [P, NT, D], F32, ctx)
        rstd = core.sb(f"{name}_rstd", [P, NT], F32, ctx)
        center(core, t, name, xm, rstd)
        block = ctx.enter_context(nc.Block())

        @block.scalar
        def _(act):
            with act.Fori(0, NI) as i:
                for u in range(NB):
                    tile = i * NB + u
                    nc.scalar.activation(hR[:, ds(tile, 1), 0:64], xm[:, ds(tile, 1), 0:64], ACT.Relu,
                                         scale=rstd[:, ds(tile, 1)])
                    last = nc.scalar.activation(
                        hR[:, ds(tile, 1), 64:D].rearrange("p a (i c) -> p (a c) i", i=3),
                        xm[:, ds(tile, 1), 64:D].rearrange("p a (c i) -> p (a c) i", i=3), ACT.Relu,
                        scale=rstd[:, ds(tile, 1)])
                last.then_inc(s_h, 1)

        @block.sync
        def _(sp):
            sp.wait_ge(s_h, NI)
            sp.dma_start(t.table.rearrange("(t p) d -> p t d", p=P), hR[:]).then_inc(s_out, 16)
            sp.wait_ge(s_out, 16)


def edge_sums(core, t, name, acc, mlp=None):
    nc = core.nc
    names = ["attr_used", "hidden_ready", "weights_ready", "sums_ready", "eq_ready", "products_ready", "added"]
    S = {n: core.sem(f"{name}_{n}") for n in names}
    attr_in = [core.sem(f"{name}_attr_loaded{h}") for h in range(2)]
    rows_in = [core.gpsimd_dma_sem(f"{name}_rows_gathered{h}") for h in range(2)]
    s_idx, s_zero, s_win = core.sem(f"{name}_indices_copied"), core.sem(f"{name}_zeroed"), core.sem(f"{name}_windows")
    kinds = 0 if mlp is None else mlp.kinds
    with ExitStack() as ctx:
        sb = lambda n, s, d=F32: core.sb(f"{name}_{n}", s, d, ctx)
        idx = sb("idx", [P, 2, TG], I32)
        rows = sb("rows", [P, 2, TG, D])
        eq = sb("eq", [P, 2, TG, WIN])
        hot = sb("hot", [P, 2, TG, 4, WIN])
        iota = sb("iota", [P, WIN])
        win = sb("win", [1, NG], I32)
        if mlp:
            attr = sb("attr", [mlp.rin, 2, GE])
            hid = sb("hid", [64, 2, GE])
            ps = sb("prod_s", [P, 2, TG, 128])
            pv = sb("prod_v", [P, 2, TG, kinds, 96])
        block = ctx.enter_context(nc.Block())
        hid_ps = [core.bank[0], core.bank[1]]
        w_ps = [[core.bank[2], core.bank[3]], [core.bank[4], core.bank[5]]]
        sum_ps = [core.bank[6], core.bank[7]]

        if mlp:
            @block.sync
            def _(sp):
                passes = sp.value_load(t.passes[0:1, 0:1], min_val=1, max_val=NBIN)
                with sp.Fori(0, passes) as p:
                    with sp.Fori(0, IT) as i:
                        done, reuse, _ = group_counts(sp, p * IT + i)
                        for h in range(2):
                            sp.wait_ge(S["attr_used"], reuse[h])
                            sp.dma_start(attr[:, h, :], mlp.attrT[:, ds((2 * i + h) * GE, GE)]).then_inc(
                                attr_in[h], 16)

        @block.gpsimd
        def _(pool):
            for a in acc.halves[1]:
                nc.gpsimd.memset(a, 0.0).then_inc(s_zero, 1)
            passes = pool.value_load(t.passes[0:1, 0:1], min_val=1, max_val=NBIN)
            with pool.Fori(0, passes) as p:
                with pool.Fori(0, IT) as i:
                    n = pool.snap(p * IT + i)
                    done, reuse, _ = group_counts(pool, n)
                    for h in range(2):
                        pool.wait_ge(S["products_ready"] if mlp else S["sums_ready"], reuse[h])
                        nc.gpsimd.tensor_copy(idx[:, h, :], t.srcI[:, ds(i * 2 * TG + h * TG, TG)]).then_inc(s_idx, 1)
                        pool.wait_ge(s_idx, 1)
                        pool.sem_clear(s_idx)
                        for j in range(TG):
                            nc.gpsimd.indirect_dma_start(
                                rows[:, h, j, :], None, t.table,
                                bass.IndirectOffsetOnAxis(ap=idx[:, h, j:j + 1], axis=0)).then_inc(rows_in[h], 16)

        if mlp:
            @block.scalar
            def _(act):
                passes = act.value_load(t.passes[0:1, 0:1], min_val=1, max_val=NBIN)
                act.sem_inc(S["hidden_ready"], CREDIT)
                with act.Fori(0, passes) as p:
                    with act.Fori(0, IT) as i:
                        done, reuse, _ = group_counts(act, p * IT + i)
                        for h in range(2):
                            act.wait_ge(S["attr_used"], done[h])
                            act.wait_ge(S["weights_ready"], reuse[h])
                            nc.scalar.activation(hid[:, h, :], hid_ps[h][0:64, :], ACT.Silu,
                                                 scale=mlp.scale).then_inc(S["hidden_ready"], 1)

        @block.tensor
        def _(pe):
            passes = pe.value_load(t.passes[0:1, 0:1], min_val=1, max_val=NBIN)
            pe.sem_inc(S["sums_ready"], CREDIT)
            if mlp:
                pe.sem_inc(S["attr_used"], CREDIT)
                pe.sem_inc(S["weights_ready"], CREDIT)
            with pe.Fori(0, passes) as p:
                with pe.Fori(0, IT) as i:
                    n = pe.snap(p * IT + i)
                    done, reuse, _ = group_counts(pe, n)
                    slot_full = pe.snap(n * 16 + 16)
                    for h in range(2 if mlp else 0):
                        pe.wait_ge(attr_in[h], slot_full)
                        pe.wait_ge(S["hidden_ready"], reuse[h])
                        nc.tensor.matmul(hid_ps[h][0:96, :], mlp.w[0:mlp.rin, 0, 0:96], attr[:, h, :], start=True,
                                         stop=True).then_inc(S["attr_used"], 1)
                    for h in range(2 if mlp else 0):
                        pe.wait_ge(S["hidden_ready"], done[h])
                        pe.wait_ge(S["products_ready"], reuse[h])
                        for j in range(TG):
                            last = nc.tensor.matmul(
                                w_ps[h][j // 2][:, mlp.width * (j % 2):mlp.width * (j % 2 + 1)],
                                hid[:, h, j * P:(j + 1) * P], mlp.w[:, 0, 64:64 + mlp.width], start=True, stop=True)
                        last.then_inc(S["weights_ready"], 1)
                    for h in range(2):
                        o = sum_ps[h]
                        pe.wait_ge(S["products_ready"], done[h])
                        if not mlp:
                            pe.wait_ge(rows_in[h], n * 64 + 64)
                        pe.wait_ge(S["added"], reuse[h])
                        for j in range(TG):
                            first, end = j == 0, j == TG - 1
                            hots = hot[:, h, j, :, :].rearrange("p k w -> p (k w)")
                            if mlp:
                                nc.tensor.matmul(o[:, 0:4 * WIN], ps[:, h, j, :], hots, start=first, stop=end,
                                                 skip_group_check=True)
                                nc.tensor.matmul(o[0:96, 4 * WIN:5 * WIN], pv[:, h, j, 0, :], hots[:, 0:WIN],
                                                 start=False, stop=end, skip_group_check=True)
                                for q in range(1, kinds):
                                    last = nc.tensor.matmul(o[0:96, (2 + 3 * q) * WIN:(5 + 3 * q) * WIN],
                                                            pv[:, h, j, q, :], hots[:, WIN:4 * WIN], start=False,
                                                            stop=end, skip_group_check=True)
                            else:
                                nc.tensor.matmul(o[0:96, 0:4 * WIN], rows[:, h, j, 64:D], hots, start=first, stop=end,
                                                 skip_group_check=True)
                                last = nc.tensor.matmul(o[0:64, 4 * WIN:8 * WIN], rows[:, h, j, 0:64], hots,
                                                        start=False, stop=end, skip_group_check=True)
                        last.then_inc(S["sums_ready"], 1)

        @block.vector
        def _(dve):
            for a in acc.halves[0]:
                nc.vector.memset(a, 0.0).then_inc(s_zero, 1)
            nc.vector.tensor_copy(iota[:], t.iotaW[:]).then_inc(s_win, 1)
            nc.vector.tensor_copy(win[:], t.win0[:]).then_inc(s_win, 1)
            dve.wait_ge(s_win, 2)
            dve.wait_ge(s_zero, len(acc.halves[0]) + len(acc.halves[1]))
            passes = dve.value_load(t.passes[0:1, 0:1], min_val=1, max_val=NBIN)
            dve.sem_inc(S["products_ready"], CREDIT)
            dve.sem_inc(S["eq_ready"], CREDIT)
            dve.sem_inc(S["added"], CREDIT)
            with dve.Fori(0, passes) as p:
                with dve.Fori(0, IT) as i:
                    n = dve.snap(p * IT + i)
                    done, reuse, prev = group_counts(dve, n)
                    for h in range(2):
                        tiles = ds(i * 2 * TG + h * TG, TG)
                        dve.wait_ge(S["sums_ready"], reuse[h])
                        nc.vector.tensor_tensor(eq[:, h, :, :], iota[:].unsqueeze(1).broadcast_to([P, TG, WIN]),
                                                t.dstrel[:, tiles].unsqueeze(2).broadcast_to([P, TG, WIN]),
                                                ALU.is_equal).then_inc(S["eq_ready"], 1)
                        dve.wait_ge(S["eq_ready"], done[h])
                        last = nc.vector.tensor_tensor(
                            hot[:, h, :, :, :], eq[:, h, :, :].unsqueeze(2).broadcast_to([P, TG, 4, WIN]),
                            t.e4[:, tiles, :].unsqueeze(3).broadcast_to([P, TG, 4, WIN]), ALU.mult)
                        if mlp:
                            dve.wait_ge(S["weights_ready"], done[h])
                            dve.wait_ge(rows_in[h], n * 64 + 64)
                            for j in range(TG):
                                w = w_ps[h][j // 2][:, mlp.width * (j % 2):mlp.width * (j % 2 + 1)]
                                nc.vector.tensor_tensor(
                                    ps[:, h, j, :].rearrange("p (a c) -> p a c", a=2),
                                    w[:, 0:128].rearrange("p (a c) -> p a c", a=2),
                                    rows[:, h, j, 0:64].unsqueeze(1).broadcast_to([P, 2, 64]), ALU.mult)
                                last = nc.vector.tensor_tensor(
                                    pv[:, h, j, :, :].rearrange("p q (i c) -> p q i c", i=3),
                                    w[:, 128:128 + 32 * kinds].rearrange("p (q c) -> p q c", q=kinds).unsqueeze(
                                        2).broadcast_to([P, kinds, 3, 32]),
                                    rows[:, h, j, 64:D].rearrange("p (i c) -> p i c", i=3).unsqueeze(
                                        1).broadcast_to([P, kinds, 3, 32]), ALU.mult)
                        last.then_inc(S["products_ready"], 1)
                    for h in range(2):
                        o = sum_ps[h]
                        at = dve.value_load(win[0:1, ds(2 * i + h, 1)], min_val=0, max_val=NP - WIN)
                        w = ds(at, WIN)
                        dve.wait_ge(S["sums_ready"], done[h])
                        dve.wait_ge(S["added"], prev[h])

                        def add(dst, src):
                            return nc.vector.tensor_tensor(dst, dst, src, ALU.add)

                        if mlp:
                            add(acc.A[0:64, 0, w], o[0:64, 0:WIN])
                            add(acc.A[64:P, :, w], o[64:P, WIN:4 * WIN].rearrange("p (k w) -> p k w", k=3))
                            add(acc.B[:, w], o[0:96, 4 * WIN:5 * WIN])
                            for d in range(3):
                                last = add(acc.C[32 * d:32 * d + 32, w],
                                           o[32 * d:32 * d + 32, (5 + d) * WIN:(6 + d) * WIN])
                            if kinds == 3:
                                last = add(acc.X[:, :, w],
                                           o[0:96, 8 * WIN:11 * WIN].rearrange("p (k w) -> p k w", k=3))
                        else:
                            add(acc.V[:, :, w], o[0:96, 0:4 * WIN].rearrange("p (k w) -> p k w", k=4))
                            last = add(acc.S[:, :, w], o[0:64, 4 * WIN:8 * WIN].rearrange("p (k w) -> p k w", k=4))
                        last.then_inc(S["added"], 1)
                nc.vector.tensor_scalar(iota[:], iota[:], float(WIN), None, ALU.add).then_inc(s_win, 1)
                nc.vector.tensor_scalar(win[:], win[:], WIN, NP - WIN, ALU.add, ALU.min).then_inc(s_win, 1)
                dve.wait_ge(s_win, p * 2 + 4)


def finish_gated(core, t, name, acc, weights, last_layer):
    nc = core.nc
    S = {n: core.sem(f"{name}_{n}") for n in ("mixed", "mixed_copied", "turned", "pre", "sig", "used", "dve")}
    rot = last_layer
    cols = 64 if rot else 96
    srows = 65 if rot else 96
    with ExitStack() as ctx:
        sb = lambda n, s, d=F32: core.sb(f"{name}_{n}", s, d, ctx)
        sT = sb("sT", [96, NB * P])
        vT = sb("vT", [96, NB * P])
        pre = sb("pre", [P, NB, 192])
        sig = sb("sig", [P, NB, 96])
        tmp = sb("tmp", [P, NB, 96])
        if rot:
            conv = sb("conv", [P, NT, D])
            angle = sb("angle", [P, NT])
        s_ps = [core.bank[0], core.bank[1]]
        v_ps = [core.bank[2], core.bank[3]]
        out = [core.bank[4 + u // 2][:, 192 * (u % 2):192 * (u % 2) + 192] for u in range(NB)]
        half = NB * P // 2
        with nc.Block() as block:
            @block.tensor
            def _(pe):
                pe.sem_inc(S["turned"], 1)
                with pe.Fori(0, NI) as i:
                    pe.wait_ge(S["mixed_copied"], i + 1)
                    for q in range(2):
                        c = ds(i * NB * P + q * half, half)
                        nc.tensor.matmul(s_ps[q][0:srows, 0:half], weights[:, 0, 0:srows], acc.A[:, 0, c], start=True,
                                         stop=False)
                        nc.tensor.matmul(s_ps[q][0:srows, 0:half], weights[0:96, 1, 0:srows], acc.C[:, c],
                                         start=False, stop=True)
                        terms = [(weights[:, 2 + k, :], acc.A[:, k, c]) for k in range(3)]
                        terms.append((weights[0:96, 5, :], acc.B[:, c]))
                        if not rot:
                            terms += [(weights[0:96, 6 + k, :], acc.X[:, k, c]) for k in range(3)]
                        for m, (a, b) in enumerate(terms):
                            last = nc.tensor.matmul(v_ps[q][0:96, 0:half], a, b, start=m == 0,
                                                    stop=m == len(terms) - 1)
                    last.then_inc(S["mixed"], 1)
                    pe.wait_ge(S["mixed_copied"], i + 2)
                    pe.wait_ge(S["pre"], i + 1)
                    for u in range(NB):
                        nc.tensor.transpose(out[u][:, 0:srows], sT[0:srows, u * P:(u + 1) * P],
                                            t.ident[0:srows, 0:srows])
                        last = nc.tensor.transpose(out[u][:, 96:192], vT[:, u * P:(u + 1) * P], t.ident[0:96, 0:96])
                    last.then_inc(S["turned"], 1)

            @block.scalar
            def _(act):
                act.sem_inc(S["mixed_copied"], 1)
                with act.Fori(0, NI) as i:
                    act.wait_ge(S["mixed"], i + 1)
                    act.wait_ge(S["turned"], i + 1)
                    for q in range(2):
                        nc.scalar.copy(sT[0:srows, q * half:(q + 1) * half], s_ps[q][0:srows, 0:half])
                        last = nc.scalar.copy(vT[:, q * half:(q + 1) * half], v_ps[q][0:96, 0:half])
                    last.then_inc(S["mixed_copied"], 1)
                    if not rot:
                        act.wait_ge(S["pre"], i + 2)
                        act.wait_ge(S["used"], i + 1)
                        nc.scalar.activation(sig[:], pre[:, :, 0:96], ACT.Sigmoid).then_inc(S["sig"], 1)

            @block.vector
            def _(dve):
                dve.sem_inc(S["pre"], 1)
                dve.sem_inc(S["used"], 1)
                with dve.Fori(0, NI) as i:
                    dve.wait_ge(S["turned"], i + 2)
                    for u in range(NB):
                        tile = i * NB + u
                        a = t.attr[:, ds(tile, 1)]
                        if rot:
                            nc.vector.tensor_scalar(conv[:, ds(tile, 1), 0:64].rearrange("p a c -> p (a c)"),
                                                    out[u][:, 0:64], a, None, ALU.mult)
                            nc.vector.tensor_scalar(conv[:, ds(tile, 1), 64:D].rearrange("p a c -> p (a c)"),
                                                    out[u][:, 96:192], a, None, ALU.mult)
                            last = nc.vector.tensor_scalar(angle[:, ds(tile, 1)], out[u][:, 64:65], a, None, ALU.mult)
                        else:
                            last = nc.vector.scalar_tensor_tensor(
                                out=pre[:, u, :], in0=out[u], scalar=a,
                                in1=t.sc[:, ds(tile, 1), :].rearrange("p a c -> p (a c)"), op0=ALU.mult, op1=ALU.add)
                    last.then_inc(S["pre"], 1)
                    if not rot:
                        dve.wait_ge(S["sig"], i + 1)
                        dve.wait_ge(S["pre"], i + 2)
                        xs = t.x[:, ds(i * NB, NB), 0:64]
                        nc.vector.tensor_tensor(tmp[:, :, 0:64], pre[:, :, 0:64], sig[:, :, 0:64],
                                                ALU.mult).then_inc(S["dve"], 1)
                        dve.wait_ge(S["dve"], i * 2 + 1)
                        nc.vector.tensor_tensor(xs, xs, tmp[:, :, 0:64], ALU.add)
                        vec = pre[:, :, 96:192].rearrange("p u (i c) -> p u i c", i=3)
                        nc.vector.tensor_tensor(vec, vec, sig[:, :, 64:96].unsqueeze(2).broadcast_to([P, NB, 3, 32]),
                                                ALU.mult).then_inc(S["dve"], 1)
                        dve.wait_ge(S["dve"], i * 2 + 2)
                        xv = t.x[:, ds(i * NB, NB), 64:D].rearrange("p u (c i) -> p u i c", i=3)
                        nc.vector.tensor_tensor(xv, xv, vec, ALU.add).then_inc(S["used"], 1)
                        dve.wait_ge(S["used"], i + 2)

        if rot:
            ang, tri = sb("ang", [P, 2, NT]), sb("tri", [P, 2, NT])
            turns, turnsI = sb("turns", [P, 2, NT]), sb("turns_int", [P, 2, NT], I32)
            s_rot, s_ang, s_tri = core.sem(f"{name}_rot"), core.sem(f"{name}_ang"), core.sem(f"{name}_tri")
            block = ctx.enter_context(nc.Block())

            @block.vector
            def _(dve):
                link = linker(dve, s_rot)
                nc.vector.tensor_copy(ang[:, 0, :], angle[:])
                link(nc.vector.tensor_scalar(ang[:, 1, :], angle[:], math.pi / 2, None, ALU.add))
                link(nc.vector.tensor_scalar(turns[:], ang[:], 1 / (2 * math.pi), None, ALU.mult))
                link(nc.vector.tensor_copy(turnsI[:], turns[:]))
                link(nc.vector.tensor_copy(turns[:], turnsI[:]))
                two_pi_hi = 6.28125
                two_pi_lo = 2 * math.pi - two_pi_hi
                link(nc.vector.scalar_tensor_tensor(out=ang[:], in0=turns[:], scalar=-two_pi_hi, in1=ang[:],
                                                    op0=ALU.mult, op1=ALU.add))
                link(nc.vector.scalar_tensor_tensor(out=ang[:], in0=turns[:], scalar=-two_pi_lo, in1=ang[:],
                                                    op0=ALU.mult, op1=ALU.add))
                link(nc.vector.tensor_scalar(turns[:], ang[:], math.pi, -2 * math.pi, ALU.is_gt, ALU.mult))
                link(nc.vector.tensor_tensor(ang[:], ang[:], turns[:], ALU.add))
                link(nc.vector.tensor_scalar(turns[:], ang[:], -math.pi, 2 * math.pi, ALU.is_lt, ALU.mult))
                link(nc.vector.tensor_tensor(ang[:], ang[:], turns[:], ALU.add))
                nc.vector.tensor_scalar(ang[:], ang[:], 3.1415925, -3.1415925, ALU.min, ALU.max).then_inc(s_ang, 1)
                dve.wait_ge(s_tri, 1)
                scv = t.sc[:, :, 0:D]
                link(nc.vector.tensor_tensor(scv, scv, tri[:, 1, :].unsqueeze(2).broadcast_to([P, NT, D]), ALU.mult))
                link(nc.vector.tensor_tensor(conv[:], conv[:], tri[:, 0, :].unsqueeze(2).broadcast_to([P, NT, D]),
                                             ALU.mult))
                link(nc.vector.tensor_tensor(conv[:], conv[:], scv, ALU.add))
                link(nc.vector.tensor_tensor(t.x[:, :, 0:64], t.x[:, :, 0:64], conv[:, :, 0:64], ALU.add))
                xv = t.x[:, :, 64:D].rearrange("p u (c i) -> p u i c", i=3)
                link(nc.vector.tensor_tensor(xv, xv, conv[:, :, 64:D].rearrange("p u (i c) -> p u i c", i=3),
                                             ALU.add))

            @block.scalar
            def _(act):
                act.wait_ge(s_ang, 1)
                nc.scalar.activation(tri[:], ang[:], ACT.Sin).then_inc(s_tri, 1)


def finish_product(core, t, name, acc, weights, hR):
    nc = core.nc
    S = {n: core.sem(f"{name}_{n}") for n in ("mixed", "mixed_copied", "out", "tmp", "used")}
    with ExitStack() as ctx:
        sb = lambda n, s, d=F32: core.sb(f"{name}_{n}", s, d, ctx)
        sT = sb("sT", [64, NB * P])
        vT = sb("vT", [96, NB * P])
        tmp = sb("tmp", [P, NB, D])
        half = NB * P // 2
        s_ps = [core.bank[0], core.bank[1]]
        v_ps = [core.bank[2], core.bank[3]]
        out = [core.bank[4 + u // 2][:, D * (u % 2):D * (u % 2) + D] for u in range(NB)]
        block = ctx.enter_context(nc.Block())

        @block.tensor
        def _(pe):
            pe.sem_inc(S["out"], 1)
            with pe.Fori(0, NI) as i:
                pe.wait_ge(S["mixed_copied"], i + 1)
                for q in range(2):
                    c = ds(i * NB * P + q * half, half)
                    terms = [(weights[0:96, 5 + k, :], acc.V[:, 1 + k, c]) for k in range(3)]
                    terms.append((weights[0:64, 0, :], acc.S[:, 0, c]))
                    for m, (a, b) in enumerate(terms):
                        nc.tensor.matmul(s_ps[q][0:96, 0:half], a, b, start=m == 0, stop=m == len(terms) - 1)
                    terms = [(weights[0:64, 1 + k, :], acc.S[:, 1 + k, c]) for k in range(3)]
                    terms.append((weights[0:96, 4, :], acc.V[:, 0, c]))
                    terms += [(weights[0:96, 8 + k, :], acc.V[:, 1 + k, c]) for k in range(3)]
                    for m, (a, b) in enumerate(terms):
                        last = nc.tensor.matmul(v_ps[q][0:96, 0:half], a, b, start=m == 0, stop=m == len(terms) - 1)
                last.then_inc(S["mixed"], 1)
                pe.wait_ge(S["mixed_copied"], i + 2)
                pe.wait_ge(S["tmp"], i + 1)
                for u in range(NB):
                    nc.tensor.matmul(out[u][:, 0:64], sT[:, u * P:(u + 1) * P], weights[0:64, 11, 0:64],
                                     start=u % 2 == 0, stop=False, skip_group_check=True)
                    last = nc.tensor.matmul(out[u][:, 64:D], vT[:, u * P:(u + 1) * P], weights[0:96, 12, :],
                                            start=False, stop=True, skip_group_check=True)
                last.then_inc(S["out"], 1)

        @block.scalar
        def _(act):
            act.sem_inc(S["mixed_copied"], 1)
            with act.Fori(0, NI) as i:
                act.wait_ge(S["mixed"], i + 1)
                act.wait_ge(S["out"], i + 1)
                for q in range(2):
                    nc.scalar.copy(sT[:, q * half:(q + 1) * half], s_ps[q][0:64, 0:half])
                    last = nc.scalar.copy(vT[:, q * half:(q + 1) * half], v_ps[q][0:96, 0:half])
                last.then_inc(S["mixed_copied"], 1)

        @block.vector
        def _(dve):
            dve.sem_inc(S["tmp"], 1)
            with dve.Fori(0, NI) as i:
                dve.wait_ge(S["out"], i + 2)
                for u in range(NB):
                    last = nc.vector.scalar_tensor_tensor(
                        out=tmp[:, u, :], in0=out[u], scalar=0.0,
                        in1=hR[:, ds(i * NB + u, 1), :].rearrange("p a c -> p (a c)"), op0=ALU.max, op1=ALU.add)
                last.then_inc(S["tmp"], 1)
                dve.wait_ge(S["tmp"], i + 2)
                xs = t.x[:, ds(i * NB, NB), 0:64]
                nc.vector.tensor_tensor(xs, xs, tmp[:, :, 0:64], ALU.add)
                xv = t.x[:, ds(i * NB, NB), 64:D].rearrange("p u (c i) -> p u i c", i=3)
                nc.vector.tensor_tensor(xv, xv, tmp[:, :, 64:D].rearrange("p u (i c) -> p u i c", i=3),
                                        ALU.add).then_inc(S["used"], 1)
                dve.wait_ge(S["used"], i + 1)


class Group:

    def __init__(self, eng, m, h):
        snap = eng.snap if not isinstance(m, int) else (lambda v: v)
        self.m, self.h = m, h
        self.g = 2 * m + h
        self.done, self.prev, self.reuse = (snap(self.g + k) for k in (3, 2, 1))
        self.tiles = ds(self.g * TG, TG) if not isinstance(m, int) else slice(self.g * TG, self.g * TG + TG)

    def tile(self, j):
        return ds(self.g * TG + j, 1) if not isinstance(self.m, int) else slice(self.g * TG + j, self.g * TG + j + 1)

    def landed(self, k):
        return self.m * (16 * k) + 16 * k


def attention_nodes(core, t, ins, a):
    nc = core.nc
    H = 128
    S = {n: core.sem(f"n3_{n}") for n in ("h_ready", "turned", "turned_copied", "lin", "lin_copied", "stored", "w",
                                          "self_dve", "var", "std")}
    with ExitStack() as ctx:
        sb = lambda n, s, d=F32: core.sb(f"n3_{n}", s, d, ctx)
        xm, rstd = sb("xm", [P, NT, D]), sb("rstd", [P, NT])
        center(core, t, "n3", xm, rstd)
        h = sb("h", [P, NB, D])
        hT = sb("hT", [P, NB, P])
        wy = sb("wy", [P, 512])
        ws = sb("ws", [P, 130])
        y = sb("y", [P, NB, 512])
        own = sb("own", [P, NT, H])
        hs = sb("hs", [P, NT, 32])
        rowb = sb("rowb", [P, 3, H])
        loads = [(wy[:, 0:256], ins["L3_gnn_d2t_w1"][0:128, :]), (wy[:, 256:512], ins["L3_gnn_t2d_w1"][0:128, :]),
                 (ws[:, 0:128], ins["L3_gnn_self_w"]), (ws[:, 128:129], ins["L3_gnn_w_att"][128:256, :]),
                 (ws[:, 129:130], ins["L3_gnn_w_att"][0:128, :])]
        for k, n in enumerate(("self_b", "self_g", "self_be")):
            loads.append((rowb[:, k, :], ins[f"L3_gnn_{n}"].rearrange("(a n) -> a n", a=1).broadcast_to([P, H])))
        turned = [core.bank[u // 4][:, P * (u % 4):P * (u % 4) + P] for u in range(NB)]
        lin = [(core.bank[2 + 2 * (u % 3)], core.bank[3 + 2 * (u % 3)]) for u in range(NB)]
        with nc.Block() as block:
            @block.scalar
            def _(act):
                with act.Fori(0, NI) as i:
                    act.wait_ge(S["turned_copied"], i + 1)
                    for u in range(NB):
                        tile = i * NB + u
                        last = nc.scalar.activation(h[:, u, :], xm[:, ds(tile, 1), :].rearrange("p a c -> p (a c)"),
                                                    ACT.Relu, scale=rstd[:, ds(tile, 1)])
                    last.then_inc(S["h_ready"], 1)

            @block.tensor
            def _(pe):
                pe.wait_ge(S["w"], 16 * len(loads))
                pe.sem_inc(S["turned"], 1)
                pe.sem_inc(S["lin"], 1)
                with pe.Fori(0, NI) as i:
                    pe.wait_ge(S["h_ready"], i + 1)
                    pe.wait_ge(S["turned_copied"], i + 1)
                    for u in range(NB):
                        last = nc.tensor.transpose(turned[u], h[:, u, 0:H], t.ident[:])
                    last.then_inc(S["turned"], 1)
                    pe.wait_ge(S["turned_copied"], i + 2)
                    for u in range(NB):
                        pe.wait_ge(S["lin_copied"], i * NB + max(u - 2, 0) + 1)
                        nc.tensor.matmul(lin[u][0][:, :], hT[:, u, :], wy[:], start=True, stop=True)
                        nc.tensor.matmul(lin[u][1][:, 0:130], hT[:, u, :], ws[:], start=True,
                                         stop=True).then_inc(S["lin"], 1)

            @block.vector
            def _(dve):
                dve.sem_inc(S["turned_copied"], 1)
                dve.sem_inc(S["lin_copied"], 1)
                with dve.Fori(0, NI) as i:
                    dve.wait_ge(S["h_ready"], i + 1)
                    dve.wait_ge(S["turned"], i + 2)
                    dve.wait_ge(S["lin"], i * NB + 1)
                    nc.vector.tensor_copy(hT[:, 0:4, :], core.bank[0][:, :].rearrange("p (u n) -> p u n", u=4))
                    nc.vector.tensor_copy(hT[:, 4, :], core.bank[1][:, 0:P])
                    nc.vector.tensor_copy(hs[:, ds(i * NB, NB), :], h[:, :, H:D]).then_inc(S["turned_copied"], 1)
                    dve.wait_ge(S["stored"], i * 32 + 32)
                    for u in range(NB):
                        tile = i * NB + u
                        dve.wait_ge(S["lin"], i * NB + u + 2)
                        nc.vector.tensor_copy(y[:, u, :], lin[u][0][:, :])
                        nc.vector.tensor_copy(own[:, ds(tile, 1), :].rearrange("p a c -> p (a c)"),
                                              lin[u][1][:, 0:H])
                        nc.vector.tensor_copy(a.parts[:, ds(tile, 1), :].rearrange("p a c -> p (a c)"),
                                              lin[u][1][:, H:H + 2]).then_inc(S["lin_copied"], 1)

            @block.sync
            def _(sp):
                for dst, src in loads:
                    sp.dma_start(dst, src).then_inc(S["w"], 16)
                sp.sem_inc(S["stored"], 32)
                table = a.table.rearrange("(s i u p) d -> s i p u d", s=2, u=NB, p=P)
                with sp.Fori(0, NI) as i:
                    sp.wait_ge(S["lin_copied"], i * NB + NB + 1)
                    for s in range(2):
                        sp.dma_start(table[s, ds(i, 1)].rearrange("a p u d -> (a p) u d"),
                                     y[:, :, 256 * s:256 * s + 256]).then_inc(S["stored"], 16)
                sp.wait_ge(S["stored"], NI * 32 + 32)

        add_block(core, t, "own", own, rowb, hs)


def add_block(core, t, name, v, rowb, hs=None):
    nc = core.nc
    H = 128
    s_dve, s_var, s_std = (core.sem(f"{name}_{n}") for n in ("block_dve", "block_var", "block_std"))
    with ExitStack() as ctx:
        sb = lambda n, s, d=F32: core.sb(f"{name}_{n}", s, d, ctx)
        sq, m, var, std = sb("sq", [P, NT, H]), sb("m", [P, NT]), sb("v", [P, NT]), sb("std", [P, NT])
        block = ctx.enter_context(nc.Block())

        @block.vector
        def _(dve):
            link = linker(dve, s_dve)
            tt = nc.vector.tensor_tensor
            per_node = lambda a: a.unsqueeze(2).broadcast_to([P, NT, H])
            per_col = lambda k: rowb[:, k, :].unsqueeze(1).broadcast_to([P, NT, H])
            link(tt(v[:], v[:], per_col(0), ALU.add))
            link(nc.vector.tensor_reduce(m[:], v[:], AX.X, ALU.add))
            link(nc.vector.tensor_scalar(m[:], m[:], 1.0 / H, None, ALU.mult))
            link(tt(v[:], v[:], per_node(m[:]), ALU.subtract))
            link(tt(sq[:], v[:], v[:], ALU.mult))
            link(nc.vector.tensor_reduce(var[:], sq[:], AX.X, ALU.add))
            nc.vector.tensor_scalar(var[:], var[:], 1.0 / H, EPS, ALU.mult, ALU.add).then_inc(s_var, 1)
            dve.wait_ge(s_std, 1)
            link(nc.vector.reciprocal(std[:], std[:]))
            link(tt(v[:], v[:], per_node(std[:]), ALU.mult))
            link(tt(v[:], v[:], per_col(1), ALU.mult))
            link(tt(v[:], v[:], per_col(2), ALU.add))
            xs = t.x[:, :, 0:H]
            link(nc.vector.scalar_tensor_tensor(out=xs, in0=v[:], scalar=0.0, in1=xs, op0=ALU.max, op1=ALU.add))
            if hs is not None:
                link(tt(t.x[:, :, H:D], t.x[:, :, H:D], hs[:], ALU.add))

        @block.scalar
        def _(act):
            act.wait_ge(s_var, 1)
            nc.scalar.activation(std[:], var[:], ACT.Sqrt).then_inc(s_std, 1)


def edge_masks(core, t, ins, a):
    nc = core.nc
    s_in, s_out, s_dve, s_rows, s_iota = (core.sem(f"m3_{n}") for n in ("loaded", "stored", "dve", "rows", "iota"))
    with ExitStack() as ctx:
        sb = lambda n, s, d=F32: core.sb(f"m3_{n}", s, d, ctx)
        ints = sb("ints", [P, ET, 2], I32)
        both = sb("both", [P, 2, ET], I32)
        f = sb("f", [P, ET, 2])
        idxf = sb("idxf", [P, ET])
        rowsI = sb("rowsI", [IT, 2, 2 * GE], I32)
        rowsF = sb("rowsF", [IT, 2, 2 * GE])
        low = sb("low", [IT, 2, 2 * GE], I32)
        lowB = sb("lowB", [IT, 2, 2 * GE], BF16)
        maskB = sb("maskB", [IT, 2, 2 * GE], BF16)
        binI = sb("binI", [P, ET], I32)
        iotaI = sb("iotaI", [P, P], I32)
        block = ctx.enter_context(nc.Block())

        @block.gpsimd
        def _(pool):
            nc.gpsimd.iota(iotaI[:], pattern=[[1, P]], base=0, channel_multiplier=0).then_inc(s_iota, 1)
            nc.gpsimd.iota(a.iotaP_int[:], pattern=[[0, 1]], base=0, channel_multiplier=1).then_inc(s_iota, 1)

        @block.sync
        def _(sp):
            sp.dma_start(both[:, 1, :], ins["dst_pt"]).then_inc(s_in, 16)
            sp.dma_start(both[:, 0, :], ins["src_pt"]).then_inc(s_in, 16)
            sp.dma_start(rowsI[:, 0, :], ins["src_rows"].rearrange("(i h) e -> i (h e)", h=2)).then_inc(s_in, 16)
            sp.dma_start(rowsI[:, 1, :], ins["dst_rows"].rearrange("(i h) e -> i (h e)", h=2)).then_inc(s_in, 16)
            sp.wait_ge(s_rows, 1)
            for s in range(2):
                sp.dma_start(a.low_rows[s].rearrange("(i e) -> i e", i=IT), lowB[:, s, :]).then_inc(s_out, 16)
                sp.dma_start(a.mask_rows[s].rearrange("(i e) -> i e", i=IT), maskB[:, s, :]).then_inc(s_out, 16)
            sp.wait_ge(s_out, 64)

        @block.vector
        def _(dve):
            link = linker(dve, s_dve)
            tt, ts = nc.vector.tensor_tensor, nc.vector.tensor_scalar
            dve.wait_ge(s_iota, 2)
            link(nc.vector.tensor_copy(a.iota[:], iotaI[:]))
            link(nc.vector.tensor_copy(a.iotaP[:], a.iotaP_int[:]))
            dve.wait_ge(s_in, 64)
            for s in range(2):
                link(ts(ints[:, :, s], both[:, s, :], 7, None, ALU.logical_shift_right))
                link(nc.vector.tensor_copy(f[:, :, s], both[:, s, :]))
            link(nc.vector.tensor_copy(a.high[:], ints[:]))
            link(ts(binI[:], both[:, 0, :], 5, None, ALU.logical_shift_right))
            link(nc.vector.tensor_copy(a.bin[:], binI[:]))
            link(nc.vector.memset(a.meta[:], 0.0))
            link(nc.vector.tensor_copy(a.meta[:, :, 0], f[:, :, 0]))
            link(tt(a.meta[:, :, 1], f[:, :, 0], f[:, :, 1], ALU.is_lt))
            link(tt(a.meta[:, :, 2], f[:, :, 0], f[:, :, 1], ALU.is_gt))
            link(ts(idxf[:], a.meta[:, :, 2], float(NP), None, ALU.mult))
            link(tt(idxf[:], idxf[:], f[:, :, 1], ALU.add))
            link(nc.vector.tensor_copy(a.yidx[:], idxf[:]))
            link(nc.vector.tensor_copy(rowsF[:], rowsI[:]))
            link(ts(low[:], rowsI[:], 127, None, ALU.bitwise_and))
            link(nc.vector.tensor_copy(lowB[:], low[:]))
            link(tt(maskB[:, 0, :], rowsF[:, 0, :], rowsF[:, 1, :], ALU.is_lt))
            tt(maskB[:, 1, :], rowsF[:, 0, :], rowsF[:, 1, :], ALU.is_gt).then_inc(s_rows, 1)


def logits(core, t, ins, a):
    nc = core.nc
    S = {n: core.sem(f"g3_{n}") for n in ("spread", "hot_low", "picked", "hot_high", "prod", "logit", "chain")}
    row_in = [core.sem(f"g3_row_in{h}") for h in range(2)]
    s_ones = core.sem("g3_ones")
    with ExitStack() as ctx:
        sb = lambda n, s, d=F32: core.sb(f"g3_{n}", s, d, ctx)
        row = sb("row", [1, 2, 2, GE], BF16)
        ones = sb("ones", [1, P], BF16)
        hot = sb("hot", [P, 2, 2, GE])
        hh = sb("hh", [P, 2, TG, 2, NT])
        prod = sb("prod", [P, 2, TG, 2, NT])
        block = ctx.enter_context(nc.Block())
        spread = [[core.bank[2 * h + s] for s in range(2)] for h in range(2)]
        pick = [core.bank[4 + h] for h in range(2)]

        @block.sync
        def _(sp):
            with sp.Fori(0, IT) as m:
                for h in range(2):
                    k = Group(sp, m, h)
                    sp.wait_ge(S["spread"], k.reuse)
                    for s in range(2):
                        sp.dma_start(row[:, h, s, :], a.low_rows[s:s + 1, ds(k.g * GE, GE)]).then_inc(row_in[h], 16)

        @block.tensor
        def _(pe):
            pe.sem_inc(S["spread"], CREDIT)
            pe.sem_inc(S["picked"], CREDIT)
            pe.wait_ge(s_ones, 1)
            with pe.Fori(0, IT) as m:
                ks = [Group(pe, m, h) for h in range(2)]
                for k in ks:
                    pe.wait_ge(row_in[k.h], k.landed(2))
                    pe.wait_ge(S["hot_low"], k.reuse)
                    pe.wait_ge(S["picked"], k.reuse)
                    for s in range(2):
                        last = nc.tensor.matmul(spread[k.h][s][:, :], ones[:], row[:, k.h, s, :], start=True,
                                                stop=True)
                    last.then_inc(S["spread"], 1)
                for k in ks:
                    pe.wait_ge(S["hot_low"], k.done)
                    pe.wait_ge(S["prod"], k.reuse)
                    for j in range(TG):
                        for s in range(2):
                            last = nc.tensor.matmul(pick[k.h][:, (2 * j + s) * NT:(2 * j + s + 1) * NT],
                                                    hot[:, k.h, s, j * P:(j + 1) * P], a.parts[:, :, s],
                                                    start=True, stop=True)
                    last.then_inc(S["picked"], 1)

        @block.vector
        def _(dve):
            nc.vector.memset(ones[:], 1.0).then_inc(s_ones, 1)
            for n in ("hot_low", "hot_high", "prod", "logit"):
                dve.sem_inc(S[n], CREDIT)
            with dve.Fori(0, IT) as m:
                ks = [Group(dve, m, h) for h in range(2)]
                for k in ks:
                    dve.wait_ge(S["spread"], k.done)
                    dve.wait_ge(S["picked"], k.reuse)
                    for s in range(2):
                        last = nc.vector.tensor_scalar(hot[:, k.h, s, :], spread[k.h][s][:, :], a.iotaP[:, 0:1],
                                                       None, ALU.is_equal)
                    last.then_inc(S["hot_low"], 1)
                for k in ks:
                    dve.wait_ge(S["prod"], k.reuse)
                    nc.vector.tensor_tensor(
                        hh[:, k.h], a.iota[:, 0:NT].unsqueeze(1).broadcast_to([P, 2 * TG, NT]).rearrange(
                            "p (j s) c -> p j s c", s=2),
                        a.high[:, k.tiles, :].unsqueeze(3).broadcast_to([P, TG, 2, NT]),
                        ALU.is_equal).then_inc(S["hot_high"], 1)
                    dve.wait_ge(S["hot_high"], k.done)
                    dve.wait_ge(S["picked"], k.done)
                    dve.wait_ge(S["logit"], k.reuse)
                    nc.vector.tensor_tensor(prod[:, k.h], pick[k.h][:, 0:2 * TG * NT].rearrange(
                        "p (j s c) -> p j s c", j=TG, s=2), hh[:, k.h], ALU.mult).then_inc(S["prod"], 1)
                    dve.wait_ge(S["prod"], k.done)
                    nc.vector.tensor_reduce(a.logit[:, k.tiles], prod[:, k.h], AX.XY, ALU.add).then_inc(S["logit"], 1)


def softmax(core, t, ins, a):
    nc = core.nc
    s_dve, s_exp, s_e, s_max, s_mr, s_sum, s_sr, s_b, s_turn, s_tc, s_out = (core.sem(f"s3_{n}") for n in (
        "dve", "shifted", "exp", "max", "max_all", "sum", "sum_all", "b", "turned", "turned_copied", "stored"))
    s_w = core.sem("s3_weights")
    chunks = [(c, min(P, ET - c)) for c in range(0, ET, P)]
    with ExitStack() as ctx:
        sb = lambda n, s, d=F32: core.sb(f"s3_{n}", s, d, ctx)
        b = sb("b", [P, 1])
        mx, mxa, sm, sma = (sb(n, [P, 2]) for n in ("mx", "mxa", "sm", "sma"))
        tmp = sb("tmp", [P, ET])
        part = sb("part", [P, 2, ET])
        ex = sb("ex", [P, ET])
        turned = sb("turned", [P, 2, len(chunks), P])
        md, mt = a.meta[:, :, 1], a.meta[:, :, 2]
        block = ctx.enter_context(nc.Block())

        @block.sync
        def _(sp):
            sp.dma_start(b[:], ins["L3_gnn_b_att"].rearrange("(a n) -> a n", a=1).broadcast_to([P, 1])).then_inc(
                s_b, 16)
            for s in range(2):
                for c, (at, n) in enumerate(chunks):
                    sp.wait_ge(s_tc, s * len(chunks) + c + 1)
                    sp.dma_start(a.attn_rows[s, at * P:(at + n) * P].rearrange("(r p) -> r p", p=P),
                                 turned[0:n, s, c, :]).then_inc(s_out, 16)
            sp.wait_ge(s_out, 32 * len(chunks))

        @block.gpsimd
        def _(pool):
            pool.wait_ge(s_max, 1)
            nc.gpsimd.partition_all_reduce(mxa[:], mx[:], P, bass.bass_isa.ReduceOp.max).then_inc(s_mr, 1)
            pool.wait_ge(s_sum, 1)
            nc.gpsimd.partition_all_reduce(sma[:], sm[:], P, bass.bass_isa.ReduceOp.add).then_inc(s_sr, 1)

        @block.scalar
        def _(act):
            act.wait_ge(s_exp, 1)
            nc.scalar.activation(ex[:], tmp[:], ACT.Exp).then_inc(s_e, 1)

        @block.tensor
        def _(pe):
            pe.wait_ge(s_w, 1)
            for s in range(2):
                for c, (at, n) in enumerate(chunks):
                    k = s * len(chunks) + c
                    if k >= 2:
                        pe.wait_ge(s_tc, k - 1)
                    nc.tensor.transpose(core.bank[k % 2][0:n, 0:P], part[:, s, at:at + n], t.ident[:]).then_inc(
                        s_turn, 1)

        @block.vector
        def _(dve):
            link = linker(dve, s_dve)
            tt, ts, stt = nc.vector.tensor_tensor, nc.vector.tensor_scalar, nc.vector.scalar_tensor_tensor
            dve.wait_ge(s_b, 16)
            link(ts(a.logit[:], a.logit[:], b[:, 0:1], None, ALU.add))
            link(stt(out=a.logit[:], in0=a.logit[:], scalar=0.01, in1=a.logit[:], op0=ALU.mult, op1=ALU.max))
            for s, m in enumerate((md, mt)):
                link(tt(part[:, s, :], a.logit[:], m, ALU.mult))
                link(ts(tmp[:], m, -1.0, 1e30, ALU.add, ALU.mult))
                link(tt(part[:, s, :], part[:, s, :], tmp[:], ALU.add))
                ins_ = nc.vector.tensor_reduce(mx[:, s:s + 1], part[:, s, :], AX.X, ALU.max)
                link(ins_) if s == 0 else ins_.then_inc(s_max, 1)
            dve.wait_ge(s_mr, 1)
            link(ts(tmp[:], md, mxa[:, 0:1], None, ALU.mult))
            link(ts(part[:, 0, :], mt, mxa[:, 1:2], None, ALU.mult))
            link(tt(tmp[:], tmp[:], part[:, 0, :], ALU.add))
            link(tt(tmp[:], a.logit[:], tmp[:], ALU.subtract))
            ts(tmp[:], tmp[:], 0.0, None, ALU.min).then_inc(s_exp, 1)
            dve.wait_ge(s_e, 1)
            link(tt(part[:, 0, :], ex[:], md, ALU.mult))
            link(tt(part[:, 1, :], ex[:], mt, ALU.mult))
            nc.vector.tensor_reduce(sm[:], part[:], AX.X, ALU.add).then_inc(s_sum, 1)
            dve.wait_ge(s_sr, 1)
            link(ts(sma[:], sma[:], 1e-30, None, ALU.max))
            link(nc.vector.reciprocal(sma[:], sma[:]))
            for s in range(2):
                link(ts(part[:, s, :], part[:, s, :], sma[:, s:s + 1], None, ALU.mult))
            tt(a.attn[:], part[:, 0, :], part[:, 1, :], ALU.add).then_inc(s_w, 1)
            for k in range(2 * len(chunks)):
                s, c = divmod(k, len(chunks))
                dve.wait_ge(s_turn, k + 1)
                n = chunks[c][1]
                nc.vector.tensor_copy(turned[0:n, s, c, :], core.bank[k % 2][0:n, 0:P]).then_inc(s_tc, 1)


def source_order(core, t, a):
    nc = core.nc
    W = TG * NBIN
    s_tri, s_dve, s_base, s_bl, s_span, s_red, s_bases = (core.sem(f"o3_{n}") for n in (
        "tri", "dve", "base_stored", "base_loaded", "span", "span_all", "bases"))
    S = {n: core.sem(f"o3_{n}") for n in ("hot1", "counted", "first", "hot2", "opened", "closed", "prod", "pos", "pre")}
    with ExitStack() as ctx:
        sb = lambda n, s, d=F32: core.sb(f"o3_{n}", s, d, ctx)
        hot = sb("hot", [P, 2, TG, NBIN], BF16)
        ones, below, rest, zero = (sb(n, [P, P], BF16) for n in ("ones", "below", "rest", "zero"))
        onef = sb("onef", [1, P])
        total = sb("total", [P, NBIN])
        incl = sb("incl", [P, NBIN])
        excl = sb("excl", [P, NBIN])
        prod = sb("prod", [P, 2, TG, NBIN])
        posF = sb("posF", [P, ET])
        with nc.Block() as block:
            @block.gpsimd
            def _(pool):
                nc.gpsimd.memset(ones[:], 1.0).then_inc(s_tri, 1)
                nc.gpsimd.memset(zero[:], 0.0).then_inc(s_tri, 1)
                nc.gpsimd.memset(onef[:], 1.0).then_inc(s_tri, 1)
                pool.wait_ge(s_tri, 3)
                nc.gpsimd.affine_select(out=below[:], in_=ones[:], compare_op=ALU.is_gt, fill=0.0, base=0,
                                        pattern=[[1, P]], channel_multiplier=-1).then_inc(s_tri, 1)
                nc.gpsimd.affine_select(out=rest[:], in_=ones[:], compare_op=ALU.is_ge, fill=0.0, base=0,
                                        pattern=[[-1, P]], channel_multiplier=1).then_inc(s_tri, 1)

            def hot_of(dve, k, sem):
                return nc.vector.tensor_tensor(hot[:, k.h, :, :], a.iota[:, 0:NBIN].unsqueeze(1).broadcast_to(
                    [P, TG, NBIN]), a.bin[:, k.tiles].unsqueeze(2).broadcast_to([P, TG, NBIN]),
                    ALU.is_equal).then_inc(sem, 1)

            @block.tensor
            def _(pe):
                pe.wait_ge(s_tri, 5)
                pe.sem_inc(S["counted"], CREDIT)
                pe.wait_ge(S["hot1"], CREDIT + 1)
                nc.tensor.matmul(core.bank[0][:, 0:W], zero[:], hot[:, 0, :, :], start=True, stop=False,
                                 skip_group_check=True)
                with pe.Fori(0, IT) as m:
                    for h in range(2):
                        k = Group(pe, m, h)
                        pe.wait_ge(S["hot1"], k.done)
                        nc.tensor.matmul(core.bank[0][:, 0:W], ones[:], hot[:, h, :, :], start=False, stop=False,
                                         skip_group_check=True).then_inc(S["counted"], 1)
                nc.tensor.matmul(core.bank[0][:, 0:W], zero[:], hot[:, 0, :, :], start=False, stop=True,
                                 skip_group_check=True).then_inc(S["first"], 1)

            @block.vector
            def _(dve):
                dve.sem_inc(S["hot1"], CREDIT)
                with dve.Fori(0, IT) as m:
                    for h in range(2):
                        k = Group(dve, m, h)
                        dve.wait_ge(S["counted"], k.reuse)
                        hot_of(dve, k, S["hot1"])
                link = linker(dve, s_dve)
                dve.wait_ge(S["first"], 1)
                link(nc.vector.tensor_reduce(total[:], core.bank[0][:, 0:W].rearrange("p (j b) -> p b j", j=TG),
                                             AX.X, ALU.add))
                link(nc.vector.memset(excl[:], 0.0))
                link(nc.vector.tensor_tensor_scan(incl[:], total[:], excl[:], 0.0, ALU.add, ALU.add))
                link(nc.vector.tensor_tensor(excl[:], incl[:], total[:], ALU.subtract))
                link(nc.vector.memset(hot[:, 1, :, :], 0.0))

        with nc.Block() as block:
            bank = [core.bank[0], core.bank[1]]

            def mm(dst, lhsT, j, n):
                return nc.tensor.matmul(dst, lhsT, j.unsqueeze(1).broadcast_to([P, n, NBIN]), start=False,
                                        stop=False, skip_group_check=True)

            @block.tensor
            def _(pe):
                for b in bank:
                    last = nc.tensor.matmul(b[:, 0:W], onef[:], excl[0:1, :].unsqueeze(1).broadcast_to([1, TG, NBIN]),
                                            start=True, stop=False, skip_group_check=True)
                pe.sem_inc(S["closed"], CREDIT)
                pe.sem_inc(S["opened"], CREDIT)
                with pe.Fori(0, IT) as m:
                    for h in range(2):
                        k = Group(pe, m, h)
                        own, other = hot[:, h, :, :], hot[:, 1 - h, :, :]
                        cols = lambda b, j, n: b[:, j * NBIN:(j + n) * NBIN]
                        pe.wait_ge(S["hot2"], k.done)
                        for j in range(TG):
                            last = mm(cols(bank[h], j, 1), below[:], own[:, j, :], 1)
                        for j in range(TG - 1):
                            last = mm(cols(bank[h], j + 1, TG - 1 - j), ones[:], own[:, j, :], TG - 1 - j)
                        last.then_inc(S["opened"], 1)
                        pe.wait_ge(S["prod"], k.prev)
                        for j in range(TG):
                            mm(cols(bank[1 - h], j, 1), rest[:], other[:, j, :], 1)
                        for j in range(1, TG):
                            mm(cols(bank[1 - h], 0, j), ones[:], other[:, j, :], j)
                        for j in range(TG):
                            last = mm(cols(bank[1 - h], 0, TG), ones[:], own[:, j, :], TG)
                        last.then_inc(S["closed"], 1)

            @block.vector
            def _(dve):
                for n in ("hot2", "prod", "pos"):
                    dve.sem_inc(S[n], CREDIT)
                with dve.Fori(0, IT) as m:
                    for h in range(2):
                        k = Group(dve, m, h)
                        dve.wait_ge(S["closed"], k.prev)
                        hot_of(dve, k, S["hot2"])
                        dve.wait_ge(S["opened"], k.done)
                        dve.wait_ge(S["pos"], k.reuse)
                        nc.vector.tensor_tensor(prod[:, h], bank[h][:, 0:W].rearrange("p (j b) -> p j b", j=TG),
                                                hot[:, h, :, :], ALU.mult).then_inc(S["prod"], 1)
                        dve.wait_ge(S["prod"], k.done)
                        nc.vector.tensor_reduce(posF[:, k.tiles], prod[:, h], AX.X, ALU.add).then_inc(S["pos"], 1)

        start = sb("start", [IT, 2])
        startI = sb("startI", [IT, 2], I32)
        cmp = sb("cmp", [IT, 2, NBIN])
        lo, hi = sb("lo", [IT, 2]), sb("hi", [IT, 2])
        span, spanR, spanI = sb("span", [P, 1]), sb("spanR", [P, 1]), sb("spanI", [P, 1], I32)
        win = sb("win", [1, NG])
        block = ctx.enter_context(nc.Block())

        @block.gpsimd
        def _(pool):
            nc.gpsimd.iota(startI[:], pattern=[[GE, 2]], base=0, channel_multiplier=2 * GE).then_inc(s_tri, 1)
            pool.wait_ge(s_span, 1)
            nc.gpsimd.partition_all_reduce(spanR[:], span[:], P, bass.bass_isa.ReduceOp.max).then_inc(s_red, 1)

        @block.sync
        def _(sp):
            sp.wait_ge(s_bases, 1)
            sp.dma_start(a.base_dram.rearrange("(i h) -> i h", h=2), lo[:]).then_inc(s_base, 16)
            sp.wait_ge(s_base, 16)
            sp.dma_start(a.baseB[:], a.base_dram.rearrange("(a g) -> a g", a=1).broadcast_to([P, NG])).then_inc(
                s_bl, 16)
            sp.wait_ge(s_bl, 16)

        @block.vector
        def _(dve):
            s_d = core.sem("o3_windows_dve")
            link = linker(dve, s_d)
            nc.vector.tensor_copy(a.pos[:], posF[:])
            dve.wait_ge(s_tri, 6)
            link(nc.vector.tensor_copy(start[:], startI[:]))
            inclB = incl[0:IT, :].unsqueeze(1).broadcast_to([IT, 2, NBIN])
            for dst, last in ((lo, False), (hi, True)):
                link(nc.vector.tensor_tensor(cmp[:], inclB, start[:].unsqueeze(2).broadcast_to([IT, 2, NBIN]),
                                             ALU.is_le))
                link(nc.vector.tensor_reduce(dst[:], cmp[:], AX.X, ALU.add))
                if not last:
                    link(nc.vector.tensor_scalar(start[:], start[:], GE - 1.0, None, ALU.add))
            link(nc.vector.tensor_tensor(hi[:], hi[:], lo[:], ALU.subtract))
            nc.vector.tensor_scalar(lo[:], lo[:], 32.0, None, ALU.mult).then_inc(s_bases, 1)
            link(nc.vector.memset(span[:], 0.0))
            nc.vector.tensor_reduce(span[0:IT, :], hi[:], AX.X, ALU.max).then_inc(s_span, 1)
            dve.wait_ge(s_red, 1)
            link(nc.vector.tensor_copy(spanI[:], spanR[:]))
            link(nc.vector.tensor_scalar(spanI[:], spanI[:], 1, None, ALU.logical_shift_right))
            link(nc.vector.tensor_scalar(a.passes[:], spanI[0:1, :], 1, None, ALU.add))
            dve.wait_ge(s_bl, 16)
            link(nc.vector.tensor_copy(a.win0[:], a.baseB[0:1, :]))


def messages(core, t, ins, a):
    nc = core.nc
    H, O = 256, 128
    names = ("scaled", "z_ready", "z_copied", "stats1", "std1", "rstd1", "normed1", "turned", "hidden", "u_ready",
             "half", "comb", "stats2", "std2", "rstd2", "normed2", "gained", "message", "sent", "v1", "w2a", "parts1", "parts2")
    S = {n: core.sem(f"x3_{n}") for n in names}
    in_ = [core.sem(f"x3_loaded{h}") for h in range(2)]
    rows_in = [core.gpsimd_dma_sem(f"x3_gathered{h}") for h in range(2)]
    sent = [core.gpsimd_dma_sem(f"x3_sent{h}") for h in range(2)]
    s_w, s_raw, s_split, s_parts, s_idx, s_pidx, s_c = (core.sem(f"x3_{n}") for n in (
        "w", "raw", "split", "parts", "idx", "pidx", "const"))
    with ExitStack() as ctx:
        sb = lambda n, s, d=F32: core.sb(f"x3_{n}", s, d, ctx)
        w1b = sb("w1b", [P, H])
        w2 = sb("w2", [P, 2, 2, O])
        gb = sb("gb", [P, 2, 2, 2])
        raw = sb("raw", [2, 512])
        raw2 = sb("raw2", [1, 256])
        split, split2 = sb("split", [2, 3, 512], BF16), sb("split2", [1, 3, 256], BF16)
        vecs, vecs2 = sb("vecs", [6, 512], BF16), sb("vecs2", [3, 256], BF16)
        ones = sb("ones", [3, P], BF16)
        eps = sb("eps", [P, 1])
        idx, pidx = sb("idx", [P, 2, TG], I32), sb("pidx", [P, 2, TG], I32)
        ea, at = sb("ea", [P, 2, GE]), sb("at", [P, 2, GE])
        mask = sb("mask", [6, 2, GE], BF16)
        y = sb("y", [P, 2, TG, H])
        z = sb("z", [P, 2, TG, H])
        st1, mv1 = sb("st1", [P, 2, TG, 6]), sb("mv1", [P, 2, TG, 2])
        sd1, rs1, nb1 = (sb(n, [P, 2, TG]) for n in ("sd1", "rs1", "nb1"))
        st2, mv2 = sb("st2", [P, 2, TG, 6]), sb("mv2", [P, 2, TG, 2])
        sd2, rs2 = (sb(n, [P, 2, TG]) for n in ("sd2", "rs2"))
        dif, dif2 = sb("dif", [P, 2, TG]), sb("dif2", [P, 2, TG])
        hid = sb("hid", [P, 2, 2, GE])
        half = sb("half", [P, 2, TG, O])
        c2 = sb("c2", [P, 2, TG, O])
        row = sb("row", [P, 2, TG, ROW])
        loads = [(w1b[64 * s:64 * s + 64, :], ins[f"L3_gnn_{n}_w1"][128:192, :]) for s, n in enumerate(("d2t", "t2d"))]
        raws = []
        for s, n in enumerate(("d2t", "t2d")):
            get = lambda v: ins[f"L3_gnn_{n}_{v}"]
            loads.append((w2[:, s, :, :], get("w2").rearrange("(c p) o -> p c o", p=P)))
            loads.append((gb[:, s, :, 0], get("g1").rearrange("(c p) -> p c", p=P)))
            loads.append((gb[:, s, :, 1], get("be1").rearrange("(c p) -> p c", p=P)))
            line = lambda v: get(v).rearrange("(a n) -> a n", a=1)
            raws += [(raw[s:s + 1, 0:256], line("b1")), (raw[s:s + 1, 256:384], line("g2")),
                     (raw[s:s + 1, 384:512], line("be2")), (raw2[:, 128 * s:128 * s + 128], line("b2"))]
        with nc.Block() as block:
            @block.sync
            def _(sp):
                for dst, src in raws:
                    sp.dma_start(dst, src).then_inc(s_raw, 16)
                for dst, src in loads:
                    sp.dma_start(dst, src, allow_slow_non_contiguous=True).then_inc(s_w, 16)
                sp.wait_ge(s_split, 2)
                for q in range(3):
                    for s in range(2):
                        sp.dma_start(vecs[3 * s + q:3 * s + q + 1, :], split[s:s + 1, q, :]).then_inc(s_parts, 16)
                    sp.dma_start(vecs2[q:q + 1, :], split2[:, q, :]).then_inc(s_parts, 16)
                sp.wait_ge(s_parts, 9 * 16)
                sp.wait_ge(s_w, 16 * len(loads))

            @block.vector
            def _(dve):
                link = linker(dve, s_c)
                dve.wait_ge(s_raw, 16 * len(raws))
                link(nc.vector.memset(ones[:], 1.0))
                link(nc.vector.memset(eps[:], EPS))
                for r, sp_ in ((raw, split), (raw2, split2)):
                    for q in range(3):
                        ins_ = nc.vector.tensor_copy(sp_[:, q, :], r[:])
                        link(ins_)
                        if q < 2:
                            link(nc.vector.tensor_tensor(r[:], r[:], sp_[:, q, :], ALU.subtract))
                nc.vector.tensor_copy(eps[:], eps[:]).then_inc(s_split, 2)

        block = ctx.enter_context(nc.Block())
        z_ps = [core.bank[0], core.bank[1]]
        t_ps = [core.bank[2], core.bank[3]]
        u_ps = [core.bank[4], core.bank[5]]
        g_ps = [core.bank[6], core.bank[7]]

        def halfsteps(eng, step):
            step(Group(eng, 0, 0), None)
            with eng.Fori(0, IT - 1) as m:
                a_, b_ = Group(eng, m, 0), Group(eng, m, 1)
                step(b_, a_)
                step(Group(eng, eng.snap(m + 1), 0), b_)
            last = Group(eng, IT - 1, 1)
            step(last, Group(eng, IT - 1, 0))
            step(None, last)

        @block.sync
        def _(sp):
            def load(k):
                sp.wait_ge(S["u_ready"], k.reuse)
                cols = ds(k.g * GE, GE)
                for s in range(2):
                    sp.dma_start(ea[64 * s:64 * s + 64, k.h, :], ins["attr64T"][:, cols]).then_inc(in_[k.h], 16)
                    sp.dma_start(at[64 * s:64 * s + 64, k.h, :], a.attn_rows[s:s + 1, cols].broadcast_to(
                        [64, GE])).then_inc(in_[k.h], 16)
                    sp.dma_start(mask[3 * s:3 * s + 3, k.h, :], a.mask_rows[s:s + 1, cols].broadcast_to(
                        [3, GE])).then_inc(in_[k.h], 16)

            with sp.Fori(0, IT) as m:
                for h in range(2):
                    load(Group(sp, m, h))

        @block.gpsimd
        def _(pool):
            def gather(k):
                pool.wait_ge(S["z_copied"], k.reuse)
                nc.gpsimd.tensor_copy(idx[:, k.h, :], a.yidx[:, k.tiles]).then_inc(s_idx, 1)
                pool.wait_ge(s_idx, 1)
                pool.sem_clear(s_idx)
                for j in range(TG):
                    nc.gpsimd.indirect_dma_start(y[:, k.h, j, :], None, a.table, bass.IndirectOffsetOnAxis(
                        ap=idx[:, k.h, j:j + 1], axis=0)).then_inc(rows_in[k.h], 16)

            def scatter(k):
                pool.wait_ge(S["message"], k.done)
                nc.gpsimd.tensor_copy(pidx[:, k.h, :], a.pos[:, k.tiles]).then_inc(s_pidx, 1)
                pool.wait_ge(s_pidx, 1)
                pool.sem_clear(s_pidx)
                for j in range(TG):
                    nc.gpsimd.indirect_dma_start(a.rows, bass.IndirectOffsetOnAxis(
                        ap=pidx[:, k.h, j:j + 1], axis=0), row[:, k.h, j, :], None).then_inc(sent[k.h], 16)

            for h in range(2):
                for j in range(TG):
                    nc.gpsimd.dma_start(a.spare[h, j], a.pos[:, j:j + 1]).then_inc(sent[h], 16)
            gather(Group(pool, 0, 0))
            gather(Group(pool, 0, 1))
            with pool.Fori(0, IT - 1) as m:
                nxt = pool.snap(m + 1)
                for h in range(2):
                    gather(Group(pool, nxt, h))
                    scatter(Group(pool, m, h))
            for h in range(2):
                scatter(Group(pool, IT - 1, h))
            for h in range(2):
                pool.wait_ge(sent[h], 64 + 64 * IT)

        @block.tensor
        def _(pe):
            for n in ("z_ready", "turned", "u_ready"):
                pe.sem_inc(S[n], CREDIT)

            def step(k, prev):
                if k:
                    pe.wait_ge(in_[k.h], k.landed(6))
                    pe.wait_ge(S["scaled"], k.done)
                    pe.wait_ge(S["z_copied"], k.prev)
                    for j in range(TG):
                        o = z_ps[j // 2][:, H * (j % 2):H * (j % 2) + H]
                        e = slice(j * P, (j + 1) * P)
                        nc.tensor.matmul(o, at[:, k.h, e], w1b[:], start=True, stop=False)
                        last = nc.tensor.matmul(o, mask[:, k.h, e], vecs[:, 0:H], start=False, stop=True)
                    last.then_inc(S["z_ready"], 1)
                if prev:
                    pe.wait_ge(S["hidden"], prev.done)
                    pe.wait_ge(S["comb"], prev.prev)
                    pe.wait_ge(S["gained"], prev.prev)
                    for j in range(TG):
                        e = slice(j * P, (j + 1) * P)
                        o = u_ps[j // 2][:, 2 * O * (j % 2):2 * O * (j % 2) + 2 * O]
                        for s in range(2):
                            for c in range(2):
                                nc.tensor.matmul(o[:, s * O:(s + 1) * O], hid[:, s, c, e], w2[:, s, c, :],
                                                 start=(j % 2 == 0 and s == 0 and c == 0), stop=False,
                                                 skip_group_check=True)
                        nc.tensor.matmul(o, ones[:], vecs2[:], start=False, stop=True, skip_group_check=True)
                        o = g_ps[j // 2][:, 2 * O * (j % 2):2 * O * (j % 2) + 2 * O]
                        last = nc.tensor.matmul(o, mask[:, prev.h, e], vecs[:, H:2 * H], start=True, stop=True)
                    last.then_inc(S["u_ready"], 1)
                if k:
                    pe.wait_ge(S["normed1"], k.done)
                    pe.wait_ge(S["hidden"], k.prev)
                    for c in range(2):
                        for j in range(TG):
                            last = nc.tensor.transpose(t_ps[c][:, j * P:(j + 1) * P],
                                                       z[:, k.h, j, c * P:(c + 1) * P], t.ident[:])
                    last.then_inc(S["turned"], 1)

            halfsteps(pe, step)

        @block.scalar
        def _(act):
            for n in ("std1", "normed1", "hidden", "half", "std2", "message"):
                act.sem_inc(S[n], CREDIT)

            def step(k, prev):
                if k:
                    act.wait_ge(S["stats1"], k.done)
                    act.wait_ge(S["rstd1"], k.reuse)
                    nc.scalar.activation(sd1[:, k.h, :], mv1[:, k.h, :, 1], ACT.Sqrt, scale=1.0 / H,
                                         bias=eps[:, 0:1]).then_inc(
                        S["std1"], 1)
                    act.wait_ge(S["rstd1"], k.done)
                    for j in range(TG):
                        last = nc.scalar.activation(z[:, k.h, j, :], z[:, k.h, j, :], ACT.Identity,
                                                    scale=rs1[:, k.h, j:j + 1], bias=nb1[:, k.h, j:j + 1])
                    last.then_inc(S["normed1"], 1)
                if prev:
                    act.wait_ge(S["u_ready"], prev.done)
                    act.wait_ge(S["comb"], prev.reuse)
                    for j in range(TG):
                        o = u_ps[j // 2][:, 2 * O * (j % 2):2 * O * (j % 2) + O]
                        last = nc.scalar.activation(half[:, prev.h, j, :], o, ACT.Copy,
                                                    scale=a.meta[:, prev.tile(j), 1])
                    last.then_inc(S["half"], 1)
                    act.wait_ge(S["stats2"], prev.done)
                    act.wait_ge(S["rstd2"], prev.reuse)
                    nc.scalar.activation(sd2[:, prev.h, :], mv2[:, prev.h, :, 1], ACT.Sqrt, scale=1.0 / O,
                                         bias=eps[:, 0:1]).then_inc(S["std2"], 1)
                if k:
                    act.wait_ge(S["turned"], k.done)
                    act.wait_ge(S["u_ready"], k.prev)
                    for s in range(2):
                        for c in range(2):
                            last = nc.scalar.activation(hid[:, s, c, :], t_ps[c][:, :], ACT.Relu,
                                                        scale=gb[:, s, c, 0:1], bias=gb[:, s, c, 1:2])
                    last.then_inc(S["hidden"], 1)
                if prev:
                    act.wait_ge(S["gained"], prev.done)
                    act.wait_ge(sent[prev.h], prev.landed(4))
                    nc.scalar.activation(row[:, prev.h, :, 0:O], c2[:, prev.h, :, :], ACT.Relu)
                    nc.scalar.copy(row[:, prev.h, :, O:ROW], a.meta[:, prev.tiles, :]).then_inc(S["message"], 1)

            halfsteps(act, step)

        @block.vector
        def _(dve):
            for n in ("scaled", "z_copied", "v1", "stats1", "rstd1", "w2a", "comb", "stats2", "rstd2", "normed2",
                      "gained"):
                dve.sem_inc(S[n], CREDIT)
            tt, stt = nc.vector.tensor_tensor, nc.vector.scalar_tensor_tensor

            def scale(k):
                dve.wait_ge(in_[k.h], k.landed(6))
                tt(at[:, k.h, :], ea[:, k.h, :], at[:, k.h, :], ALU.mult).then_inc(S["scaled"], 1)

            def moments(k, st, mv, n, sem):
                s = st[:, k.h]
                tt(mv[:, k.h, :, 0], s[:, :, 1], s[:, :, 4], ALU.add)
                tt(dif[:, k.h, :], s[:, :, 1], s[:, :, 4], ALU.subtract)
                tt(mv[:, k.h, :, 1], s[:, :, 2], s[:, :, 5], ALU.add).then_inc(sem, 1)
                dve.wait_ge(sem, 2 * k.g + 1)
                nc.vector.tensor_scalar(mv[:, k.h, :, 0], mv[:, k.h, :, 0], 0.5, None, ALU.mult)
                tt(dif2[:, k.h, :], dif[:, k.h, :], dif[:, k.h, :], ALU.mult).then_inc(sem, 1)
                dve.wait_ge(sem, 2 * k.g + 2)
                return stt(out=mv[:, k.h, :, 1], in0=dif2[:, k.h, :], scalar=n / 4, in1=mv[:, k.h, :, 1],
                           op0=ALU.mult, op1=ALU.add)

            def step(k, prev):
                if k:
                    scale(k)
                    dve.wait_ge(S["z_ready"], k.done)
                    dve.wait_ge(rows_in[k.h], k.landed(4))
                    dve.wait_ge(S["turned"], k.reuse)
                    for j in range(TG):
                        last = stt(out=z[:, k.h, j, :], in0=y[:, k.h, j, :], scalar=a.attn[:, k.tile(j)],
                                   in1=z_ps[j // 2][:, H * (j % 2):H * (j % 2) + H], op0=ALU.mult, op1=ALU.add)
                    last.then_inc(S["z_copied"], 1)
                    dve.wait_ge(S["z_copied"], k.done)
                    for j in range(TG):
                        last = nc.vector.bn_stats(st1[:, k.h, j, :], z[:, k.h, j, :])
                    last.then_inc(S["v1"], 1)
                    dve.wait_ge(S["v1"], k.done)
                    moments(k, st1, mv1, H, S["parts1"]).then_inc(S["stats1"], 1)
                    dve.wait_ge(S["std1"], k.done)
                    nc.vector.reciprocal(rs1[:, k.h, :], sd1[:, k.h, :]).then_inc(S["w2a"], 1)
                    dve.wait_ge(S["w2a"], k.done)
                    stt(out=nb1[:, k.h, :], in0=mv1[:, k.h, :, 0], scalar=-1.0, in1=rs1[:, k.h, :], op0=ALU.mult,
                        op1=ALU.mult).then_inc(S["rstd1"], 1)
                if prev:
                    p = prev
                    dve.wait_ge(S["half"], p.done)
                    for j in range(TG):
                        last = stt(out=c2[:, p.h, j, :], in0=u_ps[j // 2][:, 2 * O * (j % 2) + O:2 * O * (j % 2 + 1)],
                                   scalar=a.meta[:, p.tile(j), 2], in1=half[:, p.h, j, :], op0=ALU.mult, op1=ALU.add)
                    last.then_inc(S["comb"], 1)
                    dve.wait_ge(S["comb"], p.done)
                    for j in range(TG):
                        last = nc.vector.bn_stats(st2[:, p.h, j, :], c2[:, p.h, j, :])
                    last.then_inc(S["normed2"], 1)
                    dve.wait_ge(S["normed2"], p.done)
                    moments(p, st2, mv2, O, S["parts2"]).then_inc(S["stats2"], 1)
                    dve.wait_ge(S["std2"], p.done)
                    nc.vector.reciprocal(rs2[:, p.h, :], sd2[:, p.h, :]).then_inc(S["rstd2"], 1)
                    dve.wait_ge(S["rstd2"], p.done)
                    for j in range(TG):
                        G = g_ps[j // 2][:, 2 * O * (j % 2):2 * O * (j % 2) + O]
                        last = stt(out=half[:, p.h, j, :], in0=c2[:, p.h, j, :], scalar=mv2[:, p.h, j, 0:1], in1=G,
                                   op0=ALU.subtract, op1=ALU.mult)
                    last.then_inc(S["sent"], 1)
                    dve.wait_ge(S["sent"], p.g + 1)
                    for j in range(TG):
                        B = g_ps[j // 2][:, 2 * O * (j % 2) + O:2 * O * (j % 2 + 1)]
                        last = stt(out=c2[:, p.h, j, :], in0=half[:, p.h, j, :], scalar=rs2[:, p.h, j:j + 1], in1=B,
                                   op0=ALU.mult, op1=ALU.add)
                    last.then_inc(S["gained"], 1)

            halfsteps(dve, step)


def flow_sums(core, t, ins, a):
    nc = core.nc
    H = 128
    S = {n: core.sem(f"a3_{n}") for n in ("rel", "eq", "hot", "sums", "added", "mixed", "mixed_copied", "turned",
                                          "own")}
    in_ = [core.sem(f"a3_loaded{h}") for h in range(2)]
    s_init, s_win, s_w = core.sem("a3_init"), core.sem("a3_windows"), core.sem("a3_weights")
    with ExitStack() as ctx:
        sb = lambda n, s, d=F32: core.sb(f"a3_{n}", s, d, ctx)
        acc = sb("acc", [P, 2, NP])
        flow = sb("flow", [P, NT, H])
        rowb = sb("rowb", [P, 3, H])
        nw = sb("nw", [P, 2, H])
        with ExitStack() as ectx:
            row = core.sb("a3_row", [P, 2, TG, ROW], F32, ectx)
            rel = core.sb("a3_rel", [P, 2, TG], F32, ectx)
            eq = core.sb("a3_eq", [P, 2, TG, AWIN], F32, ectx)
            hot = core.sb("a3_hot", [P, 2, TG, 2, AWIN], F32, ectx)
            iota = core.sb("a3_iota", [P, AWIN], F32, ectx)
            win = core.sb("a3_win", [1, NG], I32, ectx)
            block = ectx.enter_context(nc.Block())
            o = [core.bank[0], core.bank[1]]

            @block.sync
            def _(sp):
                passes = sp.value_load(a.passes[0:1, 0:1], min_val=1, max_val=NBIN)
                rows = a.rows.rearrange("(g p j) c -> g p (j c)", p=P, j=TG)
                with sp.Fori(0, passes) as p:
                    with sp.Fori(0, IT) as i:
                        m = sp.snap(p * IT + i)
                        for h in range(2):
                            k = Group(sp, m, h)
                            sp.wait_ge(S["sums"], k.reuse)
                            sp.dma_start(row[:, h, :, :].rearrange("p j c -> p (j c)"),
                                         rows[ds(2 * i + h, 1)].rearrange("a p f -> (a p) f")).then_inc(in_[h], 16)

            @block.tensor
            def _(pe):
                passes = pe.value_load(a.passes[0:1, 0:1], min_val=1, max_val=NBIN)
                pe.sem_inc(S["sums"], CREDIT)
                with pe.Fori(0, passes) as p:
                    with pe.Fori(0, IT) as i:
                        m = pe.snap(p * IT + i)
                        for h in range(2):
                            k = Group(pe, m, h)
                            pe.wait_ge(S["hot"], k.done)
                            pe.wait_ge(S["added"], k.reuse)
                            for j in range(TG):
                                last = nc.tensor.matmul(o[h][:, 0:2 * AWIN], row[:, h, j, 0:H],
                                                        hot[:, h, j, :, :].rearrange("p s w -> p (s w)"),
                                                        start=j == 0, stop=j == TG - 1)
                            last.then_inc(S["sums"], 1)

            @block.gpsimd
            def _(pool):
                nc.gpsimd.memset(acc[:, 1, :], 0.0).then_inc(s_init, 1)

            @block.vector
            def _(dve):
                nc.vector.memset(acc[:, 0, :], 0.0).then_inc(s_init, 1)
                nc.vector.tensor_copy(iota[:], a.iota[:, 0:AWIN]).then_inc(s_win, 1)
                nc.vector.tensor_copy(win[:], a.win0[:]).then_inc(s_win, 1)
                dve.wait_ge(s_win, 2)
                dve.wait_ge(s_init, 2)
                passes = dve.value_load(a.passes[0:1, 0:1], min_val=1, max_val=NBIN)
                for n in ("rel", "eq", "hot", "added"):
                    dve.sem_inc(S[n], CREDIT)
                with dve.Fori(0, passes) as p:
                    with dve.Fori(0, IT) as i:
                        m = dve.snap(p * IT + i)
                        for h in range(2):
                            k = Group(dve, m, h)
                            dve.wait_ge(in_[h], k.landed(1))
                            dve.wait_ge(S["sums"], k.reuse)
                            nc.vector.tensor_scalar(rel[:, h, :], row[:, h, :, H], a.baseB[:, ds(2 * i + h, 1)],
                                                    None, ALU.subtract).then_inc(S["rel"], 1)
                            dve.wait_ge(S["rel"], k.done)
                            nc.vector.tensor_tensor(eq[:, h], iota[:].unsqueeze(1).broadcast_to([P, TG, AWIN]),
                                                    rel[:, h, :].unsqueeze(2).broadcast_to([P, TG, AWIN]),
                                                    ALU.is_equal).then_inc(S["eq"], 1)
                            dve.wait_ge(S["eq"], k.done)
                            nc.vector.tensor_tensor(
                                hot[:, h], eq[:, h].unsqueeze(2).broadcast_to([P, TG, 2, AWIN]),
                                row[:, h, :, H + 1:H + 3].unsqueeze(3).broadcast_to([P, TG, 2, AWIN]),
                                ALU.mult).then_inc(S["hot"], 1)
                        for h in range(2):
                            k = Group(dve, m, h)
                            at = dve.value_load(win[0:1, ds(2 * i + h, 1)], min_val=0, max_val=NP - AWIN)
                            dve.wait_ge(S["sums"], k.done)
                            dve.wait_ge(S["added"], k.prev)
                            w = acc[:, :, ds(at, AWIN)]
                            nc.vector.tensor_tensor(w, w, o[h][:, 0:2 * AWIN].rearrange("p (s w) -> p s w", s=2),
                                                    ALU.add).then_inc(S["added"], 1)
                    nc.vector.tensor_scalar(iota[:], iota[:], float(AWIN), None, ALU.add).then_inc(s_win, 1)
                    nc.vector.tensor_scalar(win[:], win[:], AWIN, NP - AWIN, ALU.add, ALU.min).then_inc(s_win, 1)
                    dve.wait_ge(s_win, p * 2 + 4)

        oT = sb("oT", [P, NB * P])
        halfn = NB * P // 2
        m_ps = [core.bank[0], core.bank[1]]
        with nc.Block() as block:
            @block.sync
            def _(sp):
                sp.dma_start(nw[:, 1, :], ins["L3_gnn_node_w"][0:P, :]).then_inc(s_w, 16)
                sp.dma_start(nw[:, 0, :], ins["L3_gnn_node_w"][P:2 * P, :]).then_inc(s_w, 16)
                for q, n in enumerate(("node_b", "node_g", "node_be")):
                    sp.dma_start(rowb[:, q, :], ins[f"L3_gnn_{n}"].rearrange("(a n) -> a n", a=1).broadcast_to(
                        [P, H])).then_inc(s_w, 16)
                sp.wait_ge(s_w, 80)

            @block.tensor
            def _(pe):
                pe.wait_ge(s_w, 80)
                pe.sem_inc(S["turned"], 1)
                with pe.Fori(0, NI) as i:
                    pe.wait_ge(S["mixed_copied"], i + 1)
                    for q in range(2):
                        for s in range(2):
                            last = nc.tensor.matmul(m_ps[q][:, 0:halfn], nw[:, s, :],
                                                    acc[:, s, ds(i * NB * P + q * halfn, halfn)], start=s == 0,
                                                    stop=s == 1)
                    last.then_inc(S["mixed"], 1)
                    pe.wait_ge(S["mixed_copied"], i + 2)
                    pe.wait_ge(S["own"], i + 1)
                    for u in range(NB):
                        last = nc.tensor.transpose(core.bank[2 + u // 4][:, P * (u % 4):P * (u % 4) + P],
                                                   oT[:, u * P:(u + 1) * P], t.ident[:])
                    last.then_inc(S["turned"], 1)

            @block.scalar
            def _(act):
                act.sem_inc(S["mixed_copied"], 1)
                with act.Fori(0, NI) as i:
                    act.wait_ge(S["mixed"], i + 1)
                    act.wait_ge(S["turned"], i + 1)
                    for q in range(2):
                        last = nc.scalar.copy(oT[:, q * halfn:(q + 1) * halfn], m_ps[q][:, 0:halfn])
                    last.then_inc(S["mixed_copied"], 1)

            @block.vector
            def _(dve):
                dve.sem_inc(S["own"], 1)
                with dve.Fori(0, NI) as i:
                    dve.wait_ge(S["turned"], i + 2)
                    nc.vector.tensor_copy(flow[:, ds(i * NB, 4), :],
                                          core.bank[2][:, :].rearrange("p (u n) -> p u n", u=4))
                    nc.vector.tensor_copy(flow[:, ds(i * NB + 4, 1), :].rearrange("p a c -> p (a c)"),
                                          core.bank[3][:, 0:P]).then_inc(S["own"], 1)

        add_block(core, t, "node", flow, rowb)


def flow_attention(core, t, ins):
    nc = core.nc
    a = Bundle()
    a.table = nc.dram_tensor("flow_table_dram", [2 * NP, 256], F32).ap()
    a.rows = nc.dram_tensor("message_rows_dram", [EP, ROW], F32).ap()
    a.low_rows = nc.dram_tensor("low_rows_dram", [2, EP], BF16).ap()
    a.mask_rows = nc.dram_tensor("mask_rows_dram", [2, EP], BF16).ap()
    a.attn_rows = nc.dram_tensor("attn_rows_dram", [2, EP], F32).ap()
    a.spare = nc.dram_tensor("spare_dram", [2, TG, P, 1], I32).ap()
    a.base_dram = nc.dram_tensor("source_base_dram", [NG], F32).ap()
    with ExitStack() as ctx:
        sb = lambda n, s, d=F32: core.sb(f"a_{n}", s, d, ctx)
        a.parts = sb("parts", [P, NT, 2])
        a.iota = sb("iota", [P, P])
        a.iotaP, a.iotaP_int = sb("iotaP", [P, 1]), sb("iotaP_int", [P, 1], I32)
        a.meta = sb("meta", [P, ET, 4])
        a.attn = sb("attn", [P, ET])
        a.logit = a.attn
        a.yidx, a.pos = sb("yidx", [P, ET], I32), sb("pos", [P, ET], I32)
        a.baseB, a.win0 = sb("baseB", [P, NG]), sb("win0", [1, NG], I32)
        a.passes = sb("passes", [1, 1], I32)
        attention_nodes(core, t, ins, a)
        with ExitStack() as ectx:
            a.high = core.sb("a_high", [P, ET, 2], F32, ectx)
            a.bin = core.sb("a_bin", [P, ET], F32, ectx)
            edge_masks(core, t, ins, a)
            logits(core, t, ins, a)
            softmax(core, t, ins, a)
            source_order(core, t, a)
        messages(core, t, ins, a)
        flow_sums(core, t, ins, a)


def store(core, t, out):
    nc = core.nc
    s_out = core.sem("result_stored")
    whole = N // P
    with nc.Block() as block:
        @block.sync
        def _(sp):
            sp.dma_start(out[0:whole * P, :].rearrange("(t p) d -> p t d", p=P), t.x[:, 0:whole, :]).then_inc(
                s_out, 16)
            sp.dma_start(out[whole * P:N, :], t.x[0:N - whole * P, whole, :]).then_inc(s_out, 16)
            sp.wait_ge(s_out, 32)


def program(nc, ins, out, layers=4):
    with ExitStack() as ctx:
        core = Core(nc, ctx)
        t = Bundle()
        t.table = nc.dram_tensor("table_dram", [NP, D], F32).ap()
        with core.semaphores():
            prepare(core, t, ins)
        for layer in range(min(layers, 3)):
            with ExitStack() as lctx, core.semaphores():
                acc = Bundle()
                sb = lambda n, s: core.sb(f"l{layer}_{n}", s, F32, lctx)
                if layer == 1:
                    hR = sb("h", [P, NT, D])
                    table_plain(core, t, "t1", hR)
                    acc.S, acc.V = sb("acc_s", [64, 4, NP]), sb("acc_v", [96, 4, NP])
                    acc.halves = [[acc.S[:]], [acc.V[:]]]
                    edge_sums(core, t, "e1", acc)
                    finish_product(core, t, "f1", acc, t.w.post1, hR)
                    continue
                pre, post, fc, attrT, n_sc = ((t.w.pre0, t.w.post0, t.w.fc0, ins["attr64T"], 96) if layer == 0 else
                                              (t.w.pre2, t.w.post2, t.w.fc2, ins["attr8T"], 64))
                t.sc = sb("sc", [P, NT, n_sc + 96])
                node_tables(core, t, f"t{layer}", pre, n_sc)
                acc.A, acc.B, acc.C = sb("acc_a", [P, 3, NP]), sb("acc_b", [96, NP]), sb("acc_c", [96, NP])
                acc.halves = [[acc.A[:]], [acc.B[:], acc.C[:]]]
                if layer == 0:
                    acc.X = sb("acc_x", [96, 3, NP])
                    acc.halves[1].append(acc.X[:])
                mlp = Bundle()
                mlp.w, mlp.attrT = fc, attrT
                mlp.rin, mlp.kinds, mlp.width = (64, 3, 224) if layer == 0 else (8, 2, 192)
                mlp.scale = 1 / math.sqrt(mlp.rin)
                edge_sums(core, t, f"e{layer}", acc, mlp)
                finish_gated(core, t, f"f{layer}", acc, post, layer == 2)
        with core.semaphores(again=False):
            if layers > 3:
                flow_attention(core, t, ins)
            store(core, t, out)


LAYERS = 4


def kernel(**inputs):
    import concourse.bacc as _bacc
    from concourse import mybir as _mybir
    from concourse.bass_utils import run_bass_kernel_spmd as _run

    nc = _bacc.Bacc("TRN2", target_bir_lowering=False, num_devices=1)
    arrays = {k: np.asarray(v) for k, v in inputs.items() if k.startswith("L")}
    pad = ((0, EP - E), (0, 0))
    x = np.asarray(inputs["x"])
    src = np.pad(np.asarray(inputs["src"]), (0, EP - E), constant_values=N - 1)
    dst = np.pad(np.asarray(inputs["dst"]), (0, EP - E), constant_values=N - 1)
    arrays["x_pad"] = np.pad(x, ((0, NP - N), (0, 0)))
    arrays["attr_pt"] = np.pad(np.asarray(inputs["node_vec1"])[:, 0], (0, NP - N)).reshape(NT, P).T
    arrays["src_pt"], arrays["dst_pt"] = src.reshape(ET, P).T, dst.reshape(ET, P).T
    arrays["src_rows"], arrays["dst_rows"] = src.reshape(NG, GE), dst.reshape(NG, GE)
    arrays["e4_pt"] = np.pad(np.asarray(inputs["edge_attr_4"]), pad).reshape(ET, P, 4).transpose(1, 0, 2).reshape(
        P, ET * 4)
    arrays["attr64T"] = np.pad(np.asarray(inputs["edge_attr_64"]), pad).T
    arrays["attr8T"] = np.pad(np.asarray(inputs["edge_attr_8"]), pad).T
    arrays = {k: np.ascontiguousarray(v) for k, v in arrays.items()}
    ins = {k: nc.dram_tensor(f"in_{k}", v.shape, _mybir.dt.from_np(v.dtype), kind="ExternalInput").ap()
           for k, v in arrays.items()}
    out = nc.dram_tensor("result", (N, D), F32, kind="ExternalOutput").ap()
    program(nc, ins, out, LAYERS)
    r = _run(nc, [{f"in_{k}": v for k, v in arrays.items()}], core_ids=[0])
    return r.results[0]["result"]
```

```python
import math
from contextlib import ExitStack, contextmanager


import numpy as np
import concourse.bass as bass
from concourse import mybir

F32 = mybir.dt.float32
BF16 = mybir.dt.bfloat16
I32 = mybir.dt.int32
ALU = mybir.AluOpType
ACT = mybir.ActivationFunctionType
AX = mybir.AxisListType
ds = bass.ds

P = 128
N, D = 3125, 160
E = 103125
NT = 25
NP = NT * P
GE = 512
TG = GE // P
UN = 4
NG = 204
IT = NG // UN
IT2 = NG // 2
EP = NG * GE
ET = EP // P
WIN = 32
NB = 5
NI = NT // NB
EPS = 1e-5
ROW = 132
NBIN = 98
AWIN = 64
INV2, INV3, INV6 = 1 / math.sqrt(2), 1 / math.sqrt(3), 1 / math.sqrt(6)
CROSS = {(0, 1, 2): 1.0, (1, 2, 0): 1.0, (2, 0, 1): 1.0, (0, 2, 1): -1.0, (1, 0, 2): -1.0, (2, 1, 0): -1.0}


class Bundle:
    pass


class Core:

    def __init__(self, nc, ctx):
        self.nc, self.ctx = nc, ctx
        self.bank = [ctx.enter_context(nc.psum_tensor(f"bank{i}", [P, 512], F32)) for i in range(8)]

    def sb(self, name, shape, dt=F32, ctx=None):
        return (ctx or self.ctx).enter_context(self.nc.sbuf_tensor(name, shape, dt))

    def sem(self, name):
        s = self.sem_ctx.enter_context(self.nc.semaphore(name))
        self.sems.append(s)
        return s

    def gpsimd_dma_sem(self, name):
        return self.ctx.enter_context(self.nc.semaphore(name))

    @contextmanager
    def semaphores(self, again=True):
        with ExitStack() as self.sem_ctx:
            self.sems = []
            yield
            if again:
                with self.nc.Block() as block:
                    @block.gpsimd
                    def _(pool):
                        for s in self.sems:
                            pool.sem_clear(s)


def linker(eng, sem):
    count = [0]

    def link(ins):
        count[0] += 1
        ins.then_inc(sem, 1)
        eng.wait_ge(sem, count[0])

    return link


CREDIT = 4


class Group:

    def __init__(self, eng, i, c, base=0):
        static = isinstance(i, int) and isinstance(base, int)
        hold = (lambda v: v) if static else eng.snap
        self.at = i * UN + c
        self.n = hold((base + i) * UN + c)
        self.h2, self.h4 = c % 2, c % 4
        self.turn = base + i + c // UN
        self.turn2 = (base + i) * 2 + c // 2
        self.done, self.prev, self.back2, self.back4 = (self.n + k for k in (CREDIT + 1, CREDIT, CREDIT - 1, CREDIT - 3))
        self.fixed = isinstance(i, int)

    def landed(self, k):
        return self.turn * (16 * k) + 16 * k

    def landed2(self, k):
        return self.turn2 * (16 * k) + 16 * k

    def span(self, size, offset=0, width=None):
        width = width or size
        if self.fixed:
            return slice(self.at * size + offset, self.at * size + offset + width)
        return ds(self.at * size + offset, width)


def run(eng, step, ahead=0, behind=0, base=0):
    def of(i, k, whole):
        return lambda d: Group(eng, i, k + d, base) if whole or 0 <= k + d < NG else None

    count = (NG - ahead - behind) // UN
    for k in range(-ahead, behind):
        step(of(0, k, False))
    with eng.Fori(0, count) as i:
        for u in range(UN):
            step(of(i, behind + u, True))
    for k in range(behind + UN * count, NG + behind):
        step(of(0, k, False))


def weight_lists():
    loads, scales = [], []

    def put(tile, slot, r, c, src, scale=1.0):
        rows, cols = src.shape
        dst = tile[r:r + rows, slot, c:c + cols]
        loads.append((dst, src))
        if scale != 1.0:
            scales.append((dst, scale))

    return put, loads, scales


def weights_first(core, w, ins):
    put, loads, scales = weight_lists()
    w.post0 = core.sb("w_post0", [P, 9, 96])
    w.pre0 = core.sb("w_pre0", [P, 2, 192])
    w.fc0 = core.sb("w_fc0", [64, 1, 64 + 224])
    put_pre(put, w.pre0, ins["L0_gnn_lin1_ws"], ins["L0_gnn_sc_ws"], ins["L0_gnn_lin1_wv"], ins["L0_gnn_sc_wv"])
    put(w.fc0, 0, 0, 0, ins["L0_gnn_fc_w1"])
    put(w.fc0, 0, 0, 64, ins["L0_gnn_fc_w2"])
    ls, lv = ins["L0_gnn_lin2_ws"], ins["L0_gnn_lin2_wv"]
    cs, cv = 1 / 32 / math.sqrt(96), 1 / 32 / math.sqrt(128)
    put(w.post0, 0, 0, 0, ls[0:64, :], cs)
    for d in range(3):
        put(w.post0, 1, 32 * d, 0, ls[64:96, :], cs * INV3)
        put(w.post0, 2 + d, 64, 32 * d, lv[0:64, :], cv)
        put(w.post0, 5, 32 * d, 32 * d, lv[64:96, :], cv)
    for (d, j, k), sign in CROSS.items():
        put(w.post0, 6 + k, 32 * j, 32 * d, lv[96:128, :], cv * INV2 * sign)

    return [w.post0, w.pre0], loads, scales


def put_pre(put, pre, lin_s, sc_s, lin_v, sc_v):
    put(pre, 0, 0, 0, lin_s, 1 / 8)
    put(pre, 0, 0, 64, sc_s, 1 / 8)
    for d in range(3):
        put(pre, 1, 32 * d, 32 * d, lin_v, 1 / math.sqrt(32))
        put(pre, 1, 32 * d, 96 + 32 * d, sc_v, 1 / math.sqrt(32))


def weights_later(core, w, ins):
    put, loads, scales = weight_lists()
    w.post1 = core.sb("w_post1", [P, 13, 96])
    w.post2 = core.sb("w_post2", [P, 6, 96])
    w.pre2 = core.sb("w_pre2", [P, 2, 192])
    w.fc2 = core.sb("w_fc2", [64, 1, 64 + 192])
    put_pre(put, w.pre2, ins["L2_gnn_W1_s"], ins["L2_gnn_W_sc_s"], ins["L2_gnn_W1_v"], ins["L2_gnn_W_sc_v"])
    put(w.fc2, 0, 0, 0, ins["L2_gnn_fcW1"])
    put(w.fc2, 0, 0, 64, ins["L2_gnn_fcW2"])

    c0, c1 = 1 / math.sqrt(96), math.sqrt(3 / 128)
    put(w.post1, 0, 0, 0, ins["L1_gnn_W1"], c0)
    for d in range(3):
        put(w.post1, 1 + d, 0, 32 * d, ins["L1_gnn_W3"], c1 * INV3)
        put(w.post1, 4, 32 * d, 32 * d, ins["L1_gnn_W4"], c1 * INV3)
        put(w.post1, 5 + d, 32 * d, 0, ins["L1_gnn_W2"], c0 * INV3)
        put(w.post1, 12, 32 * d, 32 * d, ins["L1_gnn_Wv"], 1 / math.sqrt(32))
    for (d, j, k), sign in CROSS.items():
        put(w.post1, 8 + k, 32 * j, 32 * d, ins["L1_gnn_W5"], c1 * INV6 * sign)
    put(w.post1, 11, 0, 0, ins["L1_gnn_Ws"], 1 / 8)

    ls, lv, la = ins["L2_gnn_W2_s"], ins["L2_gnn_W2_v"], ins["L2_gnn_W3"]
    cs = 1 / 8 / math.sqrt(10) / math.sqrt(96)
    put(w.post2, 0, 0, 0, ls[0:64, :], cs)
    put(w.post2, 0, 0, 64, la[0:64, :], cs * 0.1)
    for d in range(3):
        put(w.post2, 1, 32 * d, 0, ls[64:96, :], cs * INV3)
        put(w.post2, 1, 32 * d, 64, la[64:96, :], cs * INV3 * 0.1)
        put(w.post2, 2 + d, 64, 32 * d, lv[0:64, :], cs)
        put(w.post2, 5, 32 * d, 32 * d, lv[64:96, :], cs)
    return [w.post1, w.post2, w.pre2], loads, scales


def prepare(core, t, ins):
    nc = core.nc
    t.x = core.sb("x_res", [P, NT, D])
    t.attr = core.sb("node_attr", [P, NT])
    t.e4 = core.sb("edge_vec", [P, ET, 4])
    t.srcI = core.sb("src_idx", [P, ET], I32)
    t.dstrel = core.sb("dst_in_window", [P, ET])
    t.ident = core.sb("ident", [P, P])
    t.iotaW = core.sb("iota_window", [P, WIN])
    t.win0 = core.sb("window_base", [1, NG], I32)
    t.passes = core.sb("passes", [1, 1], I32)
    t.w = Bundle()
    zero_tiles, loads, scales = weights_first(core, t.w, ins)
    t.base_dram = nc.dram_tensor("base_dram", [NG], F32).ap()
    s_zero, s_w, s_in, s_base, s_baseload = (core.sem(n) for n in (
        "w_zeroed", "w_loaded", "prep_loaded", "bases_stored", "bases_loaded"))
    s_iota, s_ident, s_red, s_span, s_bases, s_dve = (core.sem(n) for n in (
        "iota_made", "ident_made", "span_reduced", "span_ready", "bases_ready", "prep_dve"))
    with ExitStack() as ctx:
        sb = lambda n, s, d=F32: core.sb(n, s, d, ctx)
        dstI = sb("dst_idx", [P, ET], I32)
        rows = sb("dst_rows", [IT2, 2, GE], I32)
        rowsF = sb("dst_rows_f", [IT2, 2, GE])
        lo = sb("row_min", [IT2, 2])
        hi = sb("row_max", [IT2, 2])
        span = sb("span", [P, 1])
        spanR = sb("span_all", [P, 1])
        spanI = sb("span_int", [P, 1], I32)
        iotaI = sb("iota_int", [P, WIN], I32)
        baseB = sb("base_all", [P, NG])
        block = ctx.enter_context(nc.Block())

        @block.sync
        def _(sp):
            sp.dma_start(rows[:], ins["dst_rows"].rearrange("(i h) e -> i h e", h=2)).then_inc(s_in, 16)
            sp.dma_start(dstI[:], ins["dst_pt"]).then_inc(s_in, 16)
            sp.dma_start(t.srcI[:], ins["src_pt"]).then_inc(s_in, 16)
            sp.dma_start(t.attr[:], ins["attr_pt"]).then_inc(s_in, 16)
            sp.dma_start(t.x[:], ins["x_pad"].rearrange("(t p) d -> p t d", p=P)).then_inc(s_in, 16)
            sp.dma_start(t.e4[:], ins["e4_pt"].rearrange("p (t k) -> p t k", k=4)).then_inc(s_in, 16)
            sp.wait_ge(s_zero, len(zero_tiles))
            for dst, src in loads:
                sp.dma_start(dst, src).then_inc(s_w, 16)
            sp.wait_ge(s_bases, 1)
            sp.dma_start(t.base_dram.rearrange("(i h) -> i h", h=2), lo[:]).then_inc(s_base, 16)
            sp.wait_ge(s_base, 16)
            sp.dma_start(baseB[:], t.base_dram.rearrange("(a g) -> a g", a=1).broadcast_to([P, NG])).then_inc(
                s_baseload, 16)
            sp.wait_ge(s_baseload, 16)

        @block.gpsimd
        def _(pool):
            nc.gpsimd.iota(iotaI[:], pattern=[[1, WIN]], base=0, channel_multiplier=0).then_inc(s_iota, 1)
            nc.gpsimd.memset(t.ident[:], 0.0).then_inc(s_ident, 1)
            pool.wait_ge(s_ident, 1)
            nc.gpsimd.affine_select(out=t.ident[:], in_=t.ident[:], compare_op=ALU.not_equal, fill=1.0, base=0,
                                    pattern=[[-1, P]], channel_multiplier=1).then_inc(s_ident, 1)
            pool.wait_ge(s_span, 1)
            nc.gpsimd.partition_all_reduce(spanR[:], span[:], P, bass.bass_isa.ReduceOp.max).then_inc(s_red, 1)

        @block.vector
        def _(dve):
            link = linker(dve, s_dve)
            for z in zero_tiles:
                nc.vector.memset(z[:], 0.0).then_inc(s_zero, 1)
            link(nc.vector.memset(span[:], 0.0))
            dve.wait_ge(s_iota, 1)
            nc.vector.tensor_copy(t.iotaW[:], iotaI[:])
            dve.wait_ge(s_in, 96)
            link(nc.vector.tensor_copy(rowsF[:], rows[:]))
            nc.vector.tensor_reduce(lo[:], rowsF[:], AX.X, ALU.min).then_inc(s_bases, 1)
            link(nc.vector.tensor_reduce(hi[:], rowsF[:], AX.X, ALU.max))
            dve.wait_ge(s_bases, 1)
            link(nc.vector.tensor_tensor(hi[:], hi[:], lo[:], ALU.subtract))
            nc.vector.tensor_reduce(span[0:IT2, :], hi[:], AX.X, ALU.max).then_inc(s_span, 1)
            dve.wait_ge(s_red, 1)
            link(nc.vector.tensor_copy(spanI[:], spanR[:]))
            link(nc.vector.tensor_scalar(spanI[:], spanI[:], int(math.log2(WIN)), None, ALU.logical_shift_right))
            link(nc.vector.tensor_scalar(t.passes[:], spanI[0:1, :], 1, None, ALU.add))
            link(nc.vector.tensor_copy(t.dstrel[:], dstI[:]))
            dve.wait_ge(s_baseload, 16)
            nc.vector.tensor_copy(t.win0[:], baseB[0:1, :])
            rel = t.dstrel[:].rearrange("p (g j) -> p g j", j=TG)
            link(nc.vector.tensor_tensor(rel, rel, baseB[:].unsqueeze(2).broadcast_to([P, NG, TG]), ALU.subtract))
            dve.wait_ge(s_w, 16 * len(loads))
            for dst, scale in scales:
                nc.vector.tensor_scalar(dst, dst, scale, None, ALU.mult)


def center(core, t, name, xm, rstd):
    nc = core.nc
    s_dve, s_var, s_std = (core.sem(f"{name}_{n}") for n in ("stat_dve", "var_ready", "std_ready"))
    with ExitStack() as ctx:
        sq = core.sb(f"{name}_sq", [P, NT, D], F32, ctx)
        m = core.sb(f"{name}_mean", [P, NT], F32, ctx)
        v = core.sb(f"{name}_var", [P, NT], F32, ctx)
        std = core.sb(f"{name}_std", [P, NT], F32, ctx)
        block = ctx.enter_context(nc.Block())

        @block.vector
        def _(dve):
            link = linker(dve, s_dve)
            link(nc.vector.tensor_reduce(m[:], t.x[:], AX.X, ALU.add))
            link(nc.vector.tensor_scalar(m[:], m[:], 1.0 / D, None, ALU.mult))
            link(nc.vector.tensor_tensor(xm[:], t.x[:], m[:].unsqueeze(2).broadcast_to([P, NT, D]), ALU.subtract))
            link(nc.vector.tensor_tensor(sq[:], xm[:], xm[:], ALU.mult))
            link(nc.vector.tensor_reduce(v[:], sq[:], AX.X, ALU.add))
            nc.vector.tensor_scalar(v[:], v[:], 1.0 / D, EPS, ALU.mult, ALU.add).then_inc(s_var, 1)
            dve.wait_ge(s_std, 1)
            link(nc.vector.reciprocal(rstd[:], std[:]))

        @block.scalar
        def _(act):
            act.wait_ge(s_var, 1)
            nc.scalar.activation(std[:], v[:], ACT.Sqrt).then_inc(s_std, 1)



def node_tables(core, t, name, weights, n_sc):
    nc = core.nc
    S = {n: core.sem(f"{name}_{n}") for n in ("h_ready", "turned", "turned_copied", "lin", "lin_copied", "stored")}
    width = 64 + n_sc
    with ExitStack() as ctx:
        xm = core.sb(f"{name}_xm", [P, NT, D], F32, ctx)
        rstd = core.sb(f"{name}_rstd", [P, NT], F32, ctx)
        center(core, t, name, xm, rstd)
        h = core.sb(f"{name}_h", [P, NB, D], F32, ctx)
        hT = core.sb(f"{name}_hT", [96, NB, 2, P], F32, ctx)
        tab = core.sb(f"{name}_tab", [P, NB, D], F32, ctx)
        block = ctx.enter_context(nc.Block())
        turned = [core.bank[u // 2][:, 256 * (u % 2):256 * (u % 2) + 256] for u in range(NB)]
        lin = [core.bank[3 + u] for u in range(NB)]

        @block.scalar
        def _(act):
            with act.Fori(0, NI) as i:
                act.wait_ge(S["turned"], i + 1)
                for u in range(NB):
                    tile = i * NB + u
                    nc.scalar.activation(h[:, u, 0:64], xm[:, ds(tile, 1), 0:64], ACT.Relu, scale=rstd[:, ds(tile, 1)])
                    last = nc.scalar.activation(
                        h[:, u, 64:D].rearrange("p (i c) -> p c i", i=3),
                        xm[:, ds(tile, 1), 64:D].rearrange("p a (c i) -> p (a c) i", i=3), ACT.Relu,
                        scale=rstd[:, ds(tile, 1)])
                last.then_inc(S["h_ready"], 1)

        @block.tensor
        def _(pe):
            pe.sem_inc(S["turned"], 1)
            pe.sem_inc(S["lin"], 1)
            with pe.Fori(0, NI) as i:
                pe.wait_ge(S["h_ready"], i + 1)
                pe.wait_ge(S["turned_copied"], i + 1)
                for u in range(NB):
                    nc.tensor.transpose(turned[u][0:96, P:2 * P], h[:, u, 64:D], t.ident[:])
                    last = nc.tensor.transpose(turned[u][0:64, 0:P], h[:, u, 0:64], t.ident[:])
                last.then_inc(S["turned"], 1)
                pe.wait_ge(S["turned_copied"], i + 2)
                pe.wait_ge(S["lin_copied"], i + 1)
                for u in range(NB):
                    nc.tensor.matmul(lin[u][:, 0:width], hT[0:64, u, 0, :], weights[0:64, 0, 0:width], start=True,
                                     stop=False, skip_group_check=True)
                    last = nc.tensor.matmul(lin[u][:, width:width + 192], hT[0:96, u, 1, :], weights[0:96, 1, 0:192],
                                            start=False, stop=True, skip_group_check=True)
                last.then_inc(S["lin"], 1)

        @block.vector
        def _(dve):
            dve.sem_inc(S["turned_copied"], 1)
            dve.sem_inc(S["lin_copied"], 1)
            with dve.Fori(0, NI) as i:
                dve.wait_ge(S["turned"], i + 2)
                dve.wait_ge(S["lin"], i + 1)
                for u in range(NB):
                    nc.vector.tensor_copy(hT[0:64, u, 0, :], turned[u][0:64, 0:P])
                    last = nc.vector.tensor_copy(hT[0:96, u, 1, :], turned[u][0:96, P:2 * P])
                last.then_inc(S["turned_copied"], 1)
                dve.wait_ge(S["lin"], i + 2)
                dve.wait_ge(S["stored"], i * 16 + 16)
                for u in range(NB):
                    tile = i * NB + u
                    a = t.attr[:, ds(tile, 1)]
                    nc.vector.tensor_scalar(tab[:, u, 0:64], lin[u][:, 0:64], a, None, ALU.mult)
                    nc.vector.tensor_scalar(tab[:, u, 64:D], lin[u][:, width:width + 96], a, None, ALU.mult)
                    nc.vector.tensor_scalar(t.sc[:, ds(tile, 1), 0:n_sc].rearrange("p a c -> p (a c)"),
                                            lin[u][:, 64:width], a, None, ALU.mult)
                    last = nc.vector.tensor_scalar(t.sc[:, ds(tile, 1), n_sc:n_sc + 96].rearrange("p a c -> p (a c)"),
                                                   lin[u][:, width + 96:width + 192], a, None, ALU.mult)
                last.then_inc(S["lin_copied"], 1)

        @block.sync
        def _(sp):
            sp.sem_inc(S["stored"], 16)
            table = t.table.rearrange("(i u p) d -> i p u d", u=NB, p=P)
            with sp.Fori(0, NI) as i:
                sp.wait_ge(S["lin_copied"], i + 2)
                sp.dma_start(table[ds(i, 1)].rearrange("a p u d -> (a p) u d"), tab[:]).then_inc(S["stored"], 16)
            sp.wait_ge(S["stored"], NI * 16 + 16)


def table_plain(core, t, name, hR, zeroed):
    nc = core.nc
    s_h, s_out = core.sem(f"{name}_h_ready"), core.sem(f"{name}_stored")
    with ExitStack() as ctx:
        xm = core.sb(f"{name}_xm", [P, NT, D], F32, ctx)
        rstd = core.sb(f"{name}_rstd", [P, NT], F32, ctx)
        center(core, t, name, xm, rstd)
        block = ctx.enter_context(nc.Block())

        @block.scalar
        def _(act):
            with act.Fori(0, NI) as i:
                for u in range(NB):
                    tile = i * NB + u
                    nc.scalar.activation(hR[:, ds(tile, 1), 0:64], xm[:, ds(tile, 1), 0:64], ACT.Relu,
                                         scale=rstd[:, ds(tile, 1)])
                    last = nc.scalar.activation(
                        hR[:, ds(tile, 1), 64:D].rearrange("p a (i c) -> p (a c) i", i=3),
                        xm[:, ds(tile, 1), 64:D].rearrange("p a (c i) -> p (a c) i", i=3), ACT.Relu,
                        scale=rstd[:, ds(tile, 1)])
                last.then_inc(s_h, 1)

        @block.vector
        def _(dve):
            for z in zeroed:
                nc.vector.memset(z[:], 0.0)

        @block.sync
        def _(sp):
            sp.wait_ge(s_h, NI)
            sp.dma_start(t.table.rearrange("(t p) d -> p t d", p=P), hR[:]).then_inc(s_out, 16)
            sp.wait_ge(s_out, 16)


def edge_sums(core, t, name, acc, mlp=None, extra=()):
    nc = core.nc
    names = ["attr_used", "hidden_ready", "weights_ready", "sums_ready", "eq_ready", "products_ready", "added"]
    S = {n: core.sem(f"{name}_{n}") for n in names}
    attr_in = [core.sem(f"{name}_attr_loaded{h}") for h in range(2)]
    rows_in = [core.gpsimd_dma_sem(f"{name}_rows_gathered{h}") for h in range(4)]
    s_idx, s_zero, s_win = core.sem(f"{name}_indices_copied"), core.sem(f"{name}_zeroed"), core.sem(f"{name}_windows")
    s_extra = core.sem(f"{name}_extra")
    kinds = 0 if mlp is None else mlp.kinds
    with ExitStack() as ctx:
        sb = lambda n, s, d=F32: core.sb(f"{name}_{n}", s, d, ctx)
        idx = sb("idx", [P, 4, TG], I32)
        rows = sb("rows", [P, 4, TG, D])
        eq = sb("eq", [P, 2, TG, WIN])
        hot = sb("hot", [P, 2, TG, 4, WIN])
        iota = sb("iota", [P, WIN])
        win = sb("win", [1, NG], I32)
        if mlp:
            attr = sb("attr", [mlp.rin, 2, GE])
            hid = sb("hid", [64, 2, GE])
            ps = sb("prod_s", [P, 2, TG, 128])
            pv = sb("prod_v", [P, 2, TG, kinds, 96])
        block = ctx.enter_context(nc.Block())
        hid_ps = [core.bank[0], core.bank[1]]
        w_ps = [[core.bank[2], core.bank[3]], [core.bank[4], core.bank[5]]]
        sum_ps = [core.bank[6], core.bank[7]]

        def passes(eng, step, ahead=0, behind=0):
            count = eng.value_load(t.passes[0:1, 0:1], min_val=1, max_val=NBIN)
            with eng.Fori(0, count) as p:
                run(eng, step, ahead, behind, base=eng.snap(p * IT))

        @block.sync
        def _(sp):
            for dst, src in extra:
                sp.dma_start(dst, src).then_inc(s_extra, 16)

            def step(at):
                k = at(0)
                sp.wait_ge(S["attr_used"], k.back2)
                sp.dma_start(attr[:, k.h2, :], mlp.attrT[:, k.span(GE)]).then_inc(attr_in[k.h2], 16)

            if mlp:
                passes(sp, step)
            if extra:
                sp.wait_ge(s_extra, 16 * len(extra))

        @block.gpsimd
        def _(pool):
            for a in acc.halves[1]:
                nc.gpsimd.memset(a, 0.0).then_inc(s_zero, 1)

            def step(at):
                k = at(0)
                pool.wait_ge(S["products_ready"] if mlp else S["sums_ready"], k.back4)
                nc.gpsimd.tensor_copy(idx[:, k.h4, :], t.srcI[:, k.span(TG)]).then_inc(s_idx, 1)
                pool.wait_ge(s_idx, 1)
                pool.sem_clear(s_idx)
                for j in range(TG):
                    nc.gpsimd.indirect_dma_start(
                        rows[:, k.h4, j, :], None, t.table,
                        bass.IndirectOffsetOnAxis(ap=idx[:, k.h4, j:j + 1], axis=0)).then_inc(rows_in[k.h4], 16)

            passes(pool, step)

        if mlp:
            @block.scalar
            def _(act):
                act.sem_inc(S["hidden_ready"], CREDIT)

                def step(at):
                    k = at(0)
                    act.wait_ge(S["attr_used"], k.done)
                    act.wait_ge(S["weights_ready"], k.back2)
                    nc.scalar.activation(hid[:, k.h2, :], hid_ps[k.h2][0:64, :], ACT.Silu,
                                         scale=mlp.scale).then_inc(S["hidden_ready"], 1)

                passes(act, step)

        @block.tensor
        def _(pe):
            pe.sem_inc(S["sums_ready"], CREDIT)
            if mlp:
                pe.sem_inc(S["attr_used"], CREDIT)
                pe.sem_inc(S["weights_ready"], CREDIT)

            def hidden(k):
                pe.wait_ge(attr_in[k.h2], k.landed2(1))
                pe.wait_ge(S["hidden_ready"], k.back2)
                nc.tensor.matmul(hid_ps[k.h2][0:96, :], mlp.w[0:mlp.rin, 0, 0:96], attr[:, k.h2, :], start=True,
                                 stop=True).then_inc(S["attr_used"], 1)

            def edge_weights(k):
                pe.wait_ge(S["hidden_ready"], k.done)
                pe.wait_ge(S["products_ready"], k.back2)
                for j in range(TG):
                    last = nc.tensor.matmul(
                        w_ps[k.h2][j // 2][:, mlp.width * (j % 2):mlp.width * (j % 2 + 1)],
                        hid[:, k.h2, j * P:(j + 1) * P], mlp.w[:, 0, 64:64 + mlp.width], start=True, stop=True)
                last.then_inc(S["weights_ready"], 1)

            def sums(k):
                o = sum_ps[k.h2]
                pe.wait_ge(S["products_ready"], k.done)
                if not mlp:
                    pe.wait_ge(rows_in[k.h4], k.landed(TG))
                pe.wait_ge(S["added"], k.back2)
                for j in range(TG):
                    first, end = j == 0, j == TG - 1
                    hots = hot[:, k.h2, j, :, :].rearrange("p k w -> p (k w)")
                    if mlp:
                        nc.tensor.matmul(o[:, 0:4 * WIN], ps[:, k.h2, j, :], hots, start=first, stop=end,
                                         skip_group_check=True)
                        nc.tensor.matmul(o[0:96, 4 * WIN:5 * WIN], pv[:, k.h2, j, 0, :], hots[:, 0:WIN],
                                         start=False, stop=end, skip_group_check=True)
                        for q in range(1, kinds):
                            last = nc.tensor.matmul(o[0:96, (2 + 3 * q) * WIN:(5 + 3 * q) * WIN],
                                                    pv[:, k.h2, j, q, :], hots[:, WIN:4 * WIN], start=False,
                                                    stop=end, skip_group_check=True)
                    else:
                        nc.tensor.matmul(o[0:96, 0:4 * WIN], rows[:, k.h4, j, 64:D], hots, start=first, stop=end,
                                         skip_group_check=True)
                        last = nc.tensor.matmul(o[0:64, 4 * WIN:8 * WIN], rows[:, k.h4, j, 0:64], hots,
                                                start=False, stop=end, skip_group_check=True)
                last.then_inc(S["sums_ready"], 1)

            def step(at):
                if mlp:
                    if at(2):
                        hidden(at(2))
                    if at(1):
                        edge_weights(at(1))
                if at(0):
                    sums(at(0))

            passes(pe, step, ahead=2 if mlp else 0)

        @block.vector
        def _(dve):
            for a in acc.halves[0]:
                nc.vector.memset(a, 0.0).then_inc(s_zero, 1)
            nc.vector.tensor_copy(iota[:], t.iotaW[:]).then_inc(s_win, 1)
            nc.vector.tensor_copy(win[:], t.win0[:]).then_inc(s_win, 1)
            dve.wait_ge(s_win, 2)
            dve.wait_ge(s_zero, len(acc.halves[0]) + len(acc.halves[1]))
            for n in ("products_ready", "eq_ready", "added"):
                dve.sem_inc(S[n], CREDIT)

            def products(k):
                dve.wait_ge(S["sums_ready"], k.back2)
                nc.vector.tensor_tensor(eq[:, k.h2, :, :], iota[:].unsqueeze(1).broadcast_to([P, TG, WIN]),
                                        t.dstrel[:, k.span(TG)].unsqueeze(2).broadcast_to([P, TG, WIN]),
                                        ALU.is_equal).then_inc(S["eq_ready"], 1)
                dve.wait_ge(S["eq_ready"], k.done)
                last = nc.vector.tensor_tensor(
                    hot[:, k.h2, :, :, :], eq[:, k.h2, :, :].unsqueeze(2).broadcast_to([P, TG, 4, WIN]),
                    t.e4[:, k.span(TG), :].unsqueeze(3).broadcast_to([P, TG, 4, WIN]), ALU.mult)
                if mlp:
                    dve.wait_ge(S["weights_ready"], k.done)
                    dve.wait_ge(rows_in[k.h4], k.landed(TG))
                    for j in range(TG):
                        w = w_ps[k.h2][j // 2][:, mlp.width * (j % 2):mlp.width * (j % 2 + 1)]
                        nc.vector.tensor_tensor(
                            ps[:, k.h2, j, :].rearrange("p (a c) -> p a c", a=2),
                            w[:, 0:128].rearrange("p (a c) -> p a c", a=2),
                            rows[:, k.h4, j, 0:64].unsqueeze(1).broadcast_to([P, 2, 64]), ALU.mult)
                        last = nc.vector.tensor_tensor(
                            pv[:, k.h2, j, :, :].rearrange("p q (i c) -> p q i c", i=3),
                            w[:, 128:128 + 32 * kinds].rearrange("p (q c) -> p q c", q=kinds).unsqueeze(
                                2).broadcast_to([P, kinds, 3, 32]),
                            rows[:, k.h4, j, 64:D].rearrange("p (i c) -> p i c", i=3).unsqueeze(
                                1).broadcast_to([P, kinds, 3, 32]), ALU.mult)
                last.then_inc(S["products_ready"], 1)

            def add_sums(k):
                o = sum_ps[k.h2]
                at = dve.value_load(win[0:1, k.span(1)], min_val=0, max_val=NP - WIN)
                w = ds(at, WIN)
                dve.wait_ge(S["sums_ready"], k.done)
                dve.wait_ge(S["added"], k.prev)

                def add(dst, src):
                    return nc.vector.tensor_tensor(dst, dst, src, ALU.add)

                if mlp:
                    add(acc.A[0:64, 0, w], o[0:64, 0:WIN])
                    add(acc.A[64:P, :, w], o[64:P, WIN:4 * WIN].rearrange("p (k w) -> p k w", k=3))
                    add(acc.B[:, w], o[0:96, 4 * WIN:5 * WIN])
                    for d in range(3):
                        last = add(acc.C[32 * d:32 * d + 32, w], o[32 * d:32 * d + 32, (5 + d) * WIN:(6 + d) * WIN])
                    if kinds == 3:
                        last = add(acc.X[:, :, w], o[0:96, 8 * WIN:11 * WIN].rearrange("p (k w) -> p k w", k=3))
                else:
                    add(acc.V[:, :, w], o[0:96, 0:4 * WIN].rearrange("p (k w) -> p k w", k=4))
                    last = add(acc.S[:, :, w], o[0:64, 4 * WIN:8 * WIN].rearrange("p (k w) -> p k w", k=4))
                last.then_inc(S["added"], 1)

            def step(at):
                if at(1):
                    products(at(1))
                if at(-1):
                    add_sums(at(-1))

            count = dve.value_load(t.passes[0:1, 0:1], min_val=1, max_val=NBIN)
            with dve.Fori(0, count) as p:
                run(dve, step, ahead=1, behind=1, base=dve.snap(p * IT))
                nc.vector.tensor_scalar(iota[:], iota[:], float(WIN), None, ALU.add).then_inc(s_win, 1)
                nc.vector.tensor_scalar(win[:], win[:], WIN, NP - WIN, ALU.add, ALU.min).then_inc(s_win, 1)
                dve.wait_ge(s_win, p * 2 + 4)


def scale_weights(core, name, tiles, scales):
    nc = core.nc
    with nc.Block() as block:
        @block.vector
        def _(dve):
            for dst, scale in scales:
                nc.vector.tensor_scalar(dst, dst, scale, None, ALU.mult)


def finish_gated(core, t, name, acc, weights, last_layer):
    nc = core.nc
    S = {n: core.sem(f"{name}_{n}") for n in ("mixed", "mixed_copied", "turned", "pre", "sig", "used", "dve")}
    rot = last_layer
    cols = 64 if rot else 96
    srows = 65 if rot else 96
    with ExitStack() as ctx:
        sb = lambda n, s, d=F32: core.sb(f"{name}_{n}", s, d, ctx)
        sT = sb("sT", [96, NB * P])
        vT = sb("vT", [96, NB * P])
        pre = sb("pre", [P, NB, 192])
        sig = sb("sig", [P, NB, 96])
        tmp = sb("tmp", [P, NB, 96])
        if rot:
            conv = sb("conv", [P, NT, D])
            angle = sb("angle", [P, NT])
        s_ps = [core.bank[0], core.bank[1]]
        v_ps = [core.bank[2], core.bank[3]]
        out = [core.bank[4 + u // 2][:, 192 * (u % 2):192 * (u % 2) + 192] for u in range(NB)]
        half = NB * P // 2
        with nc.Block() as block:
            @block.tensor
            def _(pe):
                pe.sem_inc(S["turned"], 1)
                with pe.Fori(0, NI) as i:
                    pe.wait_ge(S["mixed_copied"], i + 1)
                    for q in range(2):
                        c = ds(i * NB * P + q * half, half)
                        nc.tensor.matmul(s_ps[q][0:srows, 0:half], weights[:, 0, 0:srows], acc.A[:, 0, c], start=True,
                                         stop=False)
                        nc.tensor.matmul(s_ps[q][0:srows, 0:half], weights[0:96, 1, 0:srows], acc.C[:, c],
                                         start=False, stop=True)
                        terms = [(weights[:, 2 + k, :], acc.A[:, k, c]) for k in range(3)]
                        terms.append((weights[0:96, 5, :], acc.B[:, c]))
                        if not rot:
                            terms += [(weights[0:96, 6 + k, :], acc.X[:, k, c]) for k in range(3)]
                        for m, (a, b) in enumerate(terms):
                            last = nc.tensor.matmul(v_ps[q][0:96, 0:half], a, b, start=m == 0,
                                                    stop=m == len(terms) - 1)
                    last.then_inc(S["mixed"], 1)
                    pe.wait_ge(S["mixed_copied"], i + 2)
                    pe.wait_ge(S["pre"], i + 1)
                    for u in range(NB):
                        nc.tensor.transpose(out[u][:, 0:srows], sT[0:srows, u * P:(u + 1) * P],
                                            t.ident[0:srows, 0:srows])
                        last = nc.tensor.transpose(out[u][:, 96:192], vT[:, u * P:(u + 1) * P], t.ident[0:96, 0:96])
                    last.then_inc(S["turned"], 1)

            @block.scalar
            def _(act):
                act.sem_inc(S["mixed_copied"], 1)
                with act.Fori(0, NI) as i:
                    act.wait_ge(S["mixed"], i + 1)
                    act.wait_ge(S["turned"], i + 1)
                    for q in range(2):
                        nc.scalar.copy(sT[0:srows, q * half:(q + 1) * half], s_ps[q][0:srows, 0:half])
                        last = nc.scalar.copy(vT[:, q * half:(q + 1) * half], v_ps[q][0:96, 0:half])
                    last.then_inc(S["mixed_copied"], 1)
                    if not rot:
                        act.wait_ge(S["pre"], i + 2)
                        act.wait_ge(S["used"], i + 1)
                        nc.scalar.activation(sig[:], pre[:, :, 0:96], ACT.Sigmoid).then_inc(S["sig"], 1)

            @block.vector
            def _(dve):
                dve.sem_inc(S["pre"], 1)
                dve.sem_inc(S["used"], 1)
                with dve.Fori(0, NI) as i:
                    dve.wait_ge(S["turned"], i + 2)
                    for u in range(NB):
                        tile = i * NB + u
                        a = t.attr[:, ds(tile, 1)]
                        if rot:
                            nc.vector.tensor_scalar(conv[:, ds(tile, 1), 0:64].rearrange("p a c -> p (a c)"),
                                                    out[u][:, 0:64], a, None, ALU.mult)
                            nc.vector.tensor_scalar(conv[:, ds(tile, 1), 64:D].rearrange("p a c -> p (a c)"),
                                                    out[u][:, 96:192], a, None, ALU.mult)
                            last = nc.vector.tensor_scalar(angle[:, ds(tile, 1)], out[u][:, 64:65], a, None, ALU.mult)
                        else:
                            last = nc.vector.scalar_tensor_tensor(
                                out=pre[:, u, :], in0=out[u], scalar=a,
                                in1=t.sc[:, ds(tile, 1), :].rearrange("p a c -> p (a c)"), op0=ALU.mult, op1=ALU.add)
                    last.then_inc(S["pre"], 1)
                    if not rot:
                        dve.wait_ge(S["sig"], i + 1)
                        dve.wait_ge(S["pre"], i + 2)
                        xs = t.x[:, ds(i * NB, NB), 0:64]
                        nc.vector.tensor_tensor(tmp[:, :, 0:64], pre[:, :, 0:64], sig[:, :, 0:64],
                                                ALU.mult).then_inc(S["dve"], 1)
                        dve.wait_ge(S["dve"], i * 2 + 1)
                        nc.vector.tensor_tensor(xs, xs, tmp[:, :, 0:64], ALU.add)
                        vec = pre[:, :, 96:192].rearrange("p u (i c) -> p u i c", i=3)
                        nc.vector.tensor_tensor(vec, vec, sig[:, :, 64:96].unsqueeze(2).broadcast_to([P, NB, 3, 32]),
                                                ALU.mult).then_inc(S["dve"], 1)
                        dve.wait_ge(S["dve"], i * 2 + 2)
                        xv = t.x[:, ds(i * NB, NB), 64:D].rearrange("p u (c i) -> p u i c", i=3)
                        nc.vector.tensor_tensor(xv, xv, vec, ALU.add).then_inc(S["used"], 1)
                        dve.wait_ge(S["used"], i + 2)

        if rot:
            ang, tri = sb("ang", [P, 2, NT]), sb("tri", [P, 2, NT])
            turns, turnsI = sb("turns", [P, 2, NT]), sb("turns_int", [P, 2, NT], I32)
            s_rot, s_ang, s_tri = core.sem(f"{name}_rot"), core.sem(f"{name}_ang"), core.sem(f"{name}_tri")
            block = ctx.enter_context(nc.Block())

            @block.vector
            def _(dve):
                link = linker(dve, s_rot)
                nc.vector.tensor_copy(ang[:, 0, :], angle[:])
                link(nc.vector.tensor_scalar(ang[:, 1, :], angle[:], math.pi / 2, None, ALU.add))
                link(nc.vector.tensor_scalar(turns[:], ang[:], 1 / (2 * math.pi), None, ALU.mult))
                link(nc.vector.tensor_copy(turnsI[:], turns[:]))
                link(nc.vector.tensor_copy(turns[:], turnsI[:]))
                two_pi_hi = 6.28125
                two_pi_lo = 2 * math.pi - two_pi_hi
                link(nc.vector.scalar_tensor_tensor(out=ang[:], in0=turns[:], scalar=-two_pi_hi, in1=ang[:],
                                                    op0=ALU.mult, op1=ALU.add))
                link(nc.vector.scalar_tensor_tensor(out=ang[:], in0=turns[:], scalar=-two_pi_lo, in1=ang[:],
                                                    op0=ALU.mult, op1=ALU.add))
                link(nc.vector.tensor_scalar(turns[:], ang[:], math.pi, -2 * math.pi, ALU.is_gt, ALU.mult))
                link(nc.vector.tensor_tensor(ang[:], ang[:], turns[:], ALU.add))
                link(nc.vector.tensor_scalar(turns[:], ang[:], -math.pi, 2 * math.pi, ALU.is_lt, ALU.mult))
                link(nc.vector.tensor_tensor(ang[:], ang[:], turns[:], ALU.add))
                nc.vector.tensor_scalar(ang[:], ang[:], 3.1415925, -3.1415925, ALU.min, ALU.max).then_inc(s_ang, 1)
                dve.wait_ge(s_tri, 1)
                scv = t.sc[:, :, 0:D]
                link(nc.vector.tensor_tensor(scv, scv, tri[:, 1, :].unsqueeze(2).broadcast_to([P, NT, D]), ALU.mult))
                link(nc.vector.tensor_tensor(conv[:], conv[:], tri[:, 0, :].unsqueeze(2).broadcast_to([P, NT, D]),
                                             ALU.mult))
                link(nc.vector.tensor_tensor(conv[:], conv[:], scv, ALU.add))
                link(nc.vector.tensor_tensor(t.x[:, :, 0:64], t.x[:, :, 0:64], conv[:, :, 0:64], ALU.add))
                xv = t.x[:, :, 64:D].rearrange("p u (c i) -> p u i c", i=3)
                link(nc.vector.tensor_tensor(xv, xv, conv[:, :, 64:D].rearrange("p u (i c) -> p u i c", i=3),
                                             ALU.add))

            @block.scalar
            def _(act):
                act.wait_ge(s_ang, 1)
                nc.scalar.activation(tri[:], ang[:], ACT.Sin).then_inc(s_tri, 1)


def finish_product(core, t, name, acc, weights, hR):
    nc = core.nc
    S = {n: core.sem(f"{name}_{n}") for n in ("mixed", "mixed_copied", "out", "tmp", "used")}
    with ExitStack() as ctx:
        sb = lambda n, s, d=F32: core.sb(f"{name}_{n}", s, d, ctx)
        sT = sb("sT", [64, NB * P])
        vT = sb("vT", [96, NB * P])
        tmp = sb("tmp", [P, NB, D])
        half = NB * P // 2
        s_ps = [core.bank[0], core.bank[1]]
        v_ps = [core.bank[2], core.bank[3]]
        out = [core.bank[4 + u // 2][:, D * (u % 2):D * (u % 2) + D] for u in range(NB)]
        block = ctx.enter_context(nc.Block())

        @block.tensor
        def _(pe):
            pe.sem_inc(S["out"], 1)
            with pe.Fori(0, NI) as i:
                pe.wait_ge(S["mixed_copied"], i + 1)
                for q in range(2):
                    c = ds(i * NB * P + q * half, half)
                    terms = [(weights[0:96, 5 + k, :], acc.V[:, 1 + k, c]) for k in range(3)]
                    terms.append((weights[0:64, 0, :], acc.S[:, 0, c]))
                    for m, (a, b) in enumerate(terms):
                        nc.tensor.matmul(s_ps[q][0:96, 0:half], a, b, start=m == 0, stop=m == len(terms) - 1)
                    terms = [(weights[0:64, 1 + k, :], acc.S[:, 1 + k, c]) for k in range(3)]
                    terms.append((weights[0:96, 4, :], acc.V[:, 0, c]))
                    terms += [(weights[0:96, 8 + k, :], acc.V[:, 1 + k, c]) for k in range(3)]
                    for m, (a, b) in enumerate(terms):
                        last = nc.tensor.matmul(v_ps[q][0:96, 0:half], a, b, start=m == 0, stop=m == len(terms) - 1)
                last.then_inc(S["mixed"], 1)
                pe.wait_ge(S["mixed_copied"], i + 2)
                pe.wait_ge(S["tmp"], i + 1)
                for u in range(NB):
                    nc.tensor.matmul(out[u][:, 0:64], sT[:, u * P:(u + 1) * P], weights[0:64, 11, 0:64],
                                     start=u % 2 == 0, stop=False, skip_group_check=True)
                    last = nc.tensor.matmul(out[u][:, 64:D], vT[:, u * P:(u + 1) * P], weights[0:96, 12, :],
                                            start=False, stop=True, skip_group_check=True)
                last.then_inc(S["out"], 1)

        @block.scalar
        def _(act):
            act.sem_inc(S["mixed_copied"], 1)
            with act.Fori(0, NI) as i:
                act.wait_ge(S["mixed"], i + 1)
                act.wait_ge(S["out"], i + 1)
                for q in range(2):
                    nc.scalar.copy(sT[:, q * half:(q + 1) * half], s_ps[q][0:64, 0:half])
                    last = nc.scalar.copy(vT[:, q * half:(q + 1) * half], v_ps[q][0:96, 0:half])
                last.then_inc(S["mixed_copied"], 1)

        @block.vector
        def _(dve):
            dve.sem_inc(S["tmp"], 1)
            with dve.Fori(0, NI) as i:
                dve.wait_ge(S["out"], i + 2)
                for u in range(NB):
                    last = nc.vector.scalar_tensor_tensor(
                        out=tmp[:, u, :], in0=out[u], scalar=0.0,
                        in1=hR[:, ds(i * NB + u, 1), :].rearrange("p a c -> p (a c)"), op0=ALU.max, op1=ALU.add)
                last.then_inc(S["tmp"], 1)
                dve.wait_ge(S["tmp"], i + 2)
                xs = t.x[:, ds(i * NB, NB), 0:64]
                nc.vector.tensor_tensor(xs, xs, tmp[:, :, 0:64], ALU.add)
                xv = t.x[:, ds(i * NB, NB), 64:D].rearrange("p u (c i) -> p u i c", i=3)
                nc.vector.tensor_tensor(xv, xv, tmp[:, :, 64:D].rearrange("p u (i c) -> p u i c", i=3),
                                        ALU.add).then_inc(S["used"], 1)
                dve.wait_ge(S["used"], i + 1)


def attention_nodes(core, t, ins, a):
    nc = core.nc
    H = 128
    S = {n: core.sem(f"n3_{n}") for n in ("h_ready", "turned", "turned_copied", "lin", "lin_copied", "stored", "w",
                                          "self_dve", "var", "std")}
    with ExitStack() as ctx:
        sb = lambda n, s, d=F32: core.sb(f"n3_{n}", s, d, ctx)
        xm, rstd = sb("xm", [P, NT, D]), sb("rstd", [P, NT])
        center(core, t, "n3", xm, rstd)
        h = sb("h", [P, NB, D])
        hT = sb("hT", [P, NB, P])
        wy = sb("wy", [P, 512])
        ws = sb("ws", [P, 130])
        y = sb("y", [P, NB, 512])
        own = sb("own", [P, NT, H])
        hs = sb("hs", [P, NT, 32])
        rowb = sb("rowb", [P, 3, H])
        loads = [(wy[:, 0:256], ins["L3_gnn_d2t_w1"][0:128, :]), (wy[:, 256:512], ins["L3_gnn_t2d_w1"][0:128, :]),
                 (ws[:, 0:128], ins["L3_gnn_self_w"]), (ws[:, 128:129], ins["L3_gnn_w_att"][128:256, :]),
                 (ws[:, 129:130], ins["L3_gnn_w_att"][0:128, :])]
        for k, n in enumerate(("self_b", "self_g", "self_be")):
            loads.append((rowb[:, k, :], ins[f"L3_gnn_{n}"].rearrange("(a n) -> a n", a=1).broadcast_to([P, H])))
        turned = [core.bank[u // 4][:, P * (u % 4):P * (u % 4) + P] for u in range(NB)]
        lin = [(core.bank[2 + 2 * (u % 3)], core.bank[3 + 2 * (u % 3)]) for u in range(NB)]
        with nc.Block() as block:
            @block.scalar
            def _(act):
                with act.Fori(0, NI) as i:
                    act.wait_ge(S["turned_copied"], i + 1)
                    for u in range(NB):
                        tile = i * NB + u
                        last = nc.scalar.activation(h[:, u, :], xm[:, ds(tile, 1), :].rearrange("p a c -> p (a c)"),
                                                    ACT.Relu, scale=rstd[:, ds(tile, 1)])
                    last.then_inc(S["h_ready"], 1)

            @block.tensor
            def _(pe):
                pe.wait_ge(S["w"], 16 * len(loads))
                pe.sem_inc(S["turned"], 1)
                pe.sem_inc(S["lin"], 1)
                with pe.Fori(0, NI) as i:
                    pe.wait_ge(S["h_ready"], i + 1)
                    pe.wait_ge(S["turned_copied"], i + 1)
                    for u in range(NB):
                        last = nc.tensor.transpose(turned[u], h[:, u, 0:H], t.ident[:])
                    last.then_inc(S["turned"], 1)
                    pe.wait_ge(S["turned_copied"], i + 2)
                    for u in range(NB):
                        pe.wait_ge(S["lin_copied"], i * NB + max(u - 2, 0) + 1)
                        nc.tensor.matmul(lin[u][0][:, :], hT[:, u, :], wy[:], start=True, stop=True)
                        nc.tensor.matmul(lin[u][1][:, 0:130], hT[:, u, :], ws[:], start=True,
                                         stop=True).then_inc(S["lin"], 1)

            @block.vector
            def _(dve):
                dve.sem_inc(S["turned_copied"], 1)
                dve.sem_inc(S["lin_copied"], 1)
                with dve.Fori(0, NI) as i:
                    dve.wait_ge(S["h_ready"], i + 1)
                    dve.wait_ge(S["turned"], i + 2)
                    dve.wait_ge(S["lin"], i * NB + 1)
                    nc.vector.tensor_copy(hT[:, 0:4, :], core.bank[0][:, :].rearrange("p (u n) -> p u n", u=4))
                    nc.vector.tensor_copy(hT[:, 4, :], core.bank[1][:, 0:P])
                    nc.vector.tensor_copy(hs[:, ds(i * NB, NB), :], h[:, :, H:D]).then_inc(S["turned_copied"], 1)
                    dve.wait_ge(S["stored"], i * 32 + 32)
                    for u in range(NB):
                        tile = i * NB + u
                        dve.wait_ge(S["lin"], i * NB + u + 2)
                        nc.vector.tensor_copy(y[:, u, :], lin[u][0][:, :])
                        nc.vector.tensor_copy(own[:, ds(tile, 1), :].rearrange("p a c -> p (a c)"),
                                              lin[u][1][:, 0:H])
                        nc.vector.tensor_copy(a.parts[:, ds(tile, 1), :].rearrange("p a c -> p (a c)"),
                                              lin[u][1][:, H:H + 2]).then_inc(S["lin_copied"], 1)

            @block.sync
            def _(sp):
                for dst, src in loads:
                    sp.dma_start(dst, src).then_inc(S["w"], 16)
                sp.sem_inc(S["stored"], 32)
                table = a.table.rearrange("(s i u p) d -> s i p u d", s=2, u=NB, p=P)
                with sp.Fori(0, NI) as i:
                    sp.wait_ge(S["lin_copied"], i * NB + NB + 1)
                    for s in range(2):
                        sp.dma_start(table[s, ds(i, 1)].rearrange("a p u d -> (a p) u d"),
                                     y[:, :, 256 * s:256 * s + 256]).then_inc(S["stored"], 16)
                sp.wait_ge(S["stored"], NI * 32 + 32)

        add_block(core, t, "own", own, rowb, hs)


def add_block(core, t, name, v, rowb, hs=None):
    nc = core.nc
    H = 128
    s_dve, s_var, s_std = (core.sem(f"{name}_{n}") for n in ("block_dve", "block_var", "block_std"))
    with ExitStack() as ctx:
        sb = lambda n, s, d=F32: core.sb(f"{name}_{n}", s, d, ctx)
        sq, m, var, std = sb("sq", [P, NT, H]), sb("m", [P, NT]), sb("v", [P, NT]), sb("std", [P, NT])
        block = ctx.enter_context(nc.Block())

        @block.vector
        def _(dve):
            link = linker(dve, s_dve)
            tt = nc.vector.tensor_tensor
            per_node = lambda a: a.unsqueeze(2).broadcast_to([P, NT, H])
            per_col = lambda k: rowb[:, k, :].unsqueeze(1).broadcast_to([P, NT, H])
            link(tt(v[:], v[:], per_col(0), ALU.add))
            link(nc.vector.tensor_reduce(m[:], v[:], AX.X, ALU.add))
            link(nc.vector.tensor_scalar(m[:], m[:], 1.0 / H, None, ALU.mult))
            link(tt(v[:], v[:], per_node(m[:]), ALU.subtract))
            link(tt(sq[:], v[:], v[:], ALU.mult))
            link(nc.vector.tensor_reduce(var[:], sq[:], AX.X, ALU.add))
            nc.vector.tensor_scalar(var[:], var[:], 1.0 / H, EPS, ALU.mult, ALU.add).then_inc(s_var, 1)
            dve.wait_ge(s_std, 1)
            link(nc.vector.reciprocal(std[:], std[:]))
            link(tt(v[:], v[:], per_node(std[:]), ALU.mult))
            link(tt(v[:], v[:], per_col(1), ALU.mult))
            link(tt(v[:], v[:], per_col(2), ALU.add))
            xs = t.x[:, :, 0:H]
            link(nc.vector.scalar_tensor_tensor(out=xs, in0=v[:], scalar=0.0, in1=xs, op0=ALU.max, op1=ALU.add))
            if hs is not None:
                link(tt(t.x[:, :, H:D], t.x[:, :, H:D], hs[:], ALU.add))

        @block.scalar
        def _(act):
            act.wait_ge(s_var, 1)
            nc.scalar.activation(std[:], var[:], ACT.Sqrt).then_inc(s_std, 1)


def edge_masks(core, t, ins, a):
    nc = core.nc
    s_in, s_out, s_dve, s_rows, s_iota = (core.sem(f"m3_{n}") for n in ("loaded", "stored", "dve", "rows", "iota"))
    with ExitStack() as ctx:
        sb = lambda n, s, d=F32: core.sb(f"m3_{n}", s, d, ctx)
        ints = sb("ints", [P, ET, 2], I32)
        both = sb("both", [P, 2, ET], I32)
        f = sb("f", [P, ET, 2])
        idxf = sb("idxf", [P, ET])
        rowsI = sb("rowsI", [IT2, 2, 2 * GE], I32)
        rowsF = sb("rowsF", [IT2, 2, 2 * GE])
        low = sb("low", [IT2, 2, 2 * GE], I32)
        lowB = sb("lowB", [IT2, 2, 2 * GE], BF16)
        maskB = sb("maskB", [IT2, 2, 2 * GE], BF16)
        binI = sb("binI", [P, ET], I32)
        iotaI = sb("iotaI", [P, P], I32)
        block = ctx.enter_context(nc.Block())

        @block.gpsimd
        def _(pool):
            nc.gpsimd.iota(iotaI[:], pattern=[[1, P]], base=0, channel_multiplier=0).then_inc(s_iota, 1)
            nc.gpsimd.iota(a.iotaP_int[:], pattern=[[0, 1]], base=0, channel_multiplier=1).then_inc(s_iota, 1)

        @block.sync
        def _(sp):
            sp.dma_start(both[:, 1, :], ins["dst_pt"]).then_inc(s_in, 16)
            sp.dma_start(both[:, 0, :], ins["src_pt"]).then_inc(s_in, 16)
            sp.dma_start(rowsI[:, 0, :], ins["src_rows"].rearrange("(i h) e -> i (h e)", h=2)).then_inc(s_in, 16)
            sp.dma_start(rowsI[:, 1, :], ins["dst_rows"].rearrange("(i h) e -> i (h e)", h=2)).then_inc(s_in, 16)
            sp.wait_ge(s_rows, 1)
            for s in range(2):
                sp.dma_start(a.low_rows[s].rearrange("(i e) -> i e", i=IT2), lowB[:, s, :]).then_inc(s_out, 16)
                sp.dma_start(a.mask_rows[s].rearrange("(i e) -> i e", i=IT2), maskB[:, s, :]).then_inc(s_out, 16)
            sp.wait_ge(s_out, 64)

        @block.vector
        def _(dve):
            link = linker(dve, s_dve)
            tt, ts = nc.vector.tensor_tensor, nc.vector.tensor_scalar
            dve.wait_ge(s_iota, 2)
            link(nc.vector.tensor_copy(a.iota[:], iotaI[:]))
            link(nc.vector.tensor_copy(a.iotaP[:], a.iotaP_int[:]))
            dve.wait_ge(s_in, 64)
            for s in range(2):
                link(ts(ints[:, :, s], both[:, s, :], 7, None, ALU.logical_shift_right))
                link(nc.vector.tensor_copy(f[:, :, s], both[:, s, :]))
            link(nc.vector.tensor_copy(a.high[:], ints[:]))
            link(ts(binI[:], both[:, 0, :], 5, None, ALU.logical_shift_right))
            link(nc.vector.tensor_copy(a.bin[:], binI[:]))
            link(nc.vector.memset(a.meta[:], 0.0))
            link(nc.vector.tensor_copy(a.meta[:, :, 0], f[:, :, 0]))
            link(tt(a.meta[:, :, 1], f[:, :, 0], f[:, :, 1], ALU.is_lt))
            link(tt(a.meta[:, :, 2], f[:, :, 0], f[:, :, 1], ALU.is_gt))
            link(ts(idxf[:], a.meta[:, :, 2], float(NP), None, ALU.mult))
            link(tt(idxf[:], idxf[:], f[:, :, 1], ALU.add))
            link(nc.vector.tensor_copy(a.yidx[:], idxf[:]))
            link(nc.vector.tensor_copy(rowsF[:], rowsI[:]))
            link(ts(low[:], rowsI[:], 127, None, ALU.bitwise_and))
            link(nc.vector.tensor_copy(lowB[:], low[:]))
            link(tt(maskB[:, 0, :], rowsF[:, 0, :], rowsF[:, 1, :], ALU.is_lt))
            tt(maskB[:, 1, :], rowsF[:, 0, :], rowsF[:, 1, :], ALU.is_gt).then_inc(s_rows, 1)


def logits(core, t, ins, a):
    nc = core.nc
    S = {n: core.sem(f"g3_{n}") for n in ("spread", "hot_low", "picked", "hot_high", "prod", "logit")}
    row_in = [core.sem(f"g3_row_in{h}") for h in range(4)]
    s_ones = core.sem("g3_ones")
    with ExitStack() as ctx:
        sb = lambda n, s, d=F32: core.sb(f"g3_{n}", s, d, ctx)
        row = sb("row", [1, 4, 2, GE], BF16)
        ones = sb("ones", [1, P], BF16)
        hot = sb("hot", [P, 2, 2, GE])
        hh = sb("hh", [P, 2, TG, 2, NT])
        prod = sb("prod", [P, 2, TG, 2, NT])
        block = ctx.enter_context(nc.Block())
        spread = [[core.bank[2 * h + s] for s in range(2)] for h in range(2)]
        pick = [core.bank[4 + h] for h in range(2)]

        @block.sync
        def _(sp):
            def step(at):
                k = at(0)
                sp.wait_ge(S["spread"], k.back4)
                for s in range(2):
                    sp.dma_start(row[:, k.h4, s, :], a.low_rows[s:s + 1, k.span(GE)]).then_inc(row_in[k.h4], 16)

            run(sp, step)

        @block.tensor
        def _(pe):
            pe.sem_inc(S["spread"], CREDIT)
            pe.sem_inc(S["picked"], CREDIT)
            pe.wait_ge(s_ones, 1)

            def spread_rows(k):
                pe.wait_ge(row_in[k.h4], k.landed(2))
                pe.wait_ge(S["hot_low"], k.back2)
                for s in range(2):
                    last = nc.tensor.matmul(spread[k.h2][s][:, :], ones[:], row[:, k.h4, s, :], start=True,
                                            stop=True)
                last.then_inc(S["spread"], 1)

            def pick_parts(k):
                pe.wait_ge(S["hot_low"], k.done)
                pe.wait_ge(S["prod"], k.back2)
                for j in range(TG):
                    for s in range(2):
                        last = nc.tensor.matmul(pick[k.h2][:, (2 * j + s) * NT:(2 * j + s + 1) * NT],
                                                hot[:, k.h2, s, j * P:(j + 1) * P], a.parts[:, :, s],
                                                start=True, stop=True)
                last.then_inc(S["picked"], 1)

            def step(at):
                if at(2):
                    spread_rows(at(2))
                if at(0):
                    pick_parts(at(0))

            run(pe, step, ahead=2)

        @block.vector
        def _(dve):
            nc.vector.memset(ones[:], 1.0).then_inc(s_ones, 1)
            for n in ("hot_low", "hot_high", "prod", "logit"):
                dve.sem_inc(S[n], CREDIT)

            def low_hots(k):
                dve.wait_ge(S["spread"], k.done)
                dve.wait_ge(S["picked"], k.back2)
                for s in range(2):
                    last = nc.vector.tensor_scalar(hot[:, k.h2, s, :], spread[k.h2][s][:, :], a.iotaP[:, 0:1],
                                                   None, ALU.is_equal)
                last.then_inc(S["hot_low"], 1)

            def high_hots(k):
                dve.wait_ge(S["prod"], k.back2)
                nc.vector.tensor_tensor(
                    hh[:, k.h2], a.iota[:, 0:NT].unsqueeze(1).broadcast_to([P, 2 * TG, NT]).rearrange(
                        "p (j s) c -> p j s c", s=2),
                    a.high[:, k.span(TG), :].unsqueeze(3).broadcast_to([P, TG, 2, NT]),
                    ALU.is_equal).then_inc(S["hot_high"], 1)

            def step(at):
                if at(1):
                    low_hots(at(1))
                if at(0):
                    high_hots(at(0))
                if at(-1):
                    k = at(-1)
                    dve.wait_ge(S["hot_high"], k.done)
                    dve.wait_ge(S["picked"], k.done)
                    dve.wait_ge(S["logit"], k.back2)
                    nc.vector.tensor_tensor(prod[:, k.h2], pick[k.h2][:, 0:2 * TG * NT].rearrange(
                        "p (j s c) -> p j s c", j=TG, s=2), hh[:, k.h2], ALU.mult).then_inc(S["prod"], 1)
                    dve.wait_ge(S["prod"], k.done)
                    nc.vector.tensor_reduce(a.logit[:, k.span(TG)], prod[:, k.h2], AX.XY, ALU.add).then_inc(
                        S["logit"], 1)

            run(dve, step, ahead=1, behind=1)


def softmax(core, t, ins, a):
    nc = core.nc
    s_dve, s_exp, s_e, s_max, s_mr, s_sum, s_sr, s_b, s_turn, s_tc, s_out = (core.sem(f"s3_{n}") for n in (
        "dve", "shifted", "exp", "max", "max_all", "sum", "sum_all", "b", "turned", "turned_copied", "stored"))
    s_w = core.sem("s3_weights")
    chunks = [(c, min(P, ET - c)) for c in range(0, ET, P)]
    with ExitStack() as ctx:
        sb = lambda n, s, d=F32: core.sb(f"s3_{n}", s, d, ctx)
        b = sb("b", [P, 1])
        mx, mxa, sm, sma = (sb(n, [P, 2]) for n in ("mx", "mxa", "sm", "sma"))
        tmp = sb("tmp", [P, ET])
        part = sb("part", [P, 2, ET])
        ex = sb("ex", [P, ET])
        turned = sb("turned", [P, 2, len(chunks), P])
        md, mt = a.meta[:, :, 1], a.meta[:, :, 2]
        block = ctx.enter_context(nc.Block())

        @block.sync
        def _(sp):
            sp.dma_start(b[:], ins["L3_gnn_b_att"].rearrange("(a n) -> a n", a=1).broadcast_to([P, 1])).then_inc(
                s_b, 16)
            for s in range(2):
                for c, (at, n) in enumerate(chunks):
                    sp.wait_ge(s_tc, s * len(chunks) + c + 1)
                    sp.dma_start(a.attn_rows[s, at * P:(at + n) * P].rearrange("(r p) -> r p", p=P),
                                 turned[0:n, s, c, :]).then_inc(s_out, 16)
            sp.wait_ge(s_out, 32 * len(chunks))

        @block.gpsimd
        def _(pool):
            pool.wait_ge(s_max, 1)
            nc.gpsimd.partition_all_reduce(mxa[:], mx[:], P, bass.bass_isa.ReduceOp.max).then_inc(s_mr, 1)
            pool.wait_ge(s_sum, 1)
            nc.gpsimd.partition_all_reduce(sma[:], sm[:], P, bass.bass_isa.ReduceOp.add).then_inc(s_sr, 1)

        @block.scalar
        def _(act):
            act.wait_ge(s_exp, 1)
            nc.scalar.activation(ex[:], tmp[:], ACT.Exp).then_inc(s_e, 1)

        @block.tensor
        def _(pe):
            pe.wait_ge(s_w, 1)
            for s in range(2):
                for c, (at, n) in enumerate(chunks):
                    k = s * len(chunks) + c
                    if k >= 2:
                        pe.wait_ge(s_tc, k - 1)
                    nc.tensor.transpose(core.bank[k % 2][0:n, 0:P], part[:, s, at:at + n], t.ident[:]).then_inc(
                        s_turn, 1)

        @block.vector
        def _(dve):
            link = linker(dve, s_dve)
            tt, ts, stt = nc.vector.tensor_tensor, nc.vector.tensor_scalar, nc.vector.scalar_tensor_tensor
            dve.wait_ge(s_b, 16)
            link(ts(a.logit[:], a.logit[:], b[:, 0:1], None, ALU.add))
            link(stt(out=a.logit[:], in0=a.logit[:], scalar=0.01, in1=a.logit[:], op0=ALU.mult, op1=ALU.max))
            for s, m in enumerate((md, mt)):
                link(tt(part[:, s, :], a.logit[:], m, ALU.mult))
                link(ts(tmp[:], m, -1.0, 1e30, ALU.add, ALU.mult))
                link(tt(part[:, s, :], part[:, s, :], tmp[:], ALU.add))
                ins_ = nc.vector.tensor_reduce(mx[:, s:s + 1], part[:, s, :], AX.X, ALU.max)
                link(ins_) if s == 0 else ins_.then_inc(s_max, 1)
            dve.wait_ge(s_mr, 1)
            link(ts(tmp[:], md, mxa[:, 0:1], None, ALU.mult))
            link(ts(part[:, 0, :], mt, mxa[:, 1:2], None, ALU.mult))
            link(tt(tmp[:], tmp[:], part[:, 0, :], ALU.add))
            link(tt(tmp[:], a.logit[:], tmp[:], ALU.subtract))
            ts(tmp[:], tmp[:], 0.0, None, ALU.min).then_inc(s_exp, 1)
            dve.wait_ge(s_e, 1)
            link(tt(part[:, 0, :], ex[:], md, ALU.mult))
            link(tt(part[:, 1, :], ex[:], mt, ALU.mult))
            nc.vector.tensor_reduce(sm[:], part[:], AX.X, ALU.add).then_inc(s_sum, 1)
            dve.wait_ge(s_sr, 1)
            link(ts(sma[:], sma[:], 1e-30, None, ALU.max))
            link(nc.vector.reciprocal(sma[:], sma[:]))
            for s in range(2):
                link(ts(part[:, s, :], part[:, s, :], sma[:, s:s + 1], None, ALU.mult))
            tt(a.attn[:], part[:, 0, :], part[:, 1, :], ALU.add).then_inc(s_w, 1)
            for k in range(2 * len(chunks)):
                s, c = divmod(k, len(chunks))
                dve.wait_ge(s_turn, k + 1)
                n = chunks[c][1]
                nc.vector.tensor_copy(turned[0:n, s, c, :], core.bank[k % 2][0:n, 0:P]).then_inc(s_tc, 1)


def source_order(core, t, a):
    nc = core.nc
    W = TG * NBIN
    s_iota = core.sem("o3_iota")
    s_tri, s_dve, s_base, s_bl, s_span, s_red, s_bases = (core.sem(f"o3_{n}") for n in (
        "tri", "dve", "base_stored", "base_loaded", "span", "span_all", "bases"))
    S = {n: core.sem(f"o3_{n}") for n in ("hot1", "hot2", "counted", "first", "opened", "closed", "prod", "pos")}
    with ExitStack() as ctx:
        sb = lambda n, s, d=F32: core.sb(f"o3_{n}", s, d, ctx)
        hot = sb("hot", [P, 4, TG, NBIN], BF16)
        ones, below, rest, zero = (sb(n, [P, P], BF16) for n in ("ones", "below", "rest", "zero"))
        iotaB = sb("iotaB", [P, NBIN], BF16)
        onef = sb("onef", [1, P])
        total = sb("total", [P, NBIN])
        incl = sb("incl", [P, NBIN])
        excl = sb("excl", [P, NBIN])
        prod = sb("prod", [P, 2, TG, NBIN])
        posF = sb("posF", [P, ET])
        before = sb("before", [P, ET])
        same = sb("same", [P, NG])

        def one_hots(k, sem):
            return nc.vector.tensor_tensor(hot[:, k.h4, :, :], iotaB[:].unsqueeze(1).broadcast_to(
                [P, TG, NBIN]), a.bin[:, k.span(TG)].unsqueeze(2).broadcast_to([P, TG, NBIN]),
                ALU.is_equal).then_inc(sem, 1)

        with nc.Block() as block:
            @block.gpsimd
            def _(pool):
                nc.gpsimd.memset(ones[:], 1.0).then_inc(s_tri, 1)
                nc.gpsimd.memset(zero[:], 0.0).then_inc(s_tri, 1)
                nc.gpsimd.memset(onef[:], 1.0).then_inc(s_tri, 1)
                pool.wait_ge(s_tri, 3)
                nc.gpsimd.affine_select(out=below[:], in_=ones[:], compare_op=ALU.is_gt, fill=0.0, base=0,
                                        pattern=[[1, P]], channel_multiplier=-1).then_inc(s_tri, 1)
                nc.gpsimd.affine_select(out=rest[:], in_=ones[:], compare_op=ALU.is_ge, fill=0.0, base=0,
                                        pattern=[[-1, P]], channel_multiplier=1).then_inc(s_tri, 1)

            @block.tensor
            def _(pe):
                pe.wait_ge(s_tri, 5)
                pe.sem_inc(S["counted"], CREDIT)
                pe.wait_ge(S["hot1"], CREDIT + 1)
                nc.tensor.matmul(core.bank[0][:, 0:W], zero[:], hot[:, 0, :, :], start=True, stop=False,
                                 skip_group_check=True)

                def step(at):
                    k = at(0)
                    pe.wait_ge(S["hot1"], k.done)
                    nc.tensor.matmul(core.bank[0][:, 0:W], ones[:], hot[:, k.h4, :, :], start=False, stop=False,
                                     skip_group_check=True).then_inc(S["counted"], 1)

                run(pe, step)
                nc.tensor.matmul(core.bank[0][:, 0:W], zero[:], hot[:, 0, :, :], start=False, stop=True,
                                 skip_group_check=True).then_inc(S["first"], 1)

            @block.vector
            def _(dve):
                dve.sem_inc(S["hot1"], CREDIT)
                nc.vector.tensor_copy(iotaB[:], a.iota[:, 0:NBIN]).then_inc(s_iota, 1)
                dve.wait_ge(s_iota, 1)

                def step(at):
                    k = at(0)
                    dve.wait_ge(S["counted"], k.back4)
                    one_hots(k, S["hot1"])

                run(dve, step)
                link = linker(dve, s_dve)
                dve.wait_ge(S["first"], 1)
                link(nc.vector.tensor_reduce(total[:], core.bank[0][:, 0:W].rearrange("p (j b) -> p b j", j=TG),
                                             AX.X, ALU.add))
                link(nc.vector.memset(excl[:], 0.0))
                link(nc.vector.tensor_tensor_scan(incl[:], total[:], excl[:], 0.0, ALU.add, ALU.add))
                link(nc.vector.tensor_tensor(excl[:], incl[:], total[:], ALU.subtract))
                link(nc.vector.memset(hot[:, TG - 1, :, :], 0.0))
                bins = a.bin[:].rearrange("p (g j) -> p g j", j=TG)
                bef = before[:].rearrange("p (g j) -> p g j", j=TG)
                link(nc.vector.memset(before[:], 0.0))
                for j in range(1, TG):
                    for q in range(j):
                        link(nc.vector.tensor_tensor(same[:], bins[:, :, j], bins[:, :, q], ALU.is_equal))
                        link(nc.vector.tensor_tensor(bef[:, :, j], bef[:, :, j], same[:], ALU.add))

        with nc.Block() as block:
            bank = [core.bank[0], core.bank[1]]

            @block.tensor
            def _(pe):
                for b in bank:
                    nc.tensor.matmul(b[:, 0:NBIN], onef[:], excl[0:1, :], start=True, stop=False,
                                     skip_group_check=True)
                pe.sem_inc(S["closed"], CREDIT)
                pe.sem_inc(S["opened"], CREDIT)

                def add(dst, lhsT, slot):
                    for j in range(TG):
                        last = nc.tensor.matmul(dst[:, 0:NBIN], lhsT, hot[:, slot, j, :], start=False, stop=False,
                                                skip_group_check=True)
                    return last

                def step(at):
                    k = at(0)
                    pe.wait_ge(S["hot2"], k.done)
                    add(bank[k.h2], below[:], k.h4).then_inc(S["opened"], 1)
                    pe.wait_ge(S["prod"], k.prev)
                    add(bank[1 - k.h2], rest[:], (k.h4 + TG - 1) % TG)
                    add(bank[1 - k.h2], ones[:], k.h4).then_inc(S["closed"], 1)

                run(pe, step)

            @block.vector
            def _(dve):
                for n in ("hot2", "prod", "pos"):
                    dve.sem_inc(S[n], CREDIT)

                def multiply(k):
                    dve.wait_ge(S["opened"], k.done)
                    dve.wait_ge(S["pos"], k.back2)
                    nc.vector.tensor_tensor(prod[:, k.h2], bank[k.h2][:, 0:NBIN].unsqueeze(1).broadcast_to(
                        [P, TG, NBIN]), hot[:, k.h4, :, :], ALU.mult).then_inc(S["prod"], 1)

                def reduce(k):
                    dve.wait_ge(S["prod"], k.done)
                    nc.vector.tensor_reduce(posF[:, k.span(TG)], prod[:, k.h2], AX.X, ALU.add).then_inc(S["pos"], 1)

                def step(at):
                    if at(1):
                        dve.wait_ge(S["closed"], at(1).back2)
                        one_hots(at(1), S["hot2"])
                    if at(0):
                        multiply(at(0))
                    if at(-1):
                        reduce(at(-1))

                run(dve, step, ahead=1, behind=1)

        start = sb("start", [IT2, 2])
        startI = sb("startI", [IT2, 2], I32)
        cmp = sb("cmp", [IT2, 2, NBIN])
        lo, hi = sb("lo", [IT2, 2]), sb("hi", [IT2, 2])
        span, spanR, spanI = sb("span", [P, 1]), sb("spanR", [P, 1]), sb("spanI", [P, 1], I32)
        win = sb("win", [1, NG])
        block = ctx.enter_context(nc.Block())

        @block.gpsimd
        def _(pool):
            nc.gpsimd.iota(startI[:], pattern=[[GE, 2]], base=0, channel_multiplier=2 * GE).then_inc(s_tri, 1)
            pool.wait_ge(s_span, 1)
            nc.gpsimd.partition_all_reduce(spanR[:], span[:], P, bass.bass_isa.ReduceOp.max).then_inc(s_red, 1)

        @block.sync
        def _(sp):
            sp.wait_ge(s_bases, 1)
            sp.dma_start(a.base_dram.rearrange("(i h) -> i h", h=2), lo[:]).then_inc(s_base, 16)
            sp.wait_ge(s_base, 16)
            sp.dma_start(a.baseB[:], a.base_dram.rearrange("(a g) -> a g", a=1).broadcast_to([P, NG])).then_inc(
                s_bl, 16)
            sp.wait_ge(s_bl, 16)

        @block.vector
        def _(dve):
            s_d = core.sem("o3_windows_dve")
            link = linker(dve, s_d)
            nc.vector.tensor_tensor(a.pos[:], posF[:], before[:], ALU.add)
            dve.wait_ge(s_tri, 6)
            link(nc.vector.tensor_copy(start[:], startI[:]))
            inclB = incl[0:IT2, :].unsqueeze(1).broadcast_to([IT2, 2, NBIN])
            for dst, last in ((lo, False), (hi, True)):
                link(nc.vector.tensor_tensor(cmp[:], inclB, start[:].unsqueeze(2).broadcast_to([IT2, 2, NBIN]),
                                             ALU.is_le))
                link(nc.vector.tensor_reduce(dst[:], cmp[:], AX.X, ALU.add))
                if not last:
                    link(nc.vector.tensor_scalar(start[:], start[:], GE - 1.0, None, ALU.add))
            link(nc.vector.tensor_tensor(hi[:], hi[:], lo[:], ALU.subtract))
            nc.vector.tensor_scalar(lo[:], lo[:], 32.0, None, ALU.mult).then_inc(s_bases, 1)
            link(nc.vector.memset(span[:], 0.0))
            nc.vector.tensor_reduce(span[0:IT2, :], hi[:], AX.X, ALU.max).then_inc(s_span, 1)
            dve.wait_ge(s_red, 1)
            link(nc.vector.tensor_copy(spanI[:], spanR[:]))
            link(nc.vector.tensor_scalar(spanI[:], spanI[:], 1, None, ALU.logical_shift_right))
            link(nc.vector.tensor_scalar(a.passes[:], spanI[0:1, :], 1, None, ALU.add))
            dve.wait_ge(s_bl, 16)
            link(nc.vector.tensor_copy(a.win0[:], a.baseB[0:1, :]))


def messages(core, t, ins, a):
    nc = core.nc
    H, O = 256, 128
    names = ("scaled", "z_ready", "z_copied", "bn1", "parts1", "stats1", "std1", "recip1", "rstd1", "normed1",
             "turned", "hidden", "u_ready", "g_ready", "half", "comb", "bn2", "parts2", "stats2", "std2", "rstd2",
             "centered", "gained", "message")
    S = {n: core.sem(f"x3_{n}") for n in names}
    in_ = [core.sem(f"x3_loaded{h}") for h in range(4)]
    rows_in = [core.gpsimd_dma_sem(f"x3_gathered{h}") for h in range(4)]
    sent = [core.gpsimd_dma_sem(f"x3_sent{h}") for h in range(2)]
    s_w, s_raw, s_split, s_parts, s_idx, s_pidx, s_c = (core.sem(f"x3_{n}") for n in (
        "w", "raw", "split", "parts", "idx", "pidx", "const"))
    with ExitStack() as ctx:
        sb = lambda n, s, d=F32: core.sb(f"x3_{n}", s, d, ctx)
        w1b = sb("w1b", [P, H])
        w2 = sb("w2", [P, 2, 2, O])
        gb = sb("gb", [P, 2, 2, 2])
        raw = sb("raw", [2, 512])
        raw2 = sb("raw2", [1, 256])
        split, split2 = sb("split", [2, 3, 512], BF16), sb("split2", [1, 3, 256], BF16)
        vecs, vecs2 = sb("vecs", [6, 512], BF16), sb("vecs2", [3, 256], BF16)
        ones = sb("ones", [3, P], BF16)
        eps = sb("eps", [P, 1])
        idx, pidx = sb("idx", [P, 4, TG], I32), sb("pidx", [P, 2, TG], I32)
        ea, scaled = sb("ea", [P, 4, GE]), sb("scaled", [P, 4, GE])
        mask = sb("mask", [6, 4, GE], BF16)
        y = sb("y", [P, 4, TG, H])
        z = sb("z", [P, 2, TG, H])
        st1, mv1 = sb("st1", [P, 2, TG, 6]), sb("mv1", [P, 2, TG, 2])
        sd1, rs1, nb1 = (sb(n, [P, 2, TG]) for n in ("sd1", "rs1", "nb1"))
        st2, mv2 = sb("st2", [P, 2, TG, 6]), sb("mv2", [P, 2, TG, 2])
        sd2, rs2 = (sb(n, [P, 2, TG]) for n in ("sd2", "rs2"))
        dif, dif2 = sb("dif", [P, 2, TG]), sb("dif2", [P, 2, TG])
        hid = sb("hid", [P, 2, 2, GE])
        half = sb("half", [P, 2, TG, O])
        c2 = sb("c2", [P, 2, TG, O])
        row = sb("row", [P, 2, TG, ROW])
        loads = [(w1b[64 * s:64 * s + 64, :], ins[f"L3_gnn_{n}_w1"][128:192, :]) for s, n in enumerate(("d2t", "t2d"))]
        raws = []
        for s, n in enumerate(("d2t", "t2d")):
            get = lambda v: ins[f"L3_gnn_{n}_{v}"]
            loads.append((w2[:, s, :, :], get("w2").rearrange("(c p) o -> p c o", p=P)))
            loads.append((gb[:, s, :, 0], get("g1").rearrange("(c p) -> p c", p=P)))
            loads.append((gb[:, s, :, 1], get("be1").rearrange("(c p) -> p c", p=P)))
            line = lambda v: get(v).rearrange("(a n) -> a n", a=1)
            raws += [(raw[s:s + 1, 0:256], line("b1")), (raw[s:s + 1, 256:384], line("g2")),
                     (raw[s:s + 1, 384:512], line("be2")), (raw2[:, 128 * s:128 * s + 128], line("b2"))]
        with nc.Block() as block:
            @block.sync
            def _(sp):
                for dst, src in raws:
                    sp.dma_start(dst, src).then_inc(s_raw, 16)
                for dst, src in loads:
                    sp.dma_start(dst, src, allow_slow_non_contiguous=True).then_inc(s_w, 16)
                sp.wait_ge(s_split, 2)
                for q in range(3):
                    for s in range(2):
                        sp.dma_start(vecs[3 * s + q:3 * s + q + 1, :], split[s:s + 1, q, :]).then_inc(s_parts, 16)
                    sp.dma_start(vecs2[q:q + 1, :], split2[:, q, :]).then_inc(s_parts, 16)
                sp.wait_ge(s_parts, 9 * 16)
                sp.wait_ge(s_w, 16 * len(loads))

            @block.vector
            def _(dve):
                link = linker(dve, s_c)
                dve.wait_ge(s_raw, 16 * len(raws))
                link(nc.vector.memset(ones[:], 1.0))
                link(nc.vector.memset(eps[:], EPS))
                for r, sp_ in ((raw, split), (raw2, split2)):
                    for q in range(3):
                        ins_ = nc.vector.tensor_copy(sp_[:, q, :], r[:])
                        link(ins_)
                        if q < 2:
                            link(nc.vector.tensor_tensor(r[:], r[:], sp_[:, q, :], ALU.subtract))
                nc.vector.tensor_copy(eps[:], eps[:]).then_inc(s_split, 2)

        block = ctx.enter_context(nc.Block())
        z_ps = [core.bank[0], core.bank[1]]
        t_ps = [core.bank[2], core.bank[3]]
        u_ps = [core.bank[4], core.bank[5]]
        g_ps = [core.bank[6], core.bank[7]]


        @block.sync
        def _(sp):
            def step(at):
                k = at(0)
                sp.wait_ge(S["g_ready"], k.back4)
                cols = k.span(GE)
                for s in range(2):
                    sp.dma_start(ea[64 * s:64 * s + 64, k.h4, :], ins["attr64T"][:, cols]).then_inc(in_[k.h4], 16)
                    sp.dma_start(scaled[64 * s:64 * s + 64, k.h4, :], a.attn_rows[s:s + 1, cols].broadcast_to(
                        [64, GE])).then_inc(in_[k.h4], 16)
                    sp.dma_start(mask[3 * s:3 * s + 3, k.h4, :], a.mask_rows[s:s + 1, cols].broadcast_to(
                        [3, GE])).then_inc(in_[k.h4], 16)

            run(sp, step)

        @block.gpsimd
        def _(pool):
            def gather(k):
                pool.wait_ge(S["z_copied"], k.back4)
                nc.gpsimd.tensor_copy(idx[:, k.h4, :], a.yidx[:, k.span(TG)]).then_inc(s_idx, 1)
                pool.wait_ge(s_idx, 1)
                pool.sem_clear(s_idx)
                for j in range(TG):
                    nc.gpsimd.indirect_dma_start(y[:, k.h4, j, :], None, a.table, bass.IndirectOffsetOnAxis(
                        ap=idx[:, k.h4, j:j + 1], axis=0)).then_inc(rows_in[k.h4], 16)

            def scatter(k):
                pool.wait_ge(S["message"], k.done)
                nc.gpsimd.tensor_copy(pidx[:, k.h2, :], a.pos[:, k.span(TG)]).then_inc(s_pidx, 1)
                pool.wait_ge(s_pidx, 1)
                pool.sem_clear(s_pidx)
                for j in range(TG):
                    nc.gpsimd.indirect_dma_start(a.rows, bass.IndirectOffsetOnAxis(
                        ap=pidx[:, k.h2, j:j + 1], axis=0), row[:, k.h2, j, :], None).then_inc(sent[k.h2], 16)

            for h in range(2):
                for j in range(TG):
                    nc.gpsimd.dma_start(a.spare[h, j], a.pos[:, j:j + 1]).then_inc(sent[h], 16)

            def step(at):
                if at(2):
                    gather(at(2))
                if at(-3):
                    scatter(at(-3))

            run(pool, step, ahead=2, behind=3)
            for h in range(2):
                pool.wait_ge(sent[h], 64 + 64 * IT2)

        @block.tensor
        def _(pe):
            for n in ("z_ready", "turned", "u_ready", "g_ready"):
                pe.sem_inc(S[n], CREDIT)

            def turn(k):
                pe.wait_ge(S["normed1"], k.done)
                pe.wait_ge(S["hidden"], k.prev)
                for c in range(2):
                    for j in range(TG):
                        last = nc.tensor.transpose(t_ps[c][:, j * P:(j + 1) * P],
                                                   z[:, k.h2, j, c * P:(c + 1) * P], t.ident[:])
                last.then_inc(S["turned"], 1)

            def first_product(k):
                pe.wait_ge(S["scaled"], k.done)
                pe.wait_ge(in_[k.h4], k.landed(6))
                pe.wait_ge(S["z_copied"], k.prev)
                for j in range(TG):
                    o = z_ps[j // 2][:, H * (j % 2):H * (j % 2) + H]
                    e = slice(j * P, (j + 1) * P)
                    nc.tensor.matmul(o, scaled[:, k.h4, e], w1b[:], start=True, stop=False)
                    last = nc.tensor.matmul(o, mask[:, k.h4, e], vecs[:, 0:H], start=False, stop=True)
                last.then_inc(S["z_ready"], 1)

            def second_product(k):
                pe.wait_ge(S["hidden"], k.done)
                pe.wait_ge(S["comb"], k.prev)
                for j in range(TG):
                    e = slice(j * P, (j + 1) * P)
                    o = u_ps[j // 2][:, 2 * O * (j % 2):2 * O * (j % 2) + 2 * O]
                    for s in range(2):
                        for c in range(2):
                            nc.tensor.matmul(o[:, s * O:(s + 1) * O], hid[:, s, c, e], w2[:, s, c, :],
                                             start=(j % 2 == 0 and s == 0 and c == 0), stop=False,
                                             skip_group_check=True)
                    last = nc.tensor.matmul(o, ones[:], vecs2[:], start=False, stop=True, skip_group_check=True)
                last.then_inc(S["u_ready"], 1)

            def gains(k):
                pe.wait_ge(S["gained"], k.prev)
                for j in range(TG):
                    o = g_ps[j // 2][:, 2 * O * (j % 2):2 * O * (j % 2) + 2 * O]
                    last = nc.tensor.matmul(o, mask[:, k.h4, j * P:(j + 1) * P], vecs[:, H:2 * H], start=True,
                                            stop=True)
                last.then_inc(S["g_ready"], 1)

            def step(at):
                if at(-1):
                    turn(at(-1))
                if at(1):
                    first_product(at(1))
                if at(-1):
                    second_product(at(-1))
                    gains(at(-1))

            run(pe, step, ahead=1, behind=1)

        @block.scalar
        def _(act):
            for n in ("std1", "normed1", "hidden", "half", "std2", "message"):
                act.sem_inc(S[n], CREDIT)

            def message(k):
                act.wait_ge(S["gained"], k.done)
                act.wait_ge(sent[k.h2], k.landed2(4))
                nc.scalar.activation(row[:, k.h2, :, 0:O], c2[:, k.h2, :, :], ACT.Relu)
                nc.scalar.copy(row[:, k.h2, :, O:ROW], a.meta[:, k.span(TG), :]).then_inc(S["message"], 1)

            def hidden(k):
                act.wait_ge(S["turned"], k.done)
                act.wait_ge(S["u_ready"], k.prev)
                for s in range(2):
                    for c in range(2):
                        last = nc.scalar.activation(hid[:, s, c, :], t_ps[c][:, :], ACT.Relu,
                                                    scale=gb[:, s, c, 0:1], bias=gb[:, s, c, 1:2])
                last.then_inc(S["hidden"], 1)

            def deviation(k, n, sd, mv, stats, used, ready):
                act.wait_ge(S[stats], k.done)
                act.wait_ge(S[used], k.back2)
                nc.scalar.activation(sd[:, k.h2, :], mv[:, k.h2, :, 1], ACT.Sqrt, scale=1.0 / n,
                                     bias=eps[:, 0:1]).then_inc(S[ready], 1)

            def normalize(k):
                act.wait_ge(S["rstd1"], k.done)
                for j in range(TG):
                    last = nc.scalar.activation(z[:, k.h2, j, :], z[:, k.h2, j, :], ACT.Identity,
                                                scale=rs1[:, k.h2, j:j + 1], bias=nb1[:, k.h2, j:j + 1])
                last.then_inc(S["normed1"], 1)

            def take_half(k):
                act.wait_ge(S["u_ready"], k.done)
                act.wait_ge(S["gained"], k.back2)
                for j in range(TG):
                    o = u_ps[j // 2][:, 2 * O * (j % 2):2 * O * (j % 2) + O]
                    last = nc.scalar.activation(half[:, k.h2, j, :], o, ACT.Copy,
                                                scale=a.meta[:, k.span(TG, j, 1), 1])
                last.then_inc(S["half"], 1)

            def step(at):
                if at(-3):
                    message(at(-3))
                if at(-1):
                    hidden(at(-1))
                if at(0):
                    deviation(at(0), H, sd1, mv1, "stats1", "rstd1", "std1")
                if at(-2):
                    deviation(at(-2), O, sd2, mv2, "stats2", "rstd2", "std2")
                if at(0):
                    normalize(at(0))
                if at(-1):
                    take_half(at(-1))

            run(act, step, behind=3)

        @block.vector
        def _(dve):
            for n in ("scaled", "z_copied", "bn1", "stats1", "recip1", "rstd1", "comb", "bn2", "stats2", "rstd2",
                      "centered", "gained"):
                dve.sem_inc(S[n], CREDIT)
            tt, stt = nc.vector.tensor_tensor, nc.vector.scalar_tensor_tensor

            def scale(k):
                dve.wait_ge(in_[k.h4], k.landed(6))
                tt(scaled[:, k.h4, :], ea[:, k.h4, :], scaled[:, k.h4, :], ALU.mult).then_inc(S["scaled"], 1)

            def add_rows(k):
                dve.wait_ge(S["z_ready"], k.done)
                dve.wait_ge(rows_in[k.h4], k.landed(4))
                dve.wait_ge(S["turned"], k.back2)
                for j in range(TG):
                    last = stt(out=z[:, k.h2, j, :], in0=y[:, k.h4, j, :], scalar=a.attn[:, k.span(TG, j, 1)],
                               in1=z_ps[j // 2][:, H * (j % 2):H * (j % 2) + H], op0=ALU.mult, op1=ALU.add)
                last.then_inc(S["z_copied"], 1)

            def statistics(k, st, v, ready, bn):
                dve.wait_ge(S[ready], k.done)
                for j in range(TG):
                    last = nc.vector.bn_stats(st[:, k.h2, j, :], v[:, k.h2, j, :])
                last.then_inc(S[bn], 1)

            def moments(k, st, mv, n, bn, parts, stats):
                s = st[:, k.h2]
                dve.wait_ge(S[bn], k.done)
                tt(mv[:, k.h2, :, 0], s[:, :, 1], s[:, :, 4], ALU.add)
                tt(dif[:, k.h2, :], s[:, :, 1], s[:, :, 4], ALU.subtract)
                tt(mv[:, k.h2, :, 1], s[:, :, 2], s[:, :, 5], ALU.add).then_inc(S[parts], 1)
                dve.wait_ge(S[parts], 2 * k.n + 1)
                nc.vector.tensor_scalar(mv[:, k.h2, :, 0], mv[:, k.h2, :, 0], 0.5, None, ALU.mult)
                tt(dif2[:, k.h2, :], dif[:, k.h2, :], dif[:, k.h2, :], ALU.mult).then_inc(S[parts], 1)
                dve.wait_ge(S[parts], 2 * k.n + 2)
                stt(out=mv[:, k.h2, :, 1], in0=dif2[:, k.h2, :], scalar=n / 4, in1=mv[:, k.h2, :, 1],
                    op0=ALU.mult, op1=ALU.add).then_inc(S[stats], 1)

            def invert1(k):
                dve.wait_ge(S["std1"], k.done)
                nc.vector.reciprocal(rs1[:, k.h2, :], sd1[:, k.h2, :]).then_inc(S["recip1"], 1)
                dve.wait_ge(S["recip1"], k.done)
                stt(out=nb1[:, k.h2, :], in0=mv1[:, k.h2, :, 0], scalar=-1.0, in1=rs1[:, k.h2, :], op0=ALU.mult,
                    op1=ALU.mult).then_inc(S["rstd1"], 1)

            def combine(k):
                dve.wait_ge(S["half"], k.done)
                dve.wait_ge(S["message"], k.back2)
                for j in range(TG):
                    last = stt(out=c2[:, k.h2, j, :], in0=u_ps[j // 2][:, 2 * O * (j % 2) + O:2 * O * (j % 2 + 1)],
                               scalar=a.meta[:, k.span(TG, j, 1), 2], in1=half[:, k.h2, j, :], op0=ALU.mult,
                               op1=ALU.add)
                last.then_inc(S["comb"], 1)

            def normalize2(k):
                dve.wait_ge(S["g_ready"], k.done)
                for j in range(TG):
                    G = g_ps[j // 2][:, 2 * O * (j % 2):2 * O * (j % 2) + O]
                    last = stt(out=half[:, k.h2, j, :], in0=c2[:, k.h2, j, :], scalar=mv2[:, k.h2, j, 0:1], in1=G,
                               op0=ALU.subtract, op1=ALU.mult)
                last.then_inc(S["centered"], 1)
                dve.wait_ge(S["std2"], k.done)
                nc.vector.reciprocal(rs2[:, k.h2, :], sd2[:, k.h2, :]).then_inc(S["rstd2"], 1)
                dve.wait_ge(S["rstd2"], k.done)
                dve.wait_ge(S["centered"], k.done)
                for j in range(TG):
                    B = g_ps[j // 2][:, 2 * O * (j % 2) + O:2 * O * (j % 2 + 1)]
                    last = stt(out=c2[:, k.h2, j, :], in0=half[:, k.h2, j, :], scalar=rs2[:, k.h2, j:j + 1], in1=B,
                               op0=ALU.mult, op1=ALU.add)
                last.then_inc(S["gained"], 1)

            def step(at):
                if at(0):
                    add_rows(at(0))
                if at(-2):
                    combine(at(-2))
                if at(0):
                    statistics(at(0), st1, z, "z_copied", "bn1")
                    moments(at(0), st1, mv1, H, "bn1", "parts1", "stats1")
                if at(-2):
                    statistics(at(-2), st2, c2, "comb", "bn2")
                if at(0):
                    invert1(at(0))
                if at(-2):
                    moments(at(-2), st2, mv2, O, "bn2", "parts2", "stats2")
                if at(2):
                    scale(at(2))
                if at(-2):
                    normalize2(at(-2))

            run(dve, step, ahead=2, behind=2)


def flow_sums(core, t, ins, a):
    nc = core.nc
    H = 128
    S = {n: core.sem(f"a3_{n}") for n in ("rel", "eq", "hot", "sums", "added", "mixed", "mixed_copied", "turned",
                                          "own")}
    in_ = [core.sem(f"a3_loaded{h}") for h in range(4)]
    s_init, s_win, s_w = core.sem("a3_init"), core.sem("a3_windows"), core.sem("a3_weights")
    with ExitStack() as ctx:
        sb = lambda n, s, d=F32: core.sb(f"a3_{n}", s, d, ctx)
        acc = sb("acc", [P, 2, NP])
        flow = sb("flow", [P, NT, H])
        rowb = sb("rowb", [P, 3, H])
        nw = sb("nw", [P, 2, H])
        with ExitStack() as ectx:
            row = core.sb("a3_row", [P, 4, TG, ROW], F32, ectx)
            rel = core.sb("a3_rel", [P, 2, TG], F32, ectx)
            eq = core.sb("a3_eq", [P, 2, TG, AWIN], F32, ectx)
            hot = core.sb("a3_hot", [P, 2, TG, 2, AWIN], F32, ectx)
            iota = core.sb("a3_iota", [P, AWIN], F32, ectx)
            win = core.sb("a3_win", [1, NG], I32, ectx)
            block = ectx.enter_context(nc.Block())
            o = [core.bank[0], core.bank[1]]

            def passes(eng, step, ahead=0, behind=0):
                count = eng.value_load(a.passes[0:1, 0:1], min_val=1, max_val=NBIN)
                with eng.Fori(0, count) as p:
                    run(eng, step, ahead, behind, base=eng.snap(p * IT))

            @block.sync
            def _(sp):
                rows = a.rows.rearrange("(g p j) c -> g p (j c)", p=P, j=TG)

                def step(at):
                    k = at(0)
                    sp.wait_ge(S["sums"], k.back4)
                    sp.dma_start(row[:, k.h4, :, :].rearrange("p j c -> p (j c)"),
                                 rows[k.span(1)].rearrange("a p f -> (a p) f")).then_inc(in_[k.h4], 16)

                passes(sp, step)

            @block.tensor
            def _(pe):
                pe.sem_inc(S["sums"], CREDIT)

                def step(at):
                    k = at(0)
                    pe.wait_ge(S["hot"], k.done)
                    pe.wait_ge(in_[k.h4], k.landed(1))
                    pe.wait_ge(S["added"], k.back2)
                    for j in range(TG):
                        last = nc.tensor.matmul(o[k.h2][:, 0:2 * AWIN], row[:, k.h4, j, 0:H],
                                                hot[:, k.h2, j, :, :].rearrange("p s w -> p (s w)"),
                                                start=j == 0, stop=j == TG - 1)
                    last.then_inc(S["sums"], 1)

                passes(pe, step)

            @block.gpsimd
            def _(pool):
                nc.gpsimd.memset(acc[:, 1, :], 0.0).then_inc(s_init, 1)

            @block.vector
            def _(dve):
                nc.vector.memset(acc[:, 0, :], 0.0).then_inc(s_init, 1)
                nc.vector.tensor_copy(iota[:], a.iota[:, 0:AWIN]).then_inc(s_win, 1)
                nc.vector.tensor_copy(win[:], a.win0[:]).then_inc(s_win, 1)
                dve.wait_ge(s_win, 2)
                dve.wait_ge(s_init, 2)
                for n in ("rel", "eq", "hot", "added"):
                    dve.sem_inc(S[n], CREDIT)

                def relative(k):
                    dve.wait_ge(in_[k.h4], k.landed(1))
                    dve.wait_ge(S["eq"], k.back2)
                    nc.vector.tensor_scalar(rel[:, k.h2, :], row[:, k.h4, :, H], a.baseB[:, k.span(1)], None,
                                            ALU.subtract).then_inc(S["rel"], 1)

                def one_hots(k):
                    dve.wait_ge(S["rel"], k.done)
                    dve.wait_ge(S["hot"], k.back2)
                    nc.vector.tensor_tensor(eq[:, k.h2], iota[:].unsqueeze(1).broadcast_to([P, TG, AWIN]),
                                            rel[:, k.h2, :].unsqueeze(2).broadcast_to([P, TG, AWIN]),
                                            ALU.is_equal).then_inc(S["eq"], 1)
                    dve.wait_ge(S["eq"], k.done)
                    dve.wait_ge(S["sums"], k.back2)
                    nc.vector.tensor_tensor(
                        hot[:, k.h2], eq[:, k.h2].unsqueeze(2).broadcast_to([P, TG, 2, AWIN]),
                        row[:, k.h4, :, H + 1:H + 3].unsqueeze(3).broadcast_to([P, TG, 2, AWIN]),
                        ALU.mult).then_inc(S["hot"], 1)

                def add_sums(k):
                    at = dve.value_load(win[0:1, k.span(1)], min_val=0, max_val=NP - AWIN)
                    dve.wait_ge(S["sums"], k.done)
                    dve.wait_ge(S["added"], k.prev)
                    w = acc[:, :, ds(at, AWIN)]
                    nc.vector.tensor_tensor(w, w, o[k.h2][:, 0:2 * AWIN].rearrange("p (s w) -> p s w", s=2),
                                            ALU.add).then_inc(S["added"], 1)

                def step(at):
                    if at(2):
                        relative(at(2))
                    if at(1):
                        one_hots(at(1))
                    if at(-1):
                        add_sums(at(-1))

                count = dve.value_load(a.passes[0:1, 0:1], min_val=1, max_val=NBIN)
                with dve.Fori(0, count) as p:
                    run(dve, step, ahead=2, behind=1, base=dve.snap(p * IT))
                    nc.vector.tensor_scalar(iota[:], iota[:], float(AWIN), None, ALU.add).then_inc(s_win, 1)
                    nc.vector.tensor_scalar(win[:], win[:], AWIN, NP - AWIN, ALU.add, ALU.min).then_inc(s_win, 1)
                    dve.wait_ge(s_win, p * 2 + 4)

        oT = sb("oT", [P, NB * P])
        halfn = NB * P // 2
        m_ps = [core.bank[0], core.bank[1]]
        with nc.Block() as block:
            @block.sync
            def _(sp):
                sp.dma_start(nw[:, 1, :], ins["L3_gnn_node_w"][0:P, :]).then_inc(s_w, 16)
                sp.dma_start(nw[:, 0, :], ins["L3_gnn_node_w"][P:2 * P, :]).then_inc(s_w, 16)
                for q, n in enumerate(("node_b", "node_g", "node_be")):
                    sp.dma_start(rowb[:, q, :], ins[f"L3_gnn_{n}"].rearrange("(a n) -> a n", a=1).broadcast_to(
                        [P, H])).then_inc(s_w, 16)
                sp.wait_ge(s_w, 80)

            @block.tensor
            def _(pe):
                pe.wait_ge(s_w, 80)
                pe.sem_inc(S["turned"], 1)
                with pe.Fori(0, NI) as i:
                    pe.wait_ge(S["mixed_copied"], i + 1)
                    for q in range(2):
                        for s in range(2):
                            last = nc.tensor.matmul(m_ps[q][:, 0:halfn], nw[:, s, :],
                                                    acc[:, s, ds(i * NB * P + q * halfn, halfn)], start=s == 0,
                                                    stop=s == 1)
                    last.then_inc(S["mixed"], 1)
                    pe.wait_ge(S["mixed_copied"], i + 2)
                    pe.wait_ge(S["own"], i + 1)
                    for u in range(NB):
                        last = nc.tensor.transpose(core.bank[2 + u // 4][:, P * (u % 4):P * (u % 4) + P],
                                                   oT[:, u * P:(u + 1) * P], t.ident[:])
                    last.then_inc(S["turned"], 1)

            @block.scalar
            def _(act):
                act.sem_inc(S["mixed_copied"], 1)
                with act.Fori(0, NI) as i:
                    act.wait_ge(S["mixed"], i + 1)
                    act.wait_ge(S["turned"], i + 1)
                    for q in range(2):
                        last = nc.scalar.copy(oT[:, q * halfn:(q + 1) * halfn], m_ps[q][:, 0:halfn])
                    last.then_inc(S["mixed_copied"], 1)

            @block.vector
            def _(dve):
                dve.sem_inc(S["own"], 1)
                with dve.Fori(0, NI) as i:
                    dve.wait_ge(S["turned"], i + 2)
                    nc.vector.tensor_copy(flow[:, ds(i * NB, 4), :],
                                          core.bank[2][:, :].rearrange("p (u n) -> p u n", u=4))
                    nc.vector.tensor_copy(flow[:, ds(i * NB + 4, 1), :].rearrange("p a c -> p (a c)"),
                                          core.bank[3][:, 0:P]).then_inc(S["own"], 1)

        add_block(core, t, "node", flow, rowb)


def flow_attention(core, t, ins):
    nc = core.nc
    a = Bundle()
    a.table = nc.dram_tensor("flow_table_dram", [2 * NP, 256], F32).ap()
    a.rows = nc.dram_tensor("message_rows_dram", [EP, ROW], F32).ap()
    a.low_rows = nc.dram_tensor("low_rows_dram", [2, EP], BF16).ap()
    a.mask_rows = nc.dram_tensor("mask_rows_dram", [2, EP], BF16).ap()
    a.attn_rows = nc.dram_tensor("attn_rows_dram", [2, EP], F32).ap()
    a.spare = nc.dram_tensor("spare_dram", [2, TG, P, 1], I32).ap()
    a.base_dram = nc.dram_tensor("source_base_dram", [NG], F32).ap()
    with ExitStack() as ctx:
        sb = lambda n, s, d=F32: core.sb(f"a_{n}", s, d, ctx)
        a.parts = sb("parts", [P, NT, 2])
        a.iota = sb("iota", [P, P])
        a.iotaP, a.iotaP_int = sb("iotaP", [P, 1]), sb("iotaP_int", [P, 1], I32)
        a.meta = sb("meta", [P, ET, 4])
        a.attn = sb("attn", [P, ET])
        a.logit = a.attn
        a.yidx, a.pos = sb("yidx", [P, ET], I32), sb("pos", [P, ET], I32)
        a.baseB, a.win0 = sb("baseB", [P, NG]), sb("win0", [1, NG], I32)
        a.passes = sb("passes", [1, 1], I32)
        attention_nodes(core, t, ins, a)
        with ExitStack() as ectx:
            a.high = core.sb("a_high", [P, ET, 2], F32, ectx)
            a.bin = core.sb("a_bin", [P, ET], BF16, ectx)
            edge_masks(core, t, ins, a)
            logits(core, t, ins, a)
            softmax(core, t, ins, a)
            source_order(core, t, a)
        messages(core, t, ins, a)
        flow_sums(core, t, ins, a)


def store(core, t, out):
    nc = core.nc
    s_out = core.sem("result_stored")
    whole = N // P
    with nc.Block() as block:
        @block.sync
        def _(sp):
            sp.dma_start(out[0:whole * P, :].rearrange("(t p) d -> p t d", p=P), t.x[:, 0:whole, :]).then_inc(
                s_out, 16)
            sp.dma_start(out[whole * P:N, :], t.x[0:N - whole * P, whole, :]).then_inc(s_out, 16)
            sp.wait_ge(s_out, 32)


def program(nc, ins, out, layers=4):
    with ExitStack() as ctx:
        core = Core(nc, ctx)
        t = Bundle()
        t.table = nc.dram_tensor("table_dram", [NP, D], F32).ap()
        with core.semaphores():
            prepare(core, t, ins)
        for layer in range(min(layers, 3)):
            if layer == 1:
                zeroed, loads, scales = weights_later(core, t.w, ins)
            with ExitStack() as lctx, core.semaphores():
                acc = Bundle()
                sb = lambda n, s: core.sb(f"l{layer}_{n}", s, F32, lctx)
                if layer == 1:
                    hR = sb("h", [P, NT, D])
                    table_plain(core, t, "t1", hR, zeroed)
                    acc.S, acc.V = sb("acc_s", [64, 4, NP]), sb("acc_v", [96, 4, NP])
                    acc.halves = [[acc.S[:]], [acc.V[:]]]
                    edge_sums(core, t, "e1", acc, extra=loads)
                    scale_weights(core, "w", zeroed, scales)
                    finish_product(core, t, "f1", acc, t.w.post1, hR)
                    continue
                pre, post, fc, attrT, n_sc = ((t.w.pre0, t.w.post0, t.w.fc0, ins["attr64T"], 96) if layer == 0 else
                                              (t.w.pre2, t.w.post2, t.w.fc2, ins["attr8T"], 64))
                t.sc = sb("sc", [P, NT, n_sc + 96])
                node_tables(core, t, f"t{layer}", pre, n_sc)
                acc.A, acc.B, acc.C = sb("acc_a", [P, 3, NP]), sb("acc_b", [96, NP]), sb("acc_c", [96, NP])
                acc.halves = [[acc.A[:]], [acc.B[:], acc.C[:]]]
                if layer == 0:
                    acc.X = sb("acc_x", [96, 3, NP])
                    acc.halves[1].append(acc.X[:])
                mlp = Bundle()
                mlp.w, mlp.attrT = fc, attrT
                mlp.rin, mlp.kinds, mlp.width = (64, 3, 224) if layer == 0 else (8, 2, 192)
                mlp.scale = 1 / math.sqrt(mlp.rin)
                edge_sums(core, t, f"e{layer}", acc, mlp)
                finish_gated(core, t, f"f{layer}", acc, post, layer == 2)
        with core.semaphores(again=False):
            if layers > 3:
                flow_attention(core, t, ins)
            store(core, t, out)


LAYERS = 4


def kernel(**inputs):
    import concourse.bacc as _bacc
    from concourse import mybir as _mybir
    from concourse.bass_utils import run_bass_kernel_spmd as _run

    nc = _bacc.Bacc("TRN2", target_bir_lowering=False, num_devices=1)
    arrays = {k: np.asarray(v) for k, v in inputs.items() if k.startswith("L")}
    pad = ((0, EP - E), (0, 0))
    x = np.asarray(inputs["x"])
    src = np.pad(np.asarray(inputs["src"]), (0, EP - E), constant_values=N - 1)
    dst = np.pad(np.asarray(inputs["dst"]), (0, EP - E), constant_values=N - 1)
    arrays["x_pad"] = np.pad(x, ((0, NP - N), (0, 0)))
    arrays["attr_pt"] = np.pad(np.asarray(inputs["node_vec1"])[:, 0], (0, NP - N)).reshape(NT, P).T
    arrays["src_pt"], arrays["dst_pt"] = src.reshape(ET, P).T, dst.reshape(ET, P).T
    arrays["src_rows"], arrays["dst_rows"] = src.reshape(NG, GE), dst.reshape(NG, GE)
    arrays["e4_pt"] = np.pad(np.asarray(inputs["edge_attr_4"]), pad).reshape(ET, P, 4).transpose(1, 0, 2).reshape(
        P, ET * 4)
    arrays["attr64T"] = np.pad(np.asarray(inputs["edge_attr_64"]), pad).T
    arrays["attr8T"] = np.pad(np.asarray(inputs["edge_attr_8"]), pad).T
    arrays = {k: np.ascontiguousarray(v) for k, v in arrays.items()}
    ins = {k: nc.dram_tensor(f"in_{k}", v.shape, _mybir.dt.from_np(v.dtype), kind="ExternalInput").ap()
           for k, v in arrays.items()}
    out = nc.dram_tensor("result", (N, D), F32, kind="ExternalOutput").ap()
    program(nc, ins, out, LAYERS)
    r = _run(nc, [{f"in_{k}": v for k, v in arrays.items()}], core_ids=[0])
    return r.results[0]["result"]
```

```python
import math
from contextlib import ExitStack, contextmanager

import numpy as np
import concourse.bass as bass
from concourse import mybir

F32 = mybir.dt.float32
BF16 = mybir.dt.bfloat16
I32 = mybir.dt.int32
ALU = mybir.AluOpType
ACT = mybir.ActivationFunctionType
AX = mybir.AxisListType
ds = bass.ds

P = 128
N, D = 3125, 160
E = 103125
NT = 25
NP = NT * P
GE = 512
TG = GE // P
UN = 4
NG = 204
IT = NG // UN
IT2 = NG // 2
EP = NG * GE
ET = EP // P
WIN = 32
NB = 5
NI = NT // NB
EPS = 1e-5
ROW = 132
NBIN = 98
AWIN = 64
INV2, INV3, INV6 = 1 / math.sqrt(2), 1 / math.sqrt(3), 1 / math.sqrt(6)
CROSS = {(0, 1, 2): 1.0, (1, 2, 0): 1.0, (2, 0, 1): 1.0, (0, 2, 1): -1.0, (1, 0, 2): -1.0, (2, 1, 0): -1.0}


class Bundle:
    pass


class Core:

    def __init__(self, nc, ctx):
        self.nc, self.ctx = nc, ctx
        self.bank = [ctx.enter_context(nc.psum_tensor(f"bank{i}", [P, 512], F32)) for i in range(8)]

    def sb(self, name, shape, dt=F32, ctx=None):
        return (ctx or self.ctx).enter_context(self.nc.sbuf_tensor(name, shape, dt))

    def sem(self, name):
        s = self.sem_ctx.enter_context(self.nc.semaphore(name))
        self.sems.append(s)
        return s

    def gpsimd_dma_sem(self, name):
        return self.ctx.enter_context(self.nc.semaphore(name))

    @contextmanager
    def semaphores(self, again=True):
        with ExitStack() as self.sem_ctx:
            self.sems = []
            yield
            if again:
                with self.nc.Block() as block:
                    @block.gpsimd
                    def _(pool):
                        for s in self.sems:
                            pool.sem_clear(s)


def linker(eng, sem):
    count = [0]

    def link(ins):
        count[0] += 1
        ins.then_inc(sem, 1)
        eng.wait_ge(sem, count[0])

    return link


CREDIT = 4


class Group:

    def __init__(self, eng, i, c, base=0):
        static = isinstance(i, int) and isinstance(base, int)
        hold = (lambda v: v) if static else eng.snap
        self.at = i * UN + c
        self.n = hold((base + i) * UN + c)
        self.h2, self.h4 = c % 2, c % 4
        self.turn = base + i + c // UN
        self.turn2 = (base + i) * 2 + c // 2
        self.done, self.prev, self.back2, self.back4 = (self.n + k for k in (CREDIT + 1, CREDIT, CREDIT - 1, CREDIT - 3))
        self.fixed = isinstance(i, int)

    def landed(self, k):
        return self.turn * (16 * k) + 16 * k

    def landed2(self, k):
        return self.turn2 * (16 * k) + 16 * k

    def span(self, size, offset=0, width=None):
        width = width or size
        if self.fixed:
            return slice(self.at * size + offset, self.at * size + offset + width)
        return ds(self.at * size + offset, width)


def run(eng, step, ahead=0, behind=0, base=0):
    def of(i, k, whole):
        groups = {}

        def at(d):
            if d not in groups:
                groups[d] = Group(eng, i, k + d, base) if whole or 0 <= k + d < NG else None
            return groups[d]

        return at

    count = (NG - ahead - behind) // UN
    for k in range(-ahead, behind):
        step(of(0, k, False))
    with eng.Fori(0, count) as i:
        for u in range(UN):
            step(of(i, behind + u, True))
    for k in range(behind + UN * count, NG + behind):
        step(of(0, k, False))


def weight_lists():
    loads, scales = [], []

    def put(tile, slot, r, c, src, scale=1.0):
        rows, cols = src.shape
        dst = tile[r:r + rows, slot, c:c + cols]
        loads.append((dst, src))
        if scale != 1.0:
            scales.append((dst, scale))

    return put, loads, scales


def weights_first(core, w, ins):
    put, loads, scales = weight_lists()
    w.post0 = core.sb("w_post0", [P, 9, 96])
    w.pre0 = core.sb("w_pre0", [P, 2, 192])
    w.fc0 = core.sb("w_fc0", [64, 1, 64 + 224])
    put_pre(put, w.pre0, ins["L0_gnn_lin1_ws"], ins["L0_gnn_sc_ws"], ins["L0_gnn_lin1_wv"], ins["L0_gnn_sc_wv"])
    put(w.fc0, 0, 0, 0, ins["L0_gnn_fc_w1"])
    put(w.fc0, 0, 0, 64, ins["L0_gnn_fc_w2"])
    ls, lv = ins["L0_gnn_lin2_ws"], ins["L0_gnn_lin2_wv"]
    cs, cv = 1 / 32 / math.sqrt(96), 1 / 32 / math.sqrt(128)
    put(w.post0, 0, 0, 0, ls[0:64, :], cs)
    for d in range(3):
        put(w.post0, 1, 32 * d, 0, ls[64:96, :], cs * INV3)
        put(w.post0, 2 + d, 64, 32 * d, lv[0:64, :], cv)
        put(w.post0, 5, 32 * d, 32 * d, lv[64:96, :], cv)
    for (d, j, k), sign in CROSS.items():
        put(w.post0, 6 + k, 32 * j, 32 * d, lv[96:128, :], cv * INV2 * sign)

    return [w.post0, w.pre0], loads, scales


def put_pre(put, pre, lin_s, sc_s, lin_v, sc_v):
    put(pre, 0, 0, 0, lin_s, 1 / 8)
    put(pre, 0, 0, 64, sc_s, 1 / 8)
    for d in range(3):
        put(pre, 1, 32 * d, 32 * d, lin_v, 1 / math.sqrt(32))
        put(pre, 1, 32 * d, 96 + 32 * d, sc_v, 1 / math.sqrt(32))


def weights_later(core, w, ins):
    put, loads, scales = weight_lists()
    w.post1 = core.sb("w_post1", [P, 13, 96])
    w.post2 = core.sb("w_post2", [P, 6, 96])
    w.pre2 = core.sb("w_pre2", [P, 2, 192])
    w.fc2 = core.sb("w_fc2", [64, 1, 64 + 192])
    put_pre(put, w.pre2, ins["L2_gnn_W1_s"], ins["L2_gnn_W_sc_s"], ins["L2_gnn_W1_v"], ins["L2_gnn_W_sc_v"])
    put(w.fc2, 0, 0, 0, ins["L2_gnn_fcW1"])
    put(w.fc2, 0, 0, 64, ins["L2_gnn_fcW2"])

    c0, c1 = 1 / math.sqrt(96), math.sqrt(3 / 128)
    put(w.post1, 0, 0, 0, ins["L1_gnn_W1"], c0)
    for d in range(3):
        put(w.post1, 1 + d, 0, 32 * d, ins["L1_gnn_W3"], c1 * INV3)
        put(w.post1, 4, 32 * d, 32 * d, ins["L1_gnn_W4"], c1 * INV3)
        put(w.post1, 5 + d, 32 * d, 0, ins["L1_gnn_W2"], c0 * INV3)
        put(w.post1, 12, 32 * d, 32 * d, ins["L1_gnn_Wv"], 1 / math.sqrt(32))
    for (d, j, k), sign in CROSS.items():
        put(w.post1, 8 + k, 32 * j, 32 * d, ins["L1_gnn_W5"], c1 * INV6 * sign)
    put(w.post1, 11, 0, 0, ins["L1_gnn_Ws"], 1 / 8)

    ls, lv, la = ins["L2_gnn_W2_s"], ins["L2_gnn_W2_v"], ins["L2_gnn_W3"]
    cs = 1 / 8 / math.sqrt(10) / math.sqrt(96)
    put(w.post2, 0, 0, 0, ls[0:64, :], cs)
    put(w.post2, 0, 0, 64, la[0:64, :], cs * 0.1)
    for d in range(3):
        put(w.post2, 1, 32 * d, 0, ls[64:96, :], cs * INV3)
        put(w.post2, 1, 32 * d, 64, la[64:96, :], cs * INV3 * 0.1)
        put(w.post2, 2 + d, 64, 32 * d, lv[0:64, :], cs)
        put(w.post2, 5, 32 * d, 32 * d, lv[64:96, :], cs)
    return [w.post1, w.post2, w.pre2], loads, scales


def prepare(core, t, ins):
    nc = core.nc
    t.x = core.sb("x_res", [P, NT, D])
    t.attr = core.sb("node_attr", [P, NT])
    t.e4 = core.sb("edge_vec", [P, ET, 4])
    t.srcI = core.sb("src_idx", [P, ET], I32)
    t.dstrel = core.sb("dst_in_window", [P, ET])
    t.ident = core.sb("ident", [P, P])
    t.iotaW = core.sb("iota_window", [P, WIN])
    t.win0 = core.sb("window_base", [1, NG], I32)
    t.passes = core.sb("passes", [1, 1], I32)
    t.w = Bundle()
    zero_tiles, loads, scales = weights_first(core, t.w, ins)
    t.base_dram = nc.dram_tensor("base_dram", [NG], F32).ap()
    s_zero, s_w, s_in, s_base, s_baseload = (core.sem(n) for n in (
        "w_zeroed", "w_loaded", "prep_loaded", "bases_stored", "bases_loaded"))
    s_iota, s_ident, s_red, s_span, s_bases, s_dve = (core.sem(n) for n in (
        "iota_made", "ident_made", "span_reduced", "span_ready", "bases_ready", "prep_dve"))
    with ExitStack() as ctx:
        sb = lambda n, s, d=F32: core.sb(n, s, d, ctx)
        dstI = sb("dst_idx", [P, ET], I32)
        rows = sb("dst_rows", [IT2, 2, GE], I32)
        rowsF = sb("dst_rows_f", [IT2, 2, GE])
        lo = sb("row_min", [IT2, 2])
        hi = sb("row_max", [IT2, 2])
        span = sb("span", [P, 1])
        spanR = sb("span_all", [P, 1])
        spanI = sb("span_int", [P, 1], I32)
        iotaI = sb("iota_int", [P, WIN], I32)
        baseB = sb("base_all", [P, NG])
        block = ctx.enter_context(nc.Block())

        @block.sync
        def _(sp):
            sp.dma_start(rows[:], ins["dst_rows"].rearrange("(i h) e -> i h e", h=2)).then_inc(s_in, 16)
            sp.dma_start(dstI[:], ins["dst_pt"]).then_inc(s_in, 16)
            sp.dma_start(t.srcI[:], ins["src_pt"]).then_inc(s_in, 16)
            sp.dma_start(t.attr[:], ins["attr_pt"]).then_inc(s_in, 16)
            sp.dma_start(t.x[:], ins["x_pad"].rearrange("(t p) d -> p t d", p=P)).then_inc(s_in, 16)
            sp.dma_start(t.e4[:], ins["e4_pt"].rearrange("p (t k) -> p t k", k=4)).then_inc(s_in, 16)
            sp.wait_ge(s_zero, len(zero_tiles))
            for dst, src in loads:
                sp.dma_start(dst, src).then_inc(s_w, 16)
            sp.wait_ge(s_bases, 1)
            sp.dma_start(t.base_dram.rearrange("(i h) -> i h", h=2), lo[:]).then_inc(s_base, 16)
            sp.wait_ge(s_base, 16)
            sp.dma_start(baseB[:], t.base_dram.rearrange("(a g) -> a g", a=1).broadcast_to([P, NG])).then_inc(
                s_baseload, 16)
            sp.wait_ge(s_baseload, 16)

        @block.gpsimd
        def _(pool):
            nc.gpsimd.iota(iotaI[:], pattern=[[1, WIN]], base=0, channel_multiplier=0).then_inc(s_iota, 1)
            nc.gpsimd.memset(t.ident[:], 0.0).then_inc(s_ident, 1)
            pool.wait_ge(s_ident, 1)
            nc.gpsimd.affine_select(out=t.ident[:], in_=t.ident[:], compare_op=ALU.not_equal, fill=1.0, base=0,
                                    pattern=[[-1, P]], channel_multiplier=1).then_inc(s_ident, 1)
            pool.wait_ge(s_span, 1)
            nc.gpsimd.partition_all_reduce(spanR[:], span[:], P, bass.bass_isa.ReduceOp.max).then_inc(s_red, 1)

        @block.vector
        def _(dve):
            link = linker(dve, s_dve)
            for z in zero_tiles:
                nc.vector.memset(z[:], 0.0).then_inc(s_zero, 1)
            link(nc.vector.memset(span[:], 0.0))
            dve.wait_ge(s_iota, 1)
            nc.vector.tensor_copy(t.iotaW[:], iotaI[:])
            dve.wait_ge(s_in, 96)
            link(nc.vector.tensor_copy(rowsF[:], rows[:]))
            nc.vector.tensor_reduce(lo[:], rowsF[:], AX.X, ALU.min).then_inc(s_bases, 1)
            link(nc.vector.tensor_reduce(hi[:], rowsF[:], AX.X, ALU.max))
            dve.wait_ge(s_bases, 1)
            link(nc.vector.tensor_tensor(hi[:], hi[:], lo[:], ALU.subtract))
            nc.vector.tensor_reduce(span[0:IT2, :], hi[:], AX.X, ALU.max).then_inc(s_span, 1)
            dve.wait_ge(s_red, 1)
            link(nc.vector.tensor_copy(spanI[:], spanR[:]))
            link(nc.vector.tensor_scalar(spanI[:], spanI[:], int(math.log2(WIN)), None, ALU.logical_shift_right))
            link(nc.vector.tensor_scalar(t.passes[:], spanI[0:1, :], 1, None, ALU.add))
            link(nc.vector.tensor_copy(t.dstrel[:], dstI[:]))
            dve.wait_ge(s_baseload, 16)
            nc.vector.tensor_copy(t.win0[:], baseB[0:1, :])
            rel = t.dstrel[:].rearrange("p (g j) -> p g j", j=TG)
            link(nc.vector.tensor_tensor(rel, rel, baseB[:].unsqueeze(2).broadcast_to([P, NG, TG]), ALU.subtract))
            dve.wait_ge(s_w, 16 * len(loads))
            for dst, scale in scales:
                nc.vector.tensor_scalar(dst, dst, scale, None, ALU.mult)


def center(core, t, name, xm, rstd):
    nc = core.nc
    s_dve, s_var, s_std = (core.sem(f"{name}_{n}") for n in ("stat_dve", "var_ready", "std_ready"))
    with ExitStack() as ctx:
        sq = core.sb(f"{name}_sq", [P, NT, D], F32, ctx)
        m = core.sb(f"{name}_mean", [P, NT], F32, ctx)
        v = core.sb(f"{name}_var", [P, NT], F32, ctx)
        std = core.sb(f"{name}_std", [P, NT], F32, ctx)
        block = ctx.enter_context(nc.Block())

        @block.vector
        def _(dve):
            link = linker(dve, s_dve)
            link(nc.vector.tensor_reduce(m[:], t.x[:], AX.X, ALU.add))
            link(nc.vector.tensor_scalar(m[:], m[:], 1.0 / D, None, ALU.mult))
            link(nc.vector.tensor_tensor(xm[:], t.x[:], m[:].unsqueeze(2).broadcast_to([P, NT, D]), ALU.subtract))
            link(nc.vector.tensor_tensor(sq[:], xm[:], xm[:], ALU.mult))
            link(nc.vector.tensor_reduce(v[:], sq[:], AX.X, ALU.add))
            nc.vector.tensor_scalar(v[:], v[:], 1.0 / D, EPS, ALU.mult, ALU.add).then_inc(s_var, 1)
            dve.wait_ge(s_std, 1)
            link(nc.vector.reciprocal(rstd[:], std[:]))

        @block.scalar
        def _(act):
            act.wait_ge(s_var, 1)
            nc.scalar.activation(std[:], v[:], ACT.Sqrt).then_inc(s_std, 1)



def node_tables(core, t, name, weights, n_sc):
    nc = core.nc
    S = {n: core.sem(f"{name}_{n}") for n in ("h_ready", "turned", "turned_copied", "lin", "lin_copied", "stored")}
    width = 64 + n_sc
    with ExitStack() as ctx:
        xm = core.sb(f"{name}_xm", [P, NT, D], F32, ctx)
        rstd = core.sb(f"{name}_rstd", [P, NT], F32, ctx)
        center(core, t, name, xm, rstd)
        h = core.sb(f"{name}_h", [P, NB, D], F32, ctx)
        hT = core.sb(f"{name}_hT", [96, NB, 2, P], F32, ctx)
        tab = core.sb(f"{name}_tab", [P, NB, D], F32, ctx)
        block = ctx.enter_context(nc.Block())
        turned = [core.bank[u // 2][:, 256 * (u % 2):256 * (u % 2) + 256] for u in range(NB)]
        lin = [core.bank[3 + u] for u in range(NB)]

        @block.scalar
        def _(act):
            with act.Fori(0, NI) as i:
                act.wait_ge(S["turned"], i + 1)
                for u in range(NB):
                    tile = i * NB + u
                    nc.scalar.activation(h[:, u, 0:64], xm[:, ds(tile, 1), 0:64], ACT.Relu, scale=rstd[:, ds(tile, 1)])
                    last = nc.scalar.activation(
                        h[:, u, 64:D].rearrange("p (i c) -> p c i", i=3),
                        xm[:, ds(tile, 1), 64:D].rearrange("p a (c i) -> p (a c) i", i=3), ACT.Relu,
                        scale=rstd[:, ds(tile, 1)])
                last.then_inc(S["h_ready"], 1)

        @block.tensor
        def _(pe):
            pe.sem_inc(S["turned"], 1)
            pe.sem_inc(S["lin"], 1)
            with pe.Fori(0, NI) as i:
                pe.wait_ge(S["h_ready"], i + 1)
                pe.wait_ge(S["turned_copied"], i + 1)
                for u in range(NB):
                    nc.tensor.transpose(turned[u][0:96, P:2 * P], h[:, u, 64:D], t.ident[:])
                    last = nc.tensor.transpose(turned[u][0:64, 0:P], h[:, u, 0:64], t.ident[:])
                last.then_inc(S["turned"], 1)
                pe.wait_ge(S["turned_copied"], i + 2)
                pe.wait_ge(S["lin_copied"], i + 1)
                for u in range(NB):
                    nc.tensor.matmul(lin[u][:, 0:width], hT[0:64, u, 0, :], weights[0:64, 0, 0:width], start=True,
                                     stop=False, skip_group_check=True)
                    last = nc.tensor.matmul(lin[u][:, width:width + 192], hT[0:96, u, 1, :], weights[0:96, 1, 0:192],
                                            start=False, stop=True, skip_group_check=True)
                last.then_inc(S["lin"], 1)

        @block.vector
        def _(dve):
            dve.sem_inc(S["turned_copied"], 1)
            dve.sem_inc(S["lin_copied"], 1)
            with dve.Fori(0, NI) as i:
                dve.wait_ge(S["turned"], i + 2)
                dve.wait_ge(S["lin"], i + 1)
                for u in range(NB):
                    nc.vector.tensor_copy(hT[0:64, u, 0, :], turned[u][0:64, 0:P])
                    last = nc.vector.tensor_copy(hT[0:96, u, 1, :], turned[u][0:96, P:2 * P])
                last.then_inc(S["turned_copied"], 1)
                dve.wait_ge(S["lin"], i + 2)
                dve.wait_ge(S["stored"], i * 16 + 16)
                for u in range(NB):
                    tile = i * NB + u
                    a = t.attr[:, ds(tile, 1)]
                    nc.vector.tensor_scalar(tab[:, u, 0:64], lin[u][:, 0:64], a, None, ALU.mult)
                    nc.vector.tensor_scalar(tab[:, u, 64:D], lin[u][:, width:width + 96], a, None, ALU.mult)
                    nc.vector.tensor_scalar(t.sc[:, ds(tile, 1), 0:n_sc].rearrange("p a c -> p (a c)"),
                                            lin[u][:, 64:width], a, None, ALU.mult)
                    last = nc.vector.tensor_scalar(t.sc[:, ds(tile, 1), n_sc:n_sc + 96].rearrange("p a c -> p (a c)"),
                                                   lin[u][:, width + 96:width + 192], a, None, ALU.mult)
                last.then_inc(S["lin_copied"], 1)

        @block.sync
        def _(sp):
            sp.sem_inc(S["stored"], 16)
            table = t.table.rearrange("(i u p) d -> i p u d", u=NB, p=P)
            with sp.Fori(0, NI) as i:
                sp.wait_ge(S["lin_copied"], i + 2)
                sp.dma_start(table[ds(i, 1)].rearrange("a p u d -> (a p) u d"), tab[:]).then_inc(S["stored"], 16)
            sp.wait_ge(S["stored"], NI * 16 + 16)


def table_plain(core, t, name, hR, zeroed):
    nc = core.nc
    s_h, s_out = core.sem(f"{name}_h_ready"), core.sem(f"{name}_stored")
    with ExitStack() as ctx:
        xm = core.sb(f"{name}_xm", [P, NT, D], F32, ctx)
        rstd = core.sb(f"{name}_rstd", [P, NT], F32, ctx)
        center(core, t, name, xm, rstd)
        block = ctx.enter_context(nc.Block())

        @block.scalar
        def _(act):
            with act.Fori(0, NI) as i:
                for u in range(NB):
                    tile = i * NB + u
                    nc.scalar.activation(hR[:, ds(tile, 1), 0:64], xm[:, ds(tile, 1), 0:64], ACT.Relu,
                                         scale=rstd[:, ds(tile, 1)])
                    last = nc.scalar.activation(
                        hR[:, ds(tile, 1), 64:D].rearrange("p a (i c) -> p (a c) i", i=3),
                        xm[:, ds(tile, 1), 64:D].rearrange("p a (c i) -> p (a c) i", i=3), ACT.Relu,
                        scale=rstd[:, ds(tile, 1)])
                last.then_inc(s_h, 1)

        @block.vector
        def _(dve):
            for z in zeroed:
                nc.vector.memset(z[:], 0.0)

        @block.sync
        def _(sp):
            sp.wait_ge(s_h, NI)
            sp.dma_start(t.table.rearrange("(t p) d -> p t d", p=P), hR[:]).then_inc(s_out, 16)
            sp.wait_ge(s_out, 16)


def edge_sums(core, t, name, acc, mlp=None, extra=(), order=None):
    nc = core.nc
    names = ["attr_used", "indices_ready", "turns", "hidden_ready", "weights_ready", "sums_ready", "eq_ready", "products_ready", "added"]
    S = {n: core.sem(f"{name}_{n}") for n in names}
    attr_in = [core.sem(f"{name}_attr_loaded{h}") for h in range(2)]
    rows_in = [core.gpsimd_dma_sem(f"{name}_rows_gathered{h}") for h in range(4)]
    s_zero, s_win = core.sem(f"{name}_zeroed"), core.sem(f"{name}_windows")
    s_extra = core.sem(f"{name}_extra")
    kinds = 0 if mlp is None else mlp.kinds
    sort = Sort(core, order) if order else None
    with ExitStack() as ctx:
        sb = lambda n, s, d=F32: core.sb(f"{name}_{n}", s, d, ctx)
        idx = sb("idx", [P, 4, TG], I32)
        rows = sb("rows", [P, 4, TG, D])
        eq = sb("eq", [P, 2, TG, WIN])
        hot = sb("hot", [P, 2, TG, 4, WIN])
        iota = sb("iota", [P, WIN])
        win = sb("win", [1, NG], I32)
        if mlp:
            attr = sb("attr", [mlp.rin, 2, GE])
            hid = sb("hid", [64, 2, GE])
            ps = sb("prod_s", [P, 2, TG, 128])
            pv = sb("prod_v", [P, 2, TG, kinds, 96])
        block = ctx.enter_context(nc.Block())
        hid_ps = [core.bank[0], core.bank[1]]
        w_ps = [[core.bank[2], core.bank[3]], [core.bank[4], core.bank[5]]]
        sum_ps = [core.bank[6], core.bank[7]]

        def passes(eng, step, ahead=0, behind=0, begin=None):
            count = eng.value_load(t.passes[0:1, 0:1], min_val=1, max_val=NBIN)
            with eng.Fori(0, count) as p:
                base = eng.snap(p * IT)
                if begin:
                    begin(eng, Group(eng, 0, 0, base))
                run(eng, step, ahead, behind, base=base)

        @block.sync
        def _(sp):
            for dst, src in extra:
                sp.dma_start(dst, src).then_inc(s_extra, 16)

            def step(at):
                k = at(0)
                sp.wait_ge(S["attr_used"], k.back2)
                sp.dma_start(attr[:, k.h2, :], mlp.attrT[:, k.span(GE)]).then_inc(attr_in[k.h2], 16)

            if mlp:
                passes(sp, step)
            if extra:
                sp.wait_ge(s_extra, 16 * len(extra))

        @block.gpsimd
        def _(pool):
            for a in acc.halves[1]:
                nc.gpsimd.memset(a, 0.0).then_inc(s_zero, 1)

            def step(at):
                k = at(0)
                pool.wait_ge(S["indices_ready"], k.done)
                pool.sem_inc(S["turns"], 1)
                for j in range(TG):
                    nc.gpsimd.indirect_dma_start(
                        rows[:, k.h4, j, :], None, t.table,
                        bass.IndirectOffsetOnAxis(ap=idx[:, k.h4, j:j + 1], axis=0)).then_inc(rows_in[k.h4], 16)

            passes(pool, step)

        @block.scalar
        def _(act):
            act.sem_inc(S["indices_ready"], CREDIT)
            act.sem_inc(S["hidden_ready"], CREDIT)

            def indices(k):
                act.wait_ge(S["products_ready"] if mlp else S["sums_ready"], k.back4)
                nc.scalar.copy(idx[:, k.h4, :], t.srcI[:, k.span(TG)]).then_inc(S["indices_ready"], 1)

            def hidden(k):
                act.wait_ge(S["attr_used"], k.done)
                act.wait_ge(S["weights_ready"], k.back2)
                nc.scalar.activation(hid[:, k.h2, :], hid_ps[k.h2][0:64, :], ACT.Silu,
                                     scale=mlp.scale).then_inc(S["hidden_ready"], 1)

            def step(at):
                if at(2):
                    indices(at(2))
                if mlp and at(0):
                    hidden(at(0))

            passes(act, step, ahead=2)

        @block.tensor
        def _(pe):
            pe.sem_inc(S["sums_ready"], CREDIT)
            if mlp:
                pe.sem_inc(S["attr_used"], CREDIT)
                pe.sem_inc(S["weights_ready"], CREDIT)

            def hidden(k):
                pe.wait_ge(attr_in[k.h2], k.landed2(1))
                pe.wait_ge(S["hidden_ready"], k.back2)
                nc.tensor.matmul(hid_ps[k.h2][0:96, :], mlp.w[0:mlp.rin, 0, 0:96], attr[:, k.h2, :], start=True,
                                 stop=True).then_inc(S["attr_used"], 1)

            def edge_weights(k):
                pe.wait_ge(S["hidden_ready"], k.done)
                pe.wait_ge(S["products_ready"], k.back2)
                for j in range(TG):
                    last = nc.tensor.matmul(
                        w_ps[k.h2][j // 2][:, mlp.width * (j % 2):mlp.width * (j % 2 + 1)],
                        hid[:, k.h2, j * P:(j + 1) * P], mlp.w[:, 0, 64:64 + mlp.width], start=True, stop=True)
                last.then_inc(S["weights_ready"], 1)

            def sums(k):
                o = sum_ps[k.h2]
                pe.wait_ge(S["products_ready"], k.done)
                if not mlp:
                    pe.wait_ge(rows_in[k.h4], k.landed(TG))
                pe.wait_ge(S["added"], k.back2)
                for j in range(TG):
                    first, end = j == 0, j == TG - 1
                    hots = hot[:, k.h2, j, :, :].rearrange("p k w -> p (k w)")
                    if mlp:
                        nc.tensor.matmul(o[:, 0:4 * WIN], ps[:, k.h2, j, :], hots, start=first, stop=end,
                                         skip_group_check=True)
                        nc.tensor.matmul(o[0:96, 4 * WIN:5 * WIN], pv[:, k.h2, j, 0, :], hots[:, 0:WIN],
                                         start=False, stop=end, skip_group_check=True)
                        for q in range(1, kinds):
                            last = nc.tensor.matmul(o[0:96, (2 + 3 * q) * WIN:(5 + 3 * q) * WIN],
                                                    pv[:, k.h2, j, q, :], hots[:, WIN:4 * WIN], start=False,
                                                    stop=end, skip_group_check=True)
                    else:
                        nc.tensor.matmul(o[0:96, 0:4 * WIN], rows[:, k.h4, j, 64:D], hots, start=first, stop=end,
                                         skip_group_check=True)
                        last = nc.tensor.matmul(o[0:64, 4 * WIN:8 * WIN], rows[:, k.h4, j, 0:64], hots,
                                                start=False, stop=end, skip_group_check=True)
                last.then_inc(S["sums_ready"], 1)

            def step(at):
                if mlp:
                    if at(2):
                        hidden(at(2))
                    if at(1):
                        edge_weights(at(1))
                if at(0):
                    sums(at(0))
                if sort and at(-1):
                    sort.count(pe, at(-1), at(-2))

            if sort:
                pe.sem_inc(sort.S["opened"], CREDIT)
                pe.sem_inc(sort.S["closed"], CREDIT)
            passes(pe, step, ahead=2 if mlp else 0, behind=2 if sort else 0, begin=sort and sort.begin_pass)

        @block.vector
        def _(dve):
            for a in acc.halves[0]:
                nc.vector.memset(a, 0.0).then_inc(s_zero, 1)
            nc.vector.tensor_copy(iota[:], t.iotaW[:]).then_inc(s_win, 1)
            nc.vector.tensor_copy(win[:], t.win0[:]).then_inc(s_win, 1)
            dve.wait_ge(s_win, 2)
            dve.wait_ge(s_zero, len(acc.halves[0]) + len(acc.halves[1]))
            for n in ("products_ready", "eq_ready", "added"):
                dve.sem_inc(S[n], CREDIT)

            def products(k):
                dve.wait_ge(S["sums_ready"], k.back2)
                nc.vector.tensor_tensor(eq[:, k.h2, :, :], iota[:].unsqueeze(1).broadcast_to([P, TG, WIN]),
                                        t.dstrel[:, k.span(TG)].unsqueeze(2).broadcast_to([P, TG, WIN]),
                                        ALU.is_equal).then_inc(S["eq_ready"], 1)
                dve.wait_ge(S["eq_ready"], k.done)
                last = nc.vector.tensor_tensor(
                    hot[:, k.h2, :, :, :], eq[:, k.h2, :, :].unsqueeze(2).broadcast_to([P, TG, 4, WIN]),
                    t.e4[:, k.span(TG), :].unsqueeze(3).broadcast_to([P, TG, 4, WIN]), ALU.mult)
                if mlp:
                    dve.wait_ge(S["weights_ready"], k.done)
                    dve.wait_ge(rows_in[k.h4], k.landed(TG))
                    for j in range(TG):
                        w = w_ps[k.h2][j // 2][:, mlp.width * (j % 2):mlp.width * (j % 2 + 1)]
                        nc.vector.tensor_tensor(
                            ps[:, k.h2, j, :].rearrange("p (a c) -> p a c", a=2),
                            w[:, 0:128].rearrange("p (a c) -> p a c", a=2),
                            rows[:, k.h4, j, 0:64].unsqueeze(1).broadcast_to([P, 2, 64]), ALU.mult)
                        last = nc.vector.tensor_tensor(
                            pv[:, k.h2, j, :, :].rearrange("p q (i c) -> p q i c", i=3),
                            w[:, 128:128 + 32 * kinds].rearrange("p (q c) -> p q c", q=kinds).unsqueeze(
                                2).broadcast_to([P, kinds, 3, 32]),
                            rows[:, k.h4, j, 64:D].rearrange("p (i c) -> p i c", i=3).unsqueeze(
                                1).broadcast_to([P, kinds, 3, 32]), ALU.mult)
                last.then_inc(S["products_ready"], 1)

            def add_sums(k):
                o = sum_ps[k.h2]
                at = dve.value_load(win[0:1, k.span(1)], min_val=0, max_val=NP - WIN)
                w = ds(at, WIN)
                dve.wait_ge(S["sums_ready"], k.done)
                dve.wait_ge(S["added"], k.prev)

                def add(dst, src):
                    return nc.vector.tensor_tensor(dst, dst, src, ALU.add)

                if mlp:
                    add(acc.A[0:64, 0, w], o[0:64, 0:WIN])
                    add(acc.A[64:P, :, w], o[64:P, WIN:4 * WIN].rearrange("p (k w) -> p k w", k=3))
                    add(acc.B[:, w], o[0:96, 4 * WIN:5 * WIN])
                    for d in range(3):
                        last = add(acc.C[32 * d:32 * d + 32, w], o[32 * d:32 * d + 32, (5 + d) * WIN:(6 + d) * WIN])
                    if kinds == 3:
                        last = add(acc.X[:, :, w], o[0:96, 8 * WIN:11 * WIN].rearrange("p (k w) -> p k w", k=3))
                else:
                    add(acc.V[:, :, w], o[0:96, 0:4 * WIN].rearrange("p (k w) -> p k w", k=4))
                    last = add(acc.S[:, :, w], o[0:64, 4 * WIN:8 * WIN].rearrange("p (k w) -> p k w", k=4))
                last.then_inc(S["added"], 1)

            def step(at):
                if at(1):
                    products(at(1))
                    if sort:
                        sort.one_hots(dve, at(1))
                if at(-1):
                    add_sums(at(-1))
                    if sort:
                        sort.pick(dve, at(-1))
                if sort and at(-2):
                    sort.place(dve, at(-2))

            if sort:
                for n in ("hot", "prod", "place"):
                    dve.sem_inc(sort.S[n], CREDIT)
            count = dve.value_load(t.passes[0:1, 0:1], min_val=1, max_val=NBIN)
            with dve.Fori(0, count) as p:
                run(dve, step, ahead=1, behind=2 if sort else 1, base=dve.snap(p * IT))
                nc.vector.tensor_scalar(iota[:], iota[:], float(WIN), None, ALU.add).then_inc(s_win, 1)
                nc.vector.tensor_scalar(win[:], win[:], WIN, NP - WIN, ALU.add, ALU.min).then_inc(s_win, 1)
                dve.wait_ge(s_win, p * 2 + 4)


def scale_weights(core, name, tiles, scales):
    nc = core.nc
    with nc.Block() as block:
        @block.vector
        def _(dve):
            for dst, scale in scales:
                nc.vector.tensor_scalar(dst, dst, scale, None, ALU.mult)


def finish_gated(core, t, name, acc, weights, last_layer):
    nc = core.nc
    S = {n: core.sem(f"{name}_{n}") for n in ("mixed", "mixed_copied", "turned", "pre", "sig", "used", "dve")}
    rot = last_layer
    cols = 64 if rot else 96
    srows = 65 if rot else 96
    with ExitStack() as ctx:
        sb = lambda n, s, d=F32: core.sb(f"{name}_{n}", s, d, ctx)
        sT = sb("sT", [96, NB * P])
        vT = sb("vT", [96, NB * P])
        pre = sb("pre", [P, NB, 192])
        sig = sb("sig", [P, NB, 96])
        tmp = sb("tmp", [P, NB, 96])
        if rot:
            conv = sb("conv", [P, NT, D])
            angle = sb("angle", [P, NT])
        s_ps = [core.bank[0], core.bank[1]]
        v_ps = [core.bank[2], core.bank[3]]
        out = [core.bank[4 + u // 2][:, 192 * (u % 2):192 * (u % 2) + 192] for u in range(NB)]
        half = NB * P // 2
        with nc.Block() as block:
            @block.tensor
            def _(pe):
                pe.sem_inc(S["turned"], 1)
                with pe.Fori(0, NI) as i:
                    pe.wait_ge(S["mixed_copied"], i + 1)
                    for q in range(2):
                        c = ds(i * NB * P + q * half, half)
                        nc.tensor.matmul(s_ps[q][0:srows, 0:half], weights[:, 0, 0:srows], acc.A[:, 0, c], start=True,
                                         stop=False)
                        nc.tensor.matmul(s_ps[q][0:srows, 0:half], weights[0:96, 1, 0:srows], acc.C[:, c],
                                         start=False, stop=True)
                        terms = [(weights[:, 2 + k, :], acc.A[:, k, c]) for k in range(3)]
                        terms.append((weights[0:96, 5, :], acc.B[:, c]))
                        if not rot:
                            terms += [(weights[0:96, 6 + k, :], acc.X[:, k, c]) for k in range(3)]
                        for m, (a, b) in enumerate(terms):
                            last = nc.tensor.matmul(v_ps[q][0:96, 0:half], a, b, start=m == 0,
                                                    stop=m == len(terms) - 1)
                    last.then_inc(S["mixed"], 1)
                    pe.wait_ge(S["mixed_copied"], i + 2)
                    pe.wait_ge(S["pre"], i + 1)
                    for u in range(NB):
                        nc.tensor.transpose(out[u][:, 0:srows], sT[0:srows, u * P:(u + 1) * P],
                                            t.ident[0:srows, 0:srows])
                        last = nc.tensor.transpose(out[u][:, 96:192], vT[:, u * P:(u + 1) * P], t.ident[0:96, 0:96])
                    last.then_inc(S["turned"], 1)

            @block.scalar
            def _(act):
                act.sem_inc(S["mixed_copied"], 1)
                with act.Fori(0, NI) as i:
                    act.wait_ge(S["mixed"], i + 1)
                    act.wait_ge(S["turned"], i + 1)
                    for q in range(2):
                        nc.scalar.copy(sT[0:srows, q * half:(q + 1) * half], s_ps[q][0:srows, 0:half])
                        last = nc.scalar.copy(vT[:, q * half:(q + 1) * half], v_ps[q][0:96, 0:half])
                    last.then_inc(S["mixed_copied"], 1)
                    if not rot:
                        act.wait_ge(S["pre"], i + 2)
                        act.wait_ge(S["used"], i + 1)
                        nc.scalar.activation(sig[:], pre[:, :, 0:96], ACT.Sigmoid).then_inc(S["sig"], 1)

            @block.vector
            def _(dve):
                dve.sem_inc(S["pre"], 1)
                dve.sem_inc(S["used"], 1)
                with dve.Fori(0, NI) as i:
                    dve.wait_ge(S["turned"], i + 2)
                    for u in range(NB):
                        tile = i * NB + u
                        a = t.attr[:, ds(tile, 1)]
                        if rot:
                            nc.vector.tensor_scalar(conv[:, ds(tile, 1), 0:64].rearrange("p a c -> p (a c)"),
                                                    out[u][:, 0:64], a, None, ALU.mult)
                            nc.vector.tensor_scalar(conv[:, ds(tile, 1), 64:D].rearrange("p a c -> p (a c)"),
                                                    out[u][:, 96:192], a, None, ALU.mult)
                            last = nc.vector.tensor_scalar(angle[:, ds(tile, 1)], out[u][:, 64:65], a, None, ALU.mult)
                        else:
                            last = nc.vector.scalar_tensor_tensor(
                                out=pre[:, u, :], in0=out[u], scalar=a,
                                in1=t.sc[:, ds(tile, 1), :].rearrange("p a c -> p (a c)"), op0=ALU.mult, op1=ALU.add)
                    last.then_inc(S["pre"], 1)
                    if not rot:
                        dve.wait_ge(S["sig"], i + 1)
                        dve.wait_ge(S["pre"], i + 2)
                        xs = t.x[:, ds(i * NB, NB), 0:64]
                        nc.vector.tensor_tensor(tmp[:, :, 0:64], pre[:, :, 0:64], sig[:, :, 0:64],
                                                ALU.mult).then_inc(S["dve"], 1)
                        dve.wait_ge(S["dve"], i * 2 + 1)
                        nc.vector.tensor_tensor(xs, xs, tmp[:, :, 0:64], ALU.add)
                        vec = pre[:, :, 96:192].rearrange("p u (i c) -> p u i c", i=3)
                        nc.vector.tensor_tensor(vec, vec, sig[:, :, 64:96].unsqueeze(2).broadcast_to([P, NB, 3, 32]),
                                                ALU.mult).then_inc(S["dve"], 1)
                        dve.wait_ge(S["dve"], i * 2 + 2)
                        xv = t.x[:, ds(i * NB, NB), 64:D].rearrange("p u (c i) -> p u i c", i=3)
                        nc.vector.tensor_tensor(xv, xv, vec, ALU.add).then_inc(S["used"], 1)
                        dve.wait_ge(S["used"], i + 2)

        if rot:
            ang, tri = sb("ang", [P, 2, NT]), sb("tri", [P, 2, NT])
            turns, turnsI = sb("turns", [P, 2, NT]), sb("turns_int", [P, 2, NT], I32)
            s_rot, s_ang, s_tri = core.sem(f"{name}_rot"), core.sem(f"{name}_ang"), core.sem(f"{name}_tri")
            block = ctx.enter_context(nc.Block())

            @block.vector
            def _(dve):
                link = linker(dve, s_rot)
                nc.vector.tensor_copy(ang[:, 0, :], angle[:])
                link(nc.vector.tensor_scalar(ang[:, 1, :], angle[:], math.pi / 2, None, ALU.add))
                link(nc.vector.tensor_scalar(turns[:], ang[:], 1 / (2 * math.pi), None, ALU.mult))
                link(nc.vector.tensor_copy(turnsI[:], turns[:]))
                link(nc.vector.tensor_copy(turns[:], turnsI[:]))
                two_pi_hi = 6.28125
                two_pi_lo = 2 * math.pi - two_pi_hi
                link(nc.vector.scalar_tensor_tensor(out=ang[:], in0=turns[:], scalar=-two_pi_hi, in1=ang[:],
                                                    op0=ALU.mult, op1=ALU.add))
                link(nc.vector.scalar_tensor_tensor(out=ang[:], in0=turns[:], scalar=-two_pi_lo, in1=ang[:],
                                                    op0=ALU.mult, op1=ALU.add))
                link(nc.vector.tensor_scalar(turns[:], ang[:], math.pi, -2 * math.pi, ALU.is_gt, ALU.mult))
                link(nc.vector.tensor_tensor(ang[:], ang[:], turns[:], ALU.add))
                link(nc.vector.tensor_scalar(turns[:], ang[:], -math.pi, 2 * math.pi, ALU.is_lt, ALU.mult))
                link(nc.vector.tensor_tensor(ang[:], ang[:], turns[:], ALU.add))
                nc.vector.tensor_scalar(ang[:], ang[:], 3.1415925, -3.1415925, ALU.min, ALU.max).then_inc(s_ang, 1)
                dve.wait_ge(s_tri, 1)
                scv = t.sc[:, :, 0:D]
                link(nc.vector.tensor_tensor(scv, scv, tri[:, 1, :].unsqueeze(2).broadcast_to([P, NT, D]), ALU.mult))
                link(nc.vector.tensor_tensor(conv[:], conv[:], tri[:, 0, :].unsqueeze(2).broadcast_to([P, NT, D]),
                                             ALU.mult))
                link(nc.vector.tensor_tensor(conv[:], conv[:], scv, ALU.add))
                link(nc.vector.tensor_tensor(t.x[:, :, 0:64], t.x[:, :, 0:64], conv[:, :, 0:64], ALU.add))
                xv = t.x[:, :, 64:D].rearrange("p u (c i) -> p u i c", i=3)
                link(nc.vector.tensor_tensor(xv, xv, conv[:, :, 64:D].rearrange("p u (i c) -> p u i c", i=3),
                                             ALU.add))

            @block.scalar
            def _(act):
                act.wait_ge(s_ang, 1)
                nc.scalar.activation(tri[:], ang[:], ACT.Sin).then_inc(s_tri, 1)


def finish_product(core, t, name, acc, weights, hR):
    nc = core.nc
    S = {n: core.sem(f"{name}_{n}") for n in ("mixed", "mixed_copied", "out", "tmp", "used")}
    with ExitStack() as ctx:
        sb = lambda n, s, d=F32: core.sb(f"{name}_{n}", s, d, ctx)
        sT = sb("sT", [64, NB * P])
        vT = sb("vT", [96, NB * P])
        tmp = sb("tmp", [P, NB, D])
        half = NB * P // 2
        s_ps = [core.bank[0], core.bank[1]]
        v_ps = [core.bank[2], core.bank[3]]
        out = [core.bank[4 + u // 2][:, D * (u % 2):D * (u % 2) + D] for u in range(NB)]
        block = ctx.enter_context(nc.Block())

        @block.tensor
        def _(pe):
            pe.sem_inc(S["out"], 1)
            with pe.Fori(0, NI) as i:
                pe.wait_ge(S["mixed_copied"], i + 1)
                for q in range(2):
                    c = ds(i * NB * P + q * half, half)
                    terms = [(weights[0:96, 5 + k, :], acc.V[:, 1 + k, c]) for k in range(3)]
                    terms.append((weights[0:64, 0, :], acc.S[:, 0, c]))
                    for m, (a, b) in enumerate(terms):
                        nc.tensor.matmul(s_ps[q][0:96, 0:half], a, b, start=m == 0, stop=m == len(terms) - 1)
                    terms = [(weights[0:64, 1 + k, :], acc.S[:, 1 + k, c]) for k in range(3)]
                    terms.append((weights[0:96, 4, :], acc.V[:, 0, c]))
                    terms += [(weights[0:96, 8 + k, :], acc.V[:, 1 + k, c]) for k in range(3)]
                    for m, (a, b) in enumerate(terms):
                        last = nc.tensor.matmul(v_ps[q][0:96, 0:half], a, b, start=m == 0, stop=m == len(terms) - 1)
                last.then_inc(S["mixed"], 1)
                pe.wait_ge(S["mixed_copied"], i + 2)
                pe.wait_ge(S["tmp"], i + 1)
                for u in range(NB):
                    nc.tensor.matmul(out[u][:, 0:64], sT[:, u * P:(u + 1) * P], weights[0:64, 11, 0:64],
                                     start=u % 2 == 0, stop=False, skip_group_check=True)
                    last = nc.tensor.matmul(out[u][:, 64:D], vT[:, u * P:(u + 1) * P], weights[0:96, 12, :],
                                            start=False, stop=True, skip_group_check=True)
                last.then_inc(S["out"], 1)

        @block.scalar
        def _(act):
            act.sem_inc(S["mixed_copied"], 1)
            with act.Fori(0, NI) as i:
                act.wait_ge(S["mixed"], i + 1)
                act.wait_ge(S["out"], i + 1)
                for q in range(2):
                    nc.scalar.copy(sT[:, q * half:(q + 1) * half], s_ps[q][0:64, 0:half])
                    last = nc.scalar.copy(vT[:, q * half:(q + 1) * half], v_ps[q][0:96, 0:half])
                last.then_inc(S["mixed_copied"], 1)

        @block.vector
        def _(dve):
            dve.sem_inc(S["tmp"], 1)
            with dve.Fori(0, NI) as i:
                dve.wait_ge(S["out"], i + 2)
                for u in range(NB):
                    last = nc.vector.scalar_tensor_tensor(
                        out=tmp[:, u, :], in0=out[u], scalar=0.0,
                        in1=hR[:, ds(i * NB + u, 1), :].rearrange("p a c -> p (a c)"), op0=ALU.max, op1=ALU.add)
                last.then_inc(S["tmp"], 1)
                dve.wait_ge(S["tmp"], i + 2)
                xs = t.x[:, ds(i * NB, NB), 0:64]
                nc.vector.tensor_tensor(xs, xs, tmp[:, :, 0:64], ALU.add)
                xv = t.x[:, ds(i * NB, NB), 64:D].rearrange("p u (c i) -> p u i c", i=3)
                nc.vector.tensor_tensor(xv, xv, tmp[:, :, 64:D].rearrange("p u (i c) -> p u i c", i=3),
                                        ALU.add).then_inc(S["used"], 1)
                dve.wait_ge(S["used"], i + 1)


def order_tensors(core):
    o = Bundle()
    o.place = core.sb("order_place", [P, ET])
    o.before = core.sb("order_before", [P, ET])
    o.incl = core.sb("order_incl", [P, NBIN])
    return o


def count_bins(core, t, o, ctx):
    nc = core.nc
    W = TG * NBIN
    S = {n: core.sem(f"count_{n}") for n in ("iota", "matrices", "hot", "counted", "total", "dve")}
    sb = lambda n, s, d=F32: core.sb(f"order_{n}", s, d, ctx)
    o.hot = sb("hot", [P, 4, TG, NBIN], BF16)
    o.ones, o.below, o.rest = (sb(n, [P, P], BF16) for n in ("ones", "below", "rest"))
    o.onef = sb("onef", [1, P])
    o.excl = sb("excl", [P, NBIN])
    o.prod = sb("prod", [P, 2, TG, NBIN])
    o.bins = sb("bins", [P, ET], BF16)
    o.iota = sb("iota", [P, NBIN], BF16)

    def one_hots(k, sem):
        return nc.vector.tensor_tensor(
            o.hot[:, k.h4, :, :], o.iota[:].unsqueeze(1).broadcast_to([P, TG, NBIN]),
            o.bins[:, k.span(TG)].unsqueeze(2).broadcast_to([P, TG, NBIN]), ALU.is_equal).then_inc(sem, 1)

    o.one_hots = one_hots
    with ExitStack() as cctx:
        iotaI = core.sb("order_iota_int", [P, NBIN], I32, cctx)
        binsI = core.sb("order_bins_int", [P, ET], I32, cctx)
        total = core.sb("order_total", [P, NBIN], F32, cctx)
        same = core.sb("order_same", [P, NG], F32, cctx)
        zero = core.sb("order_zero", [P, P], BF16, cctx)
        block = cctx.enter_context(nc.Block())

        @block.gpsimd
        def _(pool):
            nc.gpsimd.iota(iotaI[:], pattern=[[1, NBIN]], base=0, channel_multiplier=0).then_inc(S["iota"], 1)
            nc.gpsimd.memset(o.ones[:], 1.0).then_inc(S["matrices"], 1)
            nc.gpsimd.memset(zero[:], 0.0).then_inc(S["matrices"], 1)
            nc.gpsimd.memset(o.onef[:], 1.0).then_inc(S["matrices"], 1)
            pool.wait_ge(S["matrices"], 3)
            nc.gpsimd.affine_select(out=o.below[:], in_=o.ones[:], compare_op=ALU.is_gt, fill=0.0, base=0,
                                    pattern=[[1, P]], channel_multiplier=-1).then_inc(S["matrices"], 1)
            nc.gpsimd.affine_select(out=o.rest[:], in_=o.ones[:], compare_op=ALU.is_ge, fill=0.0, base=0,
                                    pattern=[[-1, P]], channel_multiplier=1).then_inc(S["matrices"], 1)

        @block.tensor
        def _(pe):
            pe.wait_ge(S["matrices"], 5)
            pe.sem_inc(S["counted"], CREDIT)
            pe.wait_ge(S["hot"], CREDIT + 1)
            nc.tensor.matmul(core.bank[0][:, 0:W], zero[:], o.hot[:, 0, :, :], start=True, stop=False,
                             skip_group_check=True)

            def step(at):
                k = at(0)
                pe.wait_ge(S["hot"], k.done)
                nc.tensor.matmul(core.bank[0][:, 0:W], o.ones[:], o.hot[:, k.h4, :, :], start=False, stop=False,
                                 skip_group_check=True).then_inc(S["counted"], 1)

            run(pe, step)
            nc.tensor.matmul(core.bank[0][:, 0:W], zero[:], o.hot[:, 0, :, :], start=False, stop=True,
                             skip_group_check=True).then_inc(S["total"], 1)

        @block.vector
        def _(dve):
            link = linker(dve, S["dve"])
            dve.wait_ge(S["iota"], 1)
            link(nc.vector.tensor_copy(o.iota[:], iotaI[:]))
            link(nc.vector.tensor_scalar(binsI[:], t.srcI[:], 5, None, ALU.logical_shift_right))
            link(nc.vector.tensor_copy(o.bins[:], binsI[:]))
            dve.sem_inc(S["hot"], CREDIT)

            def step(at):
                k = at(0)
                dve.wait_ge(S["counted"], k.back4)
                one_hots(k, S["hot"])

            run(dve, step)
            dve.wait_ge(S["total"], 1)
            link(nc.vector.tensor_reduce(total[:], core.bank[0][:, 0:W].rearrange("p (j b) -> p b j", j=TG), AX.X,
                                         ALU.add))
            link(nc.vector.memset(o.excl[:], 0.0))
            link(nc.vector.tensor_tensor_scan(o.incl[:], total[:], o.excl[:], 0.0, ALU.add, ALU.add))
            link(nc.vector.tensor_tensor(o.excl[:], o.incl[:], total[:], ALU.subtract))
            bins = o.bins[:].rearrange("p (g j) -> p g j", j=TG)
            before = o.before[:].rearrange("p (g j) -> p g j", j=TG)
            link(nc.vector.memset(o.before[:], 0.0))
            for j in range(1, TG):
                for q in range(j):
                    link(nc.vector.tensor_tensor(same[:], bins[:, :, j], bins[:, :, q], ALU.is_equal))
                    link(nc.vector.tensor_tensor(before[:, :, j], before[:, :, j], same[:], ALU.add))


class Sort:

    def __init__(self, core, o):
        self.nc, self.o = core.nc, o
        self.S = {n: core.sem(f"sort_{n}") for n in ("hot", "opened", "closed", "prod", "place")}
        self.bank = [core.bank[0], core.bank[1]]

    def add(self, dst, lhsT, slot):
        for j in range(TG):
            last = self.nc.tensor.matmul(dst[:, 0:NBIN], lhsT, self.o.hot[:, slot, j, :], start=False, stop=False,
                                         skip_group_check=True)
        return last

    def begin_pass(self, pe, first):
        pe.wait_ge(self.S["prod"], first.prev)
        for b in self.bank:
            self.nc.tensor.matmul(b[:, 0:NBIN], self.o.onef[:], self.o.excl[0:1, :], start=True, stop=False,
                                  skip_group_check=True)

    def count(self, pe, k, before):
        S, o, bank = self.S, self.o, self.bank
        pe.wait_ge(S["hot"], k.done)
        self.add(bank[k.h2], o.below[:], k.h4).then_inc(S["opened"], 1)
        pe.wait_ge(S["prod"], k.prev)
        if before:
            self.add(bank[1 - k.h2], o.rest[:], before.h4)
        self.add(bank[1 - k.h2], o.ones[:], k.h4).then_inc(S["closed"], 1)

    def one_hots(self, dve, k):
        dve.wait_ge(self.S["closed"], k.back2)
        self.o.one_hots(k, self.S["hot"])

    def pick(self, dve, k):
        S, o = self.S, self.o
        dve.wait_ge(S["opened"], k.done)
        dve.wait_ge(S["place"], k.back2)
        self.nc.vector.tensor_tensor(
            o.prod[:, k.h2], self.bank[k.h2][:, 0:NBIN].unsqueeze(1).broadcast_to([P, TG, NBIN]),
            o.hot[:, k.h4, :, :], ALU.mult).then_inc(S["prod"], 1)

    def place(self, dve, k):
        dve.wait_ge(self.S["prod"], k.done)
        self.nc.vector.tensor_reduce(self.o.place[:, k.span(TG)], self.o.prod[:, k.h2], AX.X, ALU.add).then_inc(
            self.S["place"], 1)


def attention_nodes(core, t, ins, a):
    nc = core.nc
    H = 128
    S = {n: core.sem(f"n3_{n}") for n in ("h_ready", "turned", "turned_copied", "lin", "lin_copied", "stored", "w",
                                          "self_dve", "var", "std")}
    with ExitStack() as ctx:
        sb = lambda n, s, d=F32: core.sb(f"n3_{n}", s, d, ctx)
        xm, rstd = sb("xm", [P, NT, D]), sb("rstd", [P, NT])
        center(core, t, "n3", xm, rstd)
        h = sb("h", [P, NB, D])
        hT = sb("hT", [P, NB, P])
        wy = sb("wy", [P, 512])
        ws = sb("ws", [P, 130])
        y = sb("y", [P, NB, 512])
        own = sb("own", [P, NT, H])
        hs = sb("hs", [P, NT, 32])
        rowb = sb("rowb", [P, 3, H])
        loads = [(wy[:, 0:256], ins["L3_gnn_d2t_w1"][0:128, :]), (wy[:, 256:512], ins["L3_gnn_t2d_w1"][0:128, :]),
                 (ws[:, 0:128], ins["L3_gnn_self_w"]), (ws[:, 128:129], ins["L3_gnn_w_att"][128:256, :]),
                 (ws[:, 129:130], ins["L3_gnn_w_att"][0:128, :])]
        for k, n in enumerate(("self_b", "self_g", "self_be")):
            loads.append((rowb[:, k, :], ins[f"L3_gnn_{n}"].rearrange("(a n) -> a n", a=1).broadcast_to([P, H])))
        turned = [core.bank[u // 4][:, P * (u % 4):P * (u % 4) + P] for u in range(NB)]
        lin = [(core.bank[2 + 2 * (u % 3)], core.bank[3 + 2 * (u % 3)]) for u in range(NB)]
        with nc.Block() as block:
            @block.scalar
            def _(act):
                with act.Fori(0, NI) as i:
                    act.wait_ge(S["turned_copied"], i + 1)
                    for u in range(NB):
                        tile = i * NB + u
                        last = nc.scalar.activation(h[:, u, :], xm[:, ds(tile, 1), :].rearrange("p a c -> p (a c)"),
                                                    ACT.Relu, scale=rstd[:, ds(tile, 1)])
                    last.then_inc(S["h_ready"], 1)

            @block.tensor
            def _(pe):
                pe.wait_ge(S["w"], 16 * len(loads))
                pe.sem_inc(S["turned"], 1)
                pe.sem_inc(S["lin"], 1)
                with pe.Fori(0, NI) as i:
                    pe.wait_ge(S["h_ready"], i + 1)
                    pe.wait_ge(S["turned_copied"], i + 1)
                    for u in range(NB):
                        last = nc.tensor.transpose(turned[u], h[:, u, 0:H], t.ident[:])
                    last.then_inc(S["turned"], 1)
                    pe.wait_ge(S["turned_copied"], i + 2)
                    for u in range(NB):
                        pe.wait_ge(S["lin_copied"], i * NB + max(u - 2, 0) + 1)
                        nc.tensor.matmul(lin[u][0][:, :], hT[:, u, :], wy[:], start=True, stop=True)
                        nc.tensor.matmul(lin[u][1][:, 0:130], hT[:, u, :], ws[:], start=True,
                                         stop=True).then_inc(S["lin"], 1)

            @block.vector
            def _(dve):
                dve.sem_inc(S["turned_copied"], 1)
                dve.sem_inc(S["lin_copied"], 1)
                with dve.Fori(0, NI) as i:
                    dve.wait_ge(S["h_ready"], i + 1)
                    dve.wait_ge(S["turned"], i + 2)
                    dve.wait_ge(S["lin"], i * NB + 1)
                    nc.vector.tensor_copy(hT[:, 0:4, :], core.bank[0][:, :].rearrange("p (u n) -> p u n", u=4))
                    nc.vector.tensor_copy(hT[:, 4, :], core.bank[1][:, 0:P])
                    nc.vector.tensor_copy(hs[:, ds(i * NB, NB), :], h[:, :, H:D]).then_inc(S["turned_copied"], 1)
                    dve.wait_ge(S["stored"], i * 32 + 32)
                    for u in range(NB):
                        tile = i * NB + u
                        dve.wait_ge(S["lin"], i * NB + u + 2)
                        nc.vector.tensor_copy(y[:, u, :], lin[u][0][:, :])
                        nc.vector.tensor_copy(own[:, ds(tile, 1), :].rearrange("p a c -> p (a c)"),
                                              lin[u][1][:, 0:H])
                        nc.vector.tensor_copy(a.parts[:, ds(tile, 1), :].rearrange("p a c -> p (a c)"),
                                              lin[u][1][:, H:H + 2]).then_inc(S["lin_copied"], 1)

            @block.sync
            def _(sp):
                for dst, src in loads:
                    sp.dma_start(dst, src).then_inc(S["w"], 16)
                sp.sem_inc(S["stored"], 32)
                table = a.table.rearrange("(s i u p) d -> s i p u d", s=2, u=NB, p=P)
                with sp.Fori(0, NI) as i:
                    sp.wait_ge(S["lin_copied"], i * NB + NB + 1)
                    for s in range(2):
                        sp.dma_start(table[s, ds(i, 1)].rearrange("a p u d -> (a p) u d"),
                                     y[:, :, 256 * s:256 * s + 256]).then_inc(S["stored"], 16)
                sp.wait_ge(S["stored"], NI * 32 + 32)

        add_block(core, t, "own", own, rowb, hs)


def add_block(core, t, name, v, rowb, hs=None):
    nc = core.nc
    H = 128
    s_dve, s_var, s_std = (core.sem(f"{name}_{n}") for n in ("block_dve", "block_var", "block_std"))
    with ExitStack() as ctx:
        sb = lambda n, s, d=F32: core.sb(f"{name}_{n}", s, d, ctx)
        sq, m, var, std = sb("sq", [P, NT, H]), sb("m", [P, NT]), sb("v", [P, NT]), sb("std", [P, NT])
        block = ctx.enter_context(nc.Block())

        @block.vector
        def _(dve):
            link = linker(dve, s_dve)
            tt = nc.vector.tensor_tensor
            per_node = lambda a: a.unsqueeze(2).broadcast_to([P, NT, H])
            per_col = lambda k: rowb[:, k, :].unsqueeze(1).broadcast_to([P, NT, H])
            link(tt(v[:], v[:], per_col(0), ALU.add))
            link(nc.vector.tensor_reduce(m[:], v[:], AX.X, ALU.add))
            link(nc.vector.tensor_scalar(m[:], m[:], 1.0 / H, None, ALU.mult))
            link(tt(v[:], v[:], per_node(m[:]), ALU.subtract))
            link(tt(sq[:], v[:], v[:], ALU.mult))
            link(nc.vector.tensor_reduce(var[:], sq[:], AX.X, ALU.add))
            nc.vector.tensor_scalar(var[:], var[:], 1.0 / H, EPS, ALU.mult, ALU.add).then_inc(s_var, 1)
            dve.wait_ge(s_std, 1)
            link(nc.vector.reciprocal(std[:], std[:]))
            link(tt(v[:], v[:], per_node(std[:]), ALU.mult))
            link(tt(v[:], v[:], per_col(1), ALU.mult))
            link(tt(v[:], v[:], per_col(2), ALU.add))
            xs = t.x[:, :, 0:H]
            link(nc.vector.scalar_tensor_tensor(out=xs, in0=v[:], scalar=0.0, in1=xs, op0=ALU.max, op1=ALU.add))
            if hs is not None:
                link(tt(t.x[:, :, H:D], t.x[:, :, H:D], hs[:], ALU.add))

        @block.scalar
        def _(act):
            act.wait_ge(s_var, 1)
            nc.scalar.activation(std[:], var[:], ACT.Sqrt).then_inc(s_std, 1)


def edge_masks(core, t, ins, a):
    nc = core.nc
    s_in, s_out, s_dve, s_rows, s_iota = (core.sem(f"m3_{n}") for n in ("loaded", "stored", "dve", "rows", "iota"))
    with ExitStack() as ctx:
        sb = lambda n, s, d=F32: core.sb(f"m3_{n}", s, d, ctx)
        ints = sb("ints", [P, ET, 2], I32)
        both = sb("both", [P, 2, ET], I32)
        f = sb("f", [P, ET, 2])
        idxf = sb("idxf", [P, ET])
        rowsI = sb("rowsI", [IT2, 2, 2 * GE], I32)
        rowsF = sb("rowsF", [IT2, 2, 2 * GE])
        low = sb("low", [IT2, 2, 2 * GE], I32)
        lowB = sb("lowB", [IT2, 2, 2 * GE], BF16)
        maskB = sb("maskB", [IT2, 2, 2 * GE], BF16)
        iotaI = sb("iotaI", [P, P], I32)
        block = ctx.enter_context(nc.Block())

        @block.gpsimd
        def _(pool):
            nc.gpsimd.iota(iotaI[:], pattern=[[1, P]], base=0, channel_multiplier=0).then_inc(s_iota, 1)
            nc.gpsimd.iota(a.iotaP_int[:], pattern=[[0, 1]], base=0, channel_multiplier=1).then_inc(s_iota, 1)

        @block.sync
        def _(sp):
            sp.dma_start(both[:, 1, :], ins["dst_pt"]).then_inc(s_in, 16)
            sp.dma_start(both[:, 0, :], ins["src_pt"]).then_inc(s_in, 16)
            sp.dma_start(rowsI[:, 0, :], ins["src_rows"].rearrange("(i h) e -> i (h e)", h=2)).then_inc(s_in, 16)
            sp.dma_start(rowsI[:, 1, :], ins["dst_rows"].rearrange("(i h) e -> i (h e)", h=2)).then_inc(s_in, 16)
            sp.wait_ge(s_rows, 1)
            for s in range(2):
                sp.dma_start(a.low_rows[s].rearrange("(i e) -> i e", i=IT2), lowB[:, s, :]).then_inc(s_out, 16)
                sp.dma_start(a.mask_rows[s].rearrange("(i e) -> i e", i=IT2), maskB[:, s, :]).then_inc(s_out, 16)
            sp.wait_ge(s_out, 64)

        @block.vector
        def _(dve):
            link = linker(dve, s_dve)
            tt, ts = nc.vector.tensor_tensor, nc.vector.tensor_scalar
            dve.wait_ge(s_iota, 2)
            link(nc.vector.tensor_copy(a.iota[:], iotaI[:]))
            link(nc.vector.tensor_copy(a.iotaP[:], a.iotaP_int[:]))
            dve.wait_ge(s_in, 64)
            for s in range(2):
                link(ts(ints[:, :, s], both[:, s, :], 7, None, ALU.logical_shift_right))
                link(nc.vector.tensor_copy(f[:, :, s], both[:, s, :]))
            link(nc.vector.tensor_copy(a.high[:], ints[:]))
            link(nc.vector.memset(a.meta[:], 0.0))
            link(nc.vector.tensor_copy(a.meta[:, :, 0], f[:, :, 0]))
            link(tt(a.meta[:, :, 1], f[:, :, 0], f[:, :, 1], ALU.is_lt))
            link(tt(a.meta[:, :, 2], f[:, :, 0], f[:, :, 1], ALU.is_gt))
            link(ts(idxf[:], a.meta[:, :, 2], float(NP), None, ALU.mult))
            link(tt(idxf[:], idxf[:], f[:, :, 1], ALU.add))
            link(nc.vector.tensor_copy(a.yidx[:], idxf[:]))
            link(nc.vector.tensor_copy(rowsF[:], rowsI[:]))
            link(ts(low[:], rowsI[:], 127, None, ALU.bitwise_and))
            link(nc.vector.tensor_copy(lowB[:], low[:]))
            link(tt(maskB[:, 0, :], rowsF[:, 0, :], rowsF[:, 1, :], ALU.is_lt))
            tt(maskB[:, 1, :], rowsF[:, 0, :], rowsF[:, 1, :], ALU.is_gt).then_inc(s_rows, 1)


def logits(core, t, ins, a):
    nc = core.nc
    S = {n: core.sem(f"g3_{n}") for n in ("spread", "hot_src", "distance", "hot_dst", "picked", "hot_high", "prod", "logit")}
    row_in = [core.sem(f"g3_row_in{h}") for h in range(4)]
    s_ones, s_split = core.sem("g3_ones"), core.sem("g3_split")
    with ExitStack() as ctx:
        sb = lambda n, s, d=F32: core.sb(f"g3_{n}", s, d, ctx)
        row = sb("row", [1, 4, 2, GE], BF16)
        ones = sb("ones", [1, P], BF16)
        hot = sb("hot", [P, 2, 2, GE], BF16)
        distance = sb("distance", [P, GE])
        minus_row = sb("minus_row", [P, 1])
        third = sb("third", [P, 3, NT, 2], BF16)
        rest = sb("rest", [P, NT, 2])
        hh = sb("hh", [P, 2, TG, 2, NT])
        prod = sb("prod", [P, 2, TG, 2, NT])
        block = ctx.enter_context(nc.Block())
        spread = [[core.bank[2 * h + s] for s in range(2)] for h in range(2)]
        pick = [core.bank[4 + h] for h in range(2)]

        @block.sync
        def _(sp):
            def step(at):
                k = at(0)
                sp.wait_ge(S["spread"], k.back4)
                for s in range(2):
                    sp.dma_start(row[:, k.h4, s, :], a.low_rows[s:s + 1, k.span(GE)]).then_inc(row_in[k.h4], 16)

            run(sp, step)

        @block.tensor
        def _(pe):
            pe.sem_inc(S["spread"], CREDIT)
            pe.sem_inc(S["picked"], CREDIT)
            pe.wait_ge(s_ones, 1)

            def spread_rows(k):
                pe.wait_ge(row_in[k.h4], k.landed(2))
                pe.wait_ge(S["hot_src"], k.back2)
                pe.wait_ge(S["distance"], k.back2)
                for s in range(2):
                    last = nc.tensor.matmul(spread[k.h2][s][:, :], ones[:], row[:, k.h4, s, :], start=True,
                                            stop=True)
                last.then_inc(S["spread"], 1)

            def pick_parts(k):
                pe.wait_ge(S["hot_src"], k.done)
                pe.wait_ge(S["hot_dst"], k.done)
                pe.wait_ge(S["prod"], k.back2)
                for j in range(TG):
                    for s in range(2):
                        for q in range(3):
                            last = nc.tensor.matmul(pick[k.h2][:, (2 * j + s) * NT:(2 * j + s + 1) * NT],
                                                    hot[:, k.h2, s, j * P:(j + 1) * P], third[:, q, :, s],
                                                    start=q == 0, stop=q == 2)
                last.then_inc(S["picked"], 1)

            def step(at):
                if at(2):
                    spread_rows(at(2))
                if at(0):
                    pick_parts(at(0))

            run(pe, step, ahead=2)

        @block.scalar
        def _(act):
            act.sem_inc(S["distance"], CREDIT)
            act.sem_inc(S["hot_dst"], CREDIT)
            act.wait_ge(s_ones, 1)

            def step(at):
                k = at(0)
                act.wait_ge(S["spread"], k.done)
                act.wait_ge(S["hot_dst"], k.prev)
                nc.scalar.activation(distance[:], spread[k.h2][1][:, :], ACT.Abs, bias=minus_row[:, 0:1]).then_inc(
                    S["distance"], 1)
                act.wait_ge(S["distance"], k.done)
                act.wait_ge(S["picked"], k.back2)
                nc.scalar.activation(hot[:, k.h2, 1, :], distance[:], ACT.Relu, scale=-1.0, bias=1.0).then_inc(
                    S["hot_dst"], 1)

            run(act, step)

        @block.vector
        def _(dve):
            link = linker(dve, s_split)
            link(nc.vector.memset(ones[:], 1.0))
            link(nc.vector.tensor_scalar(minus_row[:], a.iotaP[:], -1.0, None, ALU.mult))
            link(nc.vector.tensor_copy(rest[:], a.parts[:]))
            for q in range(3):
                link(nc.vector.tensor_copy(third[:, q], rest[:]))
                if q < 2:
                    link(nc.vector.tensor_tensor(rest[:], rest[:], third[:, q], ALU.subtract))
            dve.sem_inc(s_ones, 1)
            for n in ("hot_src", "hot_high", "prod", "logit"):
                dve.sem_inc(S[n], CREDIT)

            def low_hots(k):
                dve.wait_ge(S["spread"], k.done)
                dve.wait_ge(S["picked"], k.back2)
                nc.vector.tensor_scalar(hot[:, k.h2, 0, :], spread[k.h2][0][:, :], a.iotaP[:, 0:1], None,
                                        ALU.is_equal).then_inc(S["hot_src"], 1)

            def high_hots(k):
                dve.wait_ge(S["prod"], k.back2)
                nc.vector.tensor_tensor(
                    hh[:, k.h2], a.iota[:, 0:NT].unsqueeze(1).broadcast_to([P, 2 * TG, NT]).rearrange(
                        "p (j s) c -> p j s c", s=2),
                    a.high[:, k.span(TG), :].unsqueeze(3).broadcast_to([P, TG, 2, NT]),
                    ALU.is_equal).then_inc(S["hot_high"], 1)

            def multiply(k):
                dve.wait_ge(S["hot_high"], k.done)
                dve.wait_ge(S["picked"], k.done)
                dve.wait_ge(S["logit"], k.back2)
                nc.vector.tensor_tensor(prod[:, k.h2], pick[k.h2][:, 0:2 * TG * NT].rearrange(
                    "p (j s c) -> p j s c", j=TG, s=2), hh[:, k.h2], ALU.mult).then_inc(S["prod"], 1)

            def reduce(k):
                dve.wait_ge(S["prod"], k.done)
                nc.vector.tensor_reduce(a.logit[:, k.span(TG)], prod[:, k.h2], AX.XY, ALU.add).then_inc(
                    S["logit"], 1)

            def step(at):
                if at(1):
                    low_hots(at(1))
                if at(-1):
                    multiply(at(-1))
                if at(0):
                    high_hots(at(0))
                if at(-1):
                    reduce(at(-1))

            run(dve, step, ahead=1, behind=1)


def softmax(core, t, ins, a):
    nc = core.nc
    s_dve, s_exp, s_e, s_max, s_mr, s_sum, s_sr, s_b, s_turn, s_tc, s_out = (core.sem(f"s3_{n}") for n in (
        "dve", "shifted", "exp", "max", "max_all", "sum", "sum_all", "b", "turned", "turned_copied", "stored"))
    s_w = core.sem("s3_weights")
    chunks = [(c, min(P, ET - c)) for c in range(0, ET, P)]
    with ExitStack() as ctx:
        sb = lambda n, s, d=F32: core.sb(f"s3_{n}", s, d, ctx)
        b = sb("b", [P, 1])
        mx, mxa, sm, sma = (sb(n, [P, 2]) for n in ("mx", "mxa", "sm", "sma"))
        tmp = sb("tmp", [P, ET])
        part = sb("part", [P, 2, ET])
        ex = sb("ex", [P, ET])
        turned = sb("turned", [P, 2, len(chunks), P])
        md, mt = a.meta[:, :, 1], a.meta[:, :, 2]
        block = ctx.enter_context(nc.Block())

        @block.sync
        def _(sp):
            sp.dma_start(b[:], ins["L3_gnn_b_att"].rearrange("(a n) -> a n", a=1).broadcast_to([P, 1])).then_inc(
                s_b, 16)
            for s in range(2):
                for c, (at, n) in enumerate(chunks):
                    sp.wait_ge(s_tc, s * len(chunks) + c + 1)
                    sp.dma_start(a.attn_rows[s, at * P:(at + n) * P].rearrange("(r p) -> r p", p=P),
                                 turned[0:n, s, c, :]).then_inc(s_out, 16)
            sp.wait_ge(s_out, 32 * len(chunks))

        @block.gpsimd
        def _(pool):
            pool.wait_ge(s_max, 1)
            nc.gpsimd.partition_all_reduce(mxa[:], mx[:], P, bass.bass_isa.ReduceOp.max).then_inc(s_mr, 1)
            pool.wait_ge(s_sum, 1)
            nc.gpsimd.partition_all_reduce(sma[:], sm[:], P, bass.bass_isa.ReduceOp.add).then_inc(s_sr, 1)

        @block.scalar
        def _(act):
            act.wait_ge(s_exp, 1)
            nc.scalar.activation(ex[:], tmp[:], ACT.Exp).then_inc(s_e, 1)

        @block.tensor
        def _(pe):
            pe.wait_ge(s_w, 1)
            for s in range(2):
                for c, (at, n) in enumerate(chunks):
                    k = s * len(chunks) + c
                    if k >= 2:
                        pe.wait_ge(s_tc, k - 1)
                    nc.tensor.transpose(core.bank[k % 2][0:n, 0:P], part[:, s, at:at + n], t.ident[:]).then_inc(
                        s_turn, 1)

        @block.vector
        def _(dve):
            link = linker(dve, s_dve)
            tt, ts, stt = nc.vector.tensor_tensor, nc.vector.tensor_scalar, nc.vector.scalar_tensor_tensor
            dve.wait_ge(s_b, 16)
            link(ts(a.logit[:], a.logit[:], b[:, 0:1], None, ALU.add))
            link(stt(out=a.logit[:], in0=a.logit[:], scalar=0.01, in1=a.logit[:], op0=ALU.mult, op1=ALU.max))
            for s, m in enumerate((md, mt)):
                link(tt(part[:, s, :], a.logit[:], m, ALU.mult))
                link(ts(tmp[:], m, -1.0, 1e30, ALU.add, ALU.mult))
                link(tt(part[:, s, :], part[:, s, :], tmp[:], ALU.add))
                ins_ = nc.vector.tensor_reduce(mx[:, s:s + 1], part[:, s, :], AX.X, ALU.max)
                link(ins_) if s == 0 else ins_.then_inc(s_max, 1)
            dve.wait_ge(s_mr, 1)
            link(ts(tmp[:], md, mxa[:, 0:1], None, ALU.mult))
            link(ts(part[:, 0, :], mt, mxa[:, 1:2], None, ALU.mult))
            link(tt(tmp[:], tmp[:], part[:, 0, :], ALU.add))
            link(tt(tmp[:], a.logit[:], tmp[:], ALU.subtract))
            ts(tmp[:], tmp[:], 0.0, None, ALU.min).then_inc(s_exp, 1)
            dve.wait_ge(s_e, 1)
            link(tt(part[:, 0, :], ex[:], md, ALU.mult))
            link(tt(part[:, 1, :], ex[:], mt, ALU.mult))
            nc.vector.tensor_reduce(sm[:], part[:], AX.X, ALU.add).then_inc(s_sum, 1)
            dve.wait_ge(s_sr, 1)
            link(ts(sma[:], sma[:], 1e-30, None, ALU.max))
            link(nc.vector.reciprocal(sma[:], sma[:]))
            for s in range(2):
                link(ts(part[:, s, :], part[:, s, :], sma[:, s:s + 1], None, ALU.mult))
            tt(a.attn[:], part[:, 0, :], part[:, 1, :], ALU.add).then_inc(s_w, 1)
            for k in range(2 * len(chunks)):
                s, c = divmod(k, len(chunks))
                dve.wait_ge(s_turn, k + 1)
                n = chunks[c][1]
                nc.vector.tensor_copy(turned[0:n, s, c, :], core.bank[k % 2][0:n, 0:P]).then_inc(s_tc, 1)


def source_windows(core, t, a, order):
    nc = core.nc
    s_iota, s_base, s_bl, s_span, s_red, s_bases, s_d = (core.sem(f"o3_{n}") for n in (
        "starts", "base_stored", "base_loaded", "span", "span_all", "bases", "windows_dve"))
    with ExitStack() as ctx:
        sb = lambda n, s, d=F32: core.sb(f"o3_{n}", s, d, ctx)
        start = sb("start", [IT2, 2])
        startI = sb("startI", [IT2, 2], I32)
        cmp = sb("cmp", [IT2, 2, NBIN])
        lo, hi = sb("lo", [IT2, 2]), sb("hi", [IT2, 2])
        span, spanR, spanI = sb("span", [P, 1]), sb("spanR", [P, 1]), sb("spanI", [P, 1], I32)
        block = ctx.enter_context(nc.Block())

        @block.gpsimd
        def _(pool):
            nc.gpsimd.iota(startI[:], pattern=[[GE, 2]], base=0, channel_multiplier=2 * GE).then_inc(s_iota, 1)
            pool.wait_ge(s_span, 1)
            nc.gpsimd.partition_all_reduce(spanR[:], span[:], P, bass.bass_isa.ReduceOp.max).then_inc(s_red, 1)

        @block.sync
        def _(sp):
            sp.wait_ge(s_bases, 1)
            sp.dma_start(a.base_dram.rearrange("(i h) -> i h", h=2), lo[:]).then_inc(s_base, 16)
            sp.wait_ge(s_base, 16)
            sp.dma_start(a.baseB[:], a.base_dram.rearrange("(a g) -> a g", a=1).broadcast_to([P, NG])).then_inc(
                s_bl, 16)
            sp.wait_ge(s_bl, 16)

        @block.vector
        def _(dve):
            link = linker(dve, s_d)
            nc.vector.tensor_tensor(a.pos[:], order.place[:], order.before[:], ALU.add)
            dve.wait_ge(s_iota, 1)
            link(nc.vector.tensor_copy(start[:], startI[:]))
            inclB = order.incl[0:IT2, :].unsqueeze(1).broadcast_to([IT2, 2, NBIN])
            for dst, last in ((lo, False), (hi, True)):
                link(nc.vector.tensor_tensor(cmp[:], inclB, start[:].unsqueeze(2).broadcast_to([IT2, 2, NBIN]),
                                             ALU.is_le))
                link(nc.vector.tensor_reduce(dst[:], cmp[:], AX.X, ALU.add))
                if not last:
                    link(nc.vector.tensor_scalar(start[:], start[:], GE - 1.0, None, ALU.add))
            link(nc.vector.tensor_tensor(hi[:], hi[:], lo[:], ALU.subtract))
            nc.vector.tensor_scalar(lo[:], lo[:], 32.0, None, ALU.mult).then_inc(s_bases, 1)
            link(nc.vector.memset(span[:], 0.0))
            nc.vector.tensor_reduce(span[0:IT2, :], hi[:], AX.X, ALU.max).then_inc(s_span, 1)
            dve.wait_ge(s_red, 1)
            link(nc.vector.tensor_copy(spanI[:], spanR[:]))
            link(nc.vector.tensor_scalar(spanI[:], spanI[:], 1, None, ALU.logical_shift_right))
            link(nc.vector.tensor_scalar(a.passes[:], spanI[0:1, :], 1, None, ALU.add))
            dve.wait_ge(s_bl, 16)
            link(nc.vector.tensor_copy(a.win0[:], a.baseB[0:1, :]))


def messages(core, t, ins, a):
    nc = core.nc
    H, O = 256, 128
    names = ("scaled", "z_ready", "z_copied", "bn1", "stats1", "std1", "recip1", "rstd1", "normed1", "turned",
             "hidden", "u_ready", "g_ready", "half", "comb", "bn2", "stats2", "std2", "rstd2", "centered", "gained",
             "message", "indices", "places", "turns", "loads")
    S = {n: core.sem(f"x3_{n}") for n in names}
    in_ = [core.sem(f"x3_loaded{h}") for h in range(4)]
    mask_in = [core.sem(f"x3_masks_loaded{h}") for h in range(4)]
    rows_in = [core.gpsimd_dma_sem(f"x3_gathered{h}") for h in range(4)]
    sent = [core.gpsimd_dma_sem(f"x3_sent{h}") for h in range(2)]
    s_w, s_raw, s_split, s_parts, s_c = (core.sem(f"x3_{n}") for n in ("w", "raw", "split", "parts", "const"))
    with ExitStack() as ctx:
        sb = lambda n, s, d=F32: core.sb(f"x3_{n}", s, d, ctx)
        w1b = sb("w1b", [P, H])
        w2 = sb("w2", [P, 2, 2, O])
        gb = sb("gb", [P, 2, 2, 2])
        raw = sb("raw", [2, 512])
        raw2 = sb("raw2", [1, 256])
        split, split2 = sb("split", [2, 3, 512], BF16), sb("split2", [1, 3, 256], BF16)
        vecs, vecs2 = sb("vecs", [6, 512], BF16), sb("vecs2", [3, 256], BF16)
        ones = sb("ones", [3, P], BF16)
        eps = sb("eps", [P, 1])
        idx, pidx = sb("idx", [P, 4, TG], I32), sb("pidx", [P, 2, TG], I32)
        ea, scaled = sb("ea", [P, 4, GE]), sb("scaled", [P, 4, GE])
        mask = sb("mask", [6, 4, GE], BF16)
        y = sb("y", [P, 4, TG, H])
        z = sb("z", [P, 2, TG, H])
        st1, mv1 = sb("st1", [P, 2, TG, 6]), sb("mv1", [P, 2, TG, 2])
        sd1, rs1, nb1 = (sb(n, [P, 2, TG]) for n in ("sd1", "rs1", "nb1"))
        st2, mv2 = sb("st2", [P, 2, TG, 6]), sb("mv2", [P, 2, TG, 2])
        sd2, rs2 = (sb(n, [P, 2, TG]) for n in ("sd2", "rs2"))
        hid = sb("hid", [P, 2, 2, GE])
        half = sb("half", [P, 2, TG, O])
        c2 = sb("c2", [P, 2, TG, O])
        row = sb("row", [P, 2, TG, ROW])
        loads = [(w1b[64 * s:64 * s + 64, :], ins[f"L3_gnn_{n}_w1"][128:192, :]) for s, n in enumerate(("d2t", "t2d"))]
        raws = []
        for s, n in enumerate(("d2t", "t2d")):
            get = lambda v: ins[f"L3_gnn_{n}_{v}"]
            loads.append((w2[:, s, :, :], get("w2").rearrange("(c p) o -> p c o", p=P)))
            loads.append((gb[:, s, :, 0], get("g1").rearrange("(c p) -> p c", p=P)))
            loads.append((gb[:, s, :, 1], get("be1").rearrange("(c p) -> p c", p=P)))
            line = lambda v: get(v).rearrange("(a n) -> a n", a=1)
            raws += [(raw[s:s + 1, 0:256], line("b1")), (raw[s:s + 1, 256:384], line("g2")),
                     (raw[s:s + 1, 384:512], line("be2")), (raw2[:, 128 * s:128 * s + 128], line("b2"))]
        with nc.Block() as block:
            @block.sync
            def _(sp):
                for dst, src in raws:
                    sp.dma_start(dst, src).then_inc(s_raw, 16)
                for dst, src in loads:
                    sp.dma_start(dst, src, allow_slow_non_contiguous=True).then_inc(s_w, 16)
                sp.wait_ge(s_split, 2)
                for q in range(3):
                    for s in range(2):
                        sp.dma_start(vecs[3 * s + q:3 * s + q + 1, :], split[s:s + 1, q, :]).then_inc(s_parts, 16)
                    sp.dma_start(vecs2[q:q + 1, :], split2[:, q, :]).then_inc(s_parts, 16)
                sp.wait_ge(s_parts, 9 * 16)
                sp.wait_ge(s_w, 16 * len(loads))

            @block.vector
            def _(dve):
                link = linker(dve, s_c)
                dve.wait_ge(s_raw, 16 * len(raws))
                link(nc.vector.memset(ones[:], 1.0))
                link(nc.vector.memset(eps[:], EPS))
                for r, sp_ in ((raw, split), (raw2, split2)):
                    for q in range(3):
                        ins_ = nc.vector.tensor_copy(sp_[:, q, :], r[:])
                        link(ins_)
                        if q < 2:
                            link(nc.vector.tensor_tensor(r[:], r[:], sp_[:, q, :], ALU.subtract))
                nc.vector.tensor_copy(eps[:], eps[:]).then_inc(s_split, 2)

        block = ctx.enter_context(nc.Block())
        z_ps = [core.bank[0], core.bank[1]]
        t_ps = [core.bank[2], core.bank[3]]
        u_ps = [core.bank[4], core.bank[5]]
        g_ps = [core.bank[6], core.bank[7]]


        @block.sync
        def _(sp):
            def step(at):
                v, m = at(1), at(0)
                if v:
                    sp.wait_ge(S["z_ready"], v.back4)
                    sp.sem_inc(S["loads"], 1)
                if m:
                    sp.wait_ge(S["g_ready"], m.back4)
                for s in range(2):
                    if v:
                        half_rows = slice(64 * s, 64 * s + 64)
                        sp.dma_start(ea[half_rows, v.h4, :], ins["attr64T"][:, v.span(GE)]).then_inc(in_[v.h4], 16)
                        sp.dma_start(scaled[half_rows, v.h4, :], a.attn_rows[s:s + 1, v.span(GE)].broadcast_to(
                            [64, GE])).then_inc(in_[v.h4], 16)
                    if m:
                        sp.dma_start(mask[3 * s:3 * s + 3, m.h4, :], a.mask_rows[s:s + 1, m.span(GE)].broadcast_to(
                            [3, GE])).then_inc(mask_in[m.h4], 16)

            run(sp, step, ahead=1)

        @block.gpsimd
        def _(pool):
            def gather(k):
                pool.wait_ge(S["indices"], k.done)
                pool.sem_inc(S["turns"], 1)
                for j in range(TG):
                    nc.gpsimd.indirect_dma_start(y[:, k.h4, j, :], None, a.table, bass.IndirectOffsetOnAxis(
                        ap=idx[:, k.h4, j:j + 1], axis=0)).then_inc(rows_in[k.h4], 16)

            def scatter(k):
                pool.wait_ge(S["places"], k.done)
                pool.wait_ge(S["message"], k.done)
                pool.sem_inc(S["turns"], 1)
                for j in range(TG):
                    nc.gpsimd.indirect_dma_start(a.rows, bass.IndirectOffsetOnAxis(
                        ap=pidx[:, k.h2, j:j + 1], axis=0), row[:, k.h2, j, :], None).then_inc(sent[k.h2], 16)

            for h in range(2):
                for j in range(TG):
                    nc.gpsimd.dma_start(a.spare[h, j], a.pos[:, j:j + 1]).then_inc(sent[h], 16)

            def step(at):
                if at(2):
                    gather(at(2))
                if at(-3):
                    scatter(at(-3))

            run(pool, step, ahead=2, behind=3)
            for h in range(2):
                pool.wait_ge(sent[h], 64 + 64 * IT2)

        @block.tensor
        def _(pe):
            for n in ("z_ready", "turned", "u_ready", "g_ready"):
                pe.sem_inc(S[n], CREDIT)

            def turn(k):
                pe.wait_ge(S["normed1"], k.done)
                pe.wait_ge(S["hidden"], k.prev)
                for c in range(2):
                    for j in range(TG):
                        last = nc.tensor.transpose(t_ps[c][:, j * P:(j + 1) * P],
                                                   z[:, k.h2, j, c * P:(c + 1) * P], t.ident[:])
                last.then_inc(S["turned"], 1)

            def first_product(k):
                pe.wait_ge(S["scaled"], k.done)
                pe.wait_ge(mask_in[k.h4], k.landed(2))
                pe.wait_ge(S["z_copied"], k.prev)
                for j in range(TG):
                    o = z_ps[j // 2][:, H * (j % 2):H * (j % 2) + H]
                    e = slice(j * P, (j + 1) * P)
                    nc.tensor.matmul(o, scaled[:, k.h4, e], w1b[:], start=True, stop=False)
                    last = nc.tensor.matmul(o, mask[:, k.h4, e], vecs[:, 0:H], start=False, stop=True)
                last.then_inc(S["z_ready"], 1)

            def second_product(k):
                pe.wait_ge(S["hidden"], k.done)
                pe.wait_ge(S["comb"], k.prev)
                for j in range(TG):
                    e = slice(j * P, (j + 1) * P)
                    o = u_ps[j // 2][:, 2 * O * (j % 2):2 * O * (j % 2) + 2 * O]
                    for s in range(2):
                        for c in range(2):
                            nc.tensor.matmul(o[:, s * O:(s + 1) * O], hid[:, s, c, e], w2[:, s, c, :],
                                             start=(j % 2 == 0 and s == 0 and c == 0), stop=False,
                                             skip_group_check=True)
                    last = nc.tensor.matmul(o, ones[:], vecs2[:], start=False, stop=True, skip_group_check=True)
                last.then_inc(S["u_ready"], 1)

            def gains(k):
                pe.wait_ge(S["gained"], k.prev)
                for j in range(TG):
                    o = g_ps[j // 2][:, 2 * O * (j % 2):2 * O * (j % 2) + 2 * O]
                    last = nc.tensor.matmul(o, mask[:, k.h4, j * P:(j + 1) * P], vecs[:, H:2 * H], start=True,
                                            stop=True)
                last.then_inc(S["g_ready"], 1)

            def step(at):
                if at(-1):
                    turn(at(-1))
                if at(1):
                    first_product(at(1))
                if at(-1):
                    second_product(at(-1))
                    gains(at(-1))

            run(pe, step, ahead=1, behind=1)

        @block.scalar
        def _(act):
            for n in ("std1", "normed1", "hidden", "half", "std2", "message", "indices", "places"):
                act.sem_inc(S[n], CREDIT)

            def indices(k):
                act.wait_ge(S["z_copied"], k.back4)
                nc.scalar.copy(idx[:, k.h4, :], a.yidx[:, k.span(TG)]).then_inc(S["indices"], 1)

            def message(k):
                act.wait_ge(S["gained"], k.done)
                act.wait_ge(sent[k.h2], k.landed2(4))
                nc.scalar.copy(pidx[:, k.h2, :], a.pos[:, k.span(TG)]).then_inc(S["places"], 1)
                nc.scalar.activation(row[:, k.h2, :, 0:O], c2[:, k.h2, :, :], ACT.Relu)
                nc.scalar.copy(row[:, k.h2, :, O:ROW], a.meta[:, k.span(TG), :]).then_inc(S["message"], 1)

            def hidden(k):
                act.wait_ge(S["turned"], k.done)
                act.wait_ge(S["u_ready"], k.prev)
                for s in range(2):
                    for c in range(2):
                        last = nc.scalar.activation(hid[:, s, c, :], t_ps[c][:, :], ACT.Relu,
                                                    scale=gb[:, s, c, 0:1], bias=gb[:, s, c, 1:2])
                last.then_inc(S["hidden"], 1)

            def deviation(k, sd, mv, stats, used, ready):
                act.wait_ge(S[stats], k.done)
                act.wait_ge(S[used], k.back2)
                nc.scalar.activation(sd[:, k.h2, :], mv[:, k.h2, :, 1], ACT.Sqrt, bias=eps[:, 0:1]).then_inc(S[ready], 1)

            def normalize(k):
                act.wait_ge(S["rstd1"], k.done)
                for j in range(TG):
                    last = nc.scalar.activation(z[:, k.h2, j, :], z[:, k.h2, j, :], ACT.Identity,
                                                scale=rs1[:, k.h2, j:j + 1], bias=nb1[:, k.h2, j:j + 1])
                last.then_inc(S["normed1"], 1)

            def take_half(k):
                act.wait_ge(S["u_ready"], k.done)
                act.wait_ge(S["gained"], k.back2)
                for j in range(TG):
                    o = u_ps[j // 2][:, 2 * O * (j % 2):2 * O * (j % 2) + O]
                    last = nc.scalar.activation(half[:, k.h2, j, :], o, ACT.Copy,
                                                scale=a.meta[:, k.span(TG, j, 1), 1])
                last.then_inc(S["half"], 1)

            def step(at):
                if at(-1):
                    hidden(at(-1))
                if at(-3):
                    message(at(-3))
                if at(3):
                    indices(at(3))
                if at(0):
                    deviation(at(0), sd1, mv1, "stats1", "rstd1", "std1")
                if at(-2):
                    deviation(at(-2), sd2, mv2, "stats2", "rstd2", "std2")
                if at(0):
                    normalize(at(0))
                if at(-1):
                    take_half(at(-1))

            run(act, step, ahead=3, behind=3)

        @block.vector
        def _(dve):
            for n in ("scaled", "z_copied", "bn1", "stats1", "recip1", "rstd1", "comb", "bn2", "stats2", "rstd2",
                      "centered", "gained"):
                dve.sem_inc(S[n], CREDIT)
            tt, stt = nc.vector.tensor_tensor, nc.vector.scalar_tensor_tensor

            def scale(k, part):
                e = slice(part * GE // 2, (part + 1) * GE // 2)
                dve.wait_ge(in_[k.h4], k.landed(4))
                last = tt(scaled[:, k.h4, e], ea[:, k.h4, e], scaled[:, k.h4, e], ALU.mult)
                if part == 1:
                    last.then_inc(S["scaled"], 1)

            def add_rows(k):
                dve.wait_ge(S["z_ready"], k.done)
                dve.wait_ge(rows_in[k.h4], k.landed(4))
                dve.wait_ge(S["turned"], k.back2)
                for j in range(TG):
                    last = stt(out=z[:, k.h2, j, :], in0=y[:, k.h4, j, :], scalar=a.attn[:, k.span(TG, j, 1)],
                               in1=z_ps[j // 2][:, H * (j % 2):H * (j % 2) + H], op0=ALU.mult, op1=ALU.add)
                last.then_inc(S["z_copied"], 1)

            def statistics(k, st, v, bn, tiles):
                for j in tiles:
                    last = nc.vector.bn_stats(st[:, k.h2, j, :], v[:, k.h2, j, :])
                if j == TG - 1:
                    last.then_inc(S[bn], 1)

            def moments(k, st, mv, stats):
                for j in range(TG):
                    last = nc.vector.bn_aggr(mv[:, k.h2, j, :], st[:, k.h2, j, :])
                last.then_inc(S[stats], 1)

            def minus_mean(k):
                dve.wait_ge(S["recip1"], k.done)
                stt(out=nb1[:, k.h2, :], in0=mv1[:, k.h2, :, 0], scalar=-1.0, in1=rs1[:, k.h2, :], op0=ALU.mult,
                    op1=ALU.mult).then_inc(S["rstd1"], 1)

            def combine(k):
                dve.wait_ge(S["half"], k.done)
                dve.wait_ge(S["message"], k.back2)
                for j in range(TG):
                    last = stt(out=c2[:, k.h2, j, :], in0=u_ps[j // 2][:, 2 * O * (j % 2) + O:2 * O * (j % 2 + 1)],
                               scalar=a.meta[:, k.span(TG, j, 1), 2], in1=half[:, k.h2, j, :], op0=ALU.mult,
                               op1=ALU.add)
                last.then_inc(S["comb"], 1)

            def center_and_gain(k, tiles):
                for j in tiles:
                    G = g_ps[j // 2][:, 2 * O * (j % 2):2 * O * (j % 2) + O]
                    last = stt(out=half[:, k.h2, j, :], in0=c2[:, k.h2, j, :], scalar=mv2[:, k.h2, j, 0:1], in1=G,
                               op0=ALU.subtract, op1=ALU.mult)
                if j == TG - 1:
                    last.then_inc(S["centered"], 1)

            def scale_and_offset(k):
                dve.wait_ge(S["rstd2"], k.done)
                dve.wait_ge(S["centered"], k.done)
                for j in range(TG):
                    B = g_ps[j // 2][:, 2 * O * (j % 2) + O:2 * O * (j % 2 + 1)]
                    last = stt(out=c2[:, k.h2, j, :], in0=half[:, k.h2, j, :], scalar=rs2[:, k.h2, j:j + 1], in1=B,
                               op0=ALU.mult, op1=ALU.add)
                last.then_inc(S["gained"], 1)

            def step(at):
                k, p = at(0), at(-2)
                if k:
                    add_rows(k)
                if p:
                    combine(p)
                if k:
                    dve.wait_ge(S["z_copied"], k.done)
                    statistics(k, st1, z, "bn1", range(TG))
                if p:
                    dve.wait_ge(S["comb"], p.done)
                    statistics(p, st2, c2, "bn2", [0])
                if k:
                    dve.wait_ge(S["bn1"], k.done)
                if p:
                    statistics(p, st2, c2, "bn2", range(1, TG))
                if k:
                    moments(k, st1, mv1, "stats1")
                if p:
                    dve.wait_ge(S["bn2"], p.done)
                if at(2):
                    scale(at(2), 0)
                if p:
                    moments(p, st2, mv2, "stats2")
                if k:
                    dve.wait_ge(S["std1"], k.done)
                    nc.vector.reciprocal(rs1[:, k.h2, :], sd1[:, k.h2, :]).then_inc(S["recip1"], 1)
                if p:
                    dve.wait_ge(S["stats2"], p.done)
                    dve.wait_ge(S["g_ready"], p.done)
                    center_and_gain(p, [0])
                if k:
                    minus_mean(k)
                if p:
                    center_and_gain(p, [1, 2])
                    dve.wait_ge(S["std2"], p.done)
                    nc.vector.reciprocal(rs2[:, p.h2, :], sd2[:, p.h2, :]).then_inc(S["rstd2"], 1)
                    center_and_gain(p, [3])
                if at(2):
                    scale(at(2), 1)
                if p:
                    scale_and_offset(p)

            run(dve, step, ahead=2, behind=2)


def flow_sums(core, t, ins, a):
    nc = core.nc
    H = 128
    S = {n: core.sem(f"a3_{n}") for n in ("rel", "eq", "hot", "sums", "added", "mixed", "mixed_copied", "turned",
                                          "own")}
    in_ = [core.sem(f"a3_loaded{h}") for h in range(4)]
    s_init, s_win, s_w = core.sem("a3_init"), core.sem("a3_windows"), core.sem("a3_weights")
    with ExitStack() as ctx:
        sb = lambda n, s, d=F32: core.sb(f"a3_{n}", s, d, ctx)
        acc = sb("acc", [P, 2, NP])
        flow = sb("flow", [P, NT, H])
        rowb = sb("rowb", [P, 3, H])
        nw = sb("nw", [P, 2, H])
        with ExitStack() as ectx:
            row = core.sb("a3_row", [P, 4, TG, ROW], F32, ectx)
            rel = core.sb("a3_rel", [P, 2, TG], F32, ectx)
            eq = core.sb("a3_eq", [P, 2, TG, AWIN], F32, ectx)
            hot = core.sb("a3_hot", [P, 2, TG, 2, AWIN], F32, ectx)
            iota = core.sb("a3_iota", [P, AWIN], F32, ectx)
            win = core.sb("a3_win", [1, NG], I32, ectx)
            block = ectx.enter_context(nc.Block())
            o = [core.bank[0], core.bank[1]]

            def passes(eng, step, ahead=0, behind=0):
                count = eng.value_load(a.passes[0:1, 0:1], min_val=1, max_val=NBIN)
                with eng.Fori(0, count) as p:
                    run(eng, step, ahead, behind, base=eng.snap(p * IT))

            @block.sync
            def _(sp):
                rows = a.rows.rearrange("(g p j) c -> g p (j c)", p=P, j=TG)

                def step(at):
                    k = at(0)
                    sp.wait_ge(S["sums"], k.back4)
                    sp.dma_start(row[:, k.h4, :, :].rearrange("p j c -> p (j c)"),
                                 rows[k.span(1)].rearrange("a p f -> (a p) f")).then_inc(in_[k.h4], 16)

                passes(sp, step)

            @block.tensor
            def _(pe):
                pe.sem_inc(S["sums"], CREDIT)

                def step(at):
                    k = at(0)
                    pe.wait_ge(S["hot"], k.done)
                    pe.wait_ge(in_[k.h4], k.landed(1))
                    pe.wait_ge(S["added"], k.back2)
                    for j in range(TG):
                        last = nc.tensor.matmul(o[k.h2][:, 0:2 * AWIN], row[:, k.h4, j, 0:H],
                                                hot[:, k.h2, j, :, :].rearrange("p s w -> p (s w)"),
                                                start=j == 0, stop=j == TG - 1)
                    last.then_inc(S["sums"], 1)

                passes(pe, step)

            @block.gpsimd
            def _(pool):
                nc.gpsimd.memset(acc[:, 1, :], 0.0).then_inc(s_init, 1)

            @block.vector
            def _(dve):
                nc.vector.memset(acc[:, 0, :], 0.0).then_inc(s_init, 1)
                nc.vector.tensor_copy(iota[:], a.iota[:, 0:AWIN]).then_inc(s_win, 1)
                nc.vector.tensor_copy(win[:], a.win0[:]).then_inc(s_win, 1)
                dve.wait_ge(s_win, 2)
                dve.wait_ge(s_init, 2)
                for n in ("rel", "eq", "hot", "added"):
                    dve.sem_inc(S[n], CREDIT)

                def relative(k):
                    dve.wait_ge(in_[k.h4], k.landed(1))
                    dve.wait_ge(S["eq"], k.back2)
                    nc.vector.tensor_scalar(rel[:, k.h2, :], row[:, k.h4, :, H], a.baseB[:, k.span(1)], None,
                                            ALU.subtract).then_inc(S["rel"], 1)

                def compare(k):
                    dve.wait_ge(S["rel"], k.done)
                    dve.wait_ge(S["hot"], k.back2)
                    nc.vector.tensor_tensor(eq[:, k.h2], iota[:].unsqueeze(1).broadcast_to([P, TG, AWIN]),
                                            rel[:, k.h2, :].unsqueeze(2).broadcast_to([P, TG, AWIN]),
                                            ALU.is_equal).then_inc(S["eq"], 1)

                def one_hots(k):
                    dve.wait_ge(S["eq"], k.done)
                    dve.wait_ge(S["sums"], k.back2)
                    nc.vector.tensor_tensor(
                        hot[:, k.h2], eq[:, k.h2].unsqueeze(2).broadcast_to([P, TG, 2, AWIN]),
                        row[:, k.h4, :, H + 1:H + 3].unsqueeze(3).broadcast_to([P, TG, 2, AWIN]),
                        ALU.mult).then_inc(S["hot"], 1)

                def add_sums(k, at):
                    dve.wait_ge(S["sums"], k.done)
                    dve.wait_ge(S["added"], k.prev)
                    w = acc[:, :, ds(at, AWIN)]
                    nc.vector.tensor_tensor(w, w, o[k.h2][:, 0:2 * AWIN].rearrange("p (s w) -> p s w", s=2),
                                            ALU.add).then_inc(S["added"], 1)

                def step(at):
                    if at(1):
                        relative(at(1))
                        compare(at(1))
                    if at(-1):
                        begin = dve.value_load(win[0:1, at(-1).span(1)], min_val=0, max_val=NP - AWIN)
                    if at(1):
                        one_hots(at(1))
                    if at(-1):
                        add_sums(at(-1), begin)

                count = dve.value_load(a.passes[0:1, 0:1], min_val=1, max_val=NBIN)
                with dve.Fori(0, count) as p:
                    run(dve, step, ahead=1, behind=1, base=dve.snap(p * IT))
                    nc.vector.tensor_scalar(iota[:], iota[:], float(AWIN), None, ALU.add).then_inc(s_win, 1)
                    nc.vector.tensor_scalar(win[:], win[:], AWIN, NP - AWIN, ALU.add, ALU.min).then_inc(s_win, 1)
                    dve.wait_ge(s_win, p * 2 + 4)

        oT = sb("oT", [P, NB * P])
        halfn = NB * P // 2
        m_ps = [core.bank[0], core.bank[1]]
        with nc.Block() as block:
            @block.sync
            def _(sp):
                sp.dma_start(nw[:, 1, :], ins["L3_gnn_node_w"][0:P, :]).then_inc(s_w, 16)
                sp.dma_start(nw[:, 0, :], ins["L3_gnn_node_w"][P:2 * P, :]).then_inc(s_w, 16)
                for q, n in enumerate(("node_b", "node_g", "node_be")):
                    sp.dma_start(rowb[:, q, :], ins[f"L3_gnn_{n}"].rearrange("(a n) -> a n", a=1).broadcast_to(
                        [P, H])).then_inc(s_w, 16)
                sp.wait_ge(s_w, 80)

            @block.tensor
            def _(pe):
                pe.wait_ge(s_w, 80)
                pe.sem_inc(S["turned"], 1)
                with pe.Fori(0, NI) as i:
                    pe.wait_ge(S["mixed_copied"], i + 1)
                    for q in range(2):
                        for s in range(2):
                            last = nc.tensor.matmul(m_ps[q][:, 0:halfn], nw[:, s, :],
                                                    acc[:, s, ds(i * NB * P + q * halfn, halfn)], start=s == 0,
                                                    stop=s == 1)
                    last.then_inc(S["mixed"], 1)
                    pe.wait_ge(S["mixed_copied"], i + 2)
                    pe.wait_ge(S["own"], i + 1)
                    for u in range(NB):
                        last = nc.tensor.transpose(core.bank[2 + u // 4][:, P * (u % 4):P * (u % 4) + P],
                                                   oT[:, u * P:(u + 1) * P], t.ident[:])
                    last.then_inc(S["turned"], 1)

            @block.scalar
            def _(act):
                act.sem_inc(S["mixed_copied"], 1)
                with act.Fori(0, NI) as i:
                    act.wait_ge(S["mixed"], i + 1)
                    act.wait_ge(S["turned"], i + 1)
                    for q in range(2):
                        last = nc.scalar.copy(oT[:, q * halfn:(q + 1) * halfn], m_ps[q][:, 0:halfn])
                    last.then_inc(S["mixed_copied"], 1)

            @block.vector
            def _(dve):
                dve.sem_inc(S["own"], 1)
                with dve.Fori(0, NI) as i:
                    dve.wait_ge(S["turned"], i + 2)
                    nc.vector.tensor_copy(flow[:, ds(i * NB, 4), :],
                                          core.bank[2][:, :].rearrange("p (u n) -> p u n", u=4))
                    nc.vector.tensor_copy(flow[:, ds(i * NB + 4, 1), :].rearrange("p a c -> p (a c)"),
                                          core.bank[3][:, 0:P]).then_inc(S["own"], 1)

        add_block(core, t, "node", flow, rowb)


def flow_attention(core, t, ins, order):
    nc = core.nc
    a = Bundle()
    a.table = nc.dram_tensor("flow_table_dram", [2 * NP, 256], F32).ap()
    a.rows = nc.dram_tensor("message_rows_dram", [EP, ROW], F32).ap()
    a.low_rows = nc.dram_tensor("low_rows_dram", [2, EP], BF16).ap()
    a.mask_rows = nc.dram_tensor("mask_rows_dram", [2, EP], BF16).ap()
    a.attn_rows = nc.dram_tensor("attn_rows_dram", [2, EP], F32).ap()
    a.spare = nc.dram_tensor("spare_dram", [2, TG, P, 1], I32).ap()
    a.base_dram = nc.dram_tensor("source_base_dram", [NG], F32).ap()
    with ExitStack() as ctx:
        sb = lambda n, s, d=F32: core.sb(f"a_{n}", s, d, ctx)
        a.parts = sb("parts", [P, NT, 2])
        a.iota = sb("iota", [P, P])
        a.iotaP, a.iotaP_int = sb("iotaP", [P, 1]), sb("iotaP_int", [P, 1], I32)
        a.meta = sb("meta", [P, ET, 4])
        a.attn = sb("attn", [P, ET])
        a.logit = a.attn
        a.yidx, a.pos = sb("yidx", [P, ET], I32), sb("pos", [P, ET], I32)
        a.baseB, a.win0 = sb("baseB", [P, NG]), sb("win0", [1, NG], I32)
        a.passes = sb("passes", [1, 1], I32)
        attention_nodes(core, t, ins, a)
        with ExitStack() as ectx:
            a.high = core.sb("a_high", [P, ET, 2], F32, ectx)
            edge_masks(core, t, ins, a)
            logits(core, t, ins, a)
            softmax(core, t, ins, a)
            source_windows(core, t, a, order)
        messages(core, t, ins, a)
        flow_sums(core, t, ins, a)


def store(core, t, out):
    nc = core.nc
    s_out = core.sem("result_stored")
    whole = N // P
    with nc.Block() as block:
        @block.sync
        def _(sp):
            sp.dma_start(out[0:whole * P, :].rearrange("(t p) d -> p t d", p=P), t.x[:, 0:whole, :]).then_inc(
                s_out, 16)
            sp.dma_start(out[whole * P:N, :], t.x[0:N - whole * P, whole, :]).then_inc(s_out, 16)
            sp.wait_ge(s_out, 32)


def program(nc, ins, out, layers=4):
    with ExitStack() as ctx:
        core = Core(nc, ctx)
        t = Bundle()
        t.table = nc.dram_tensor("table_dram", [NP, D], F32).ap()
        with core.semaphores():
            prepare(core, t, ins)
        for layer in range(min(layers, 3)):
            if layer == 1:
                order = order_tensors(core)
                zeroed, loads, scales = weights_later(core, t.w, ins)
            with ExitStack() as lctx, core.semaphores():
                acc = Bundle()
                sb = lambda n, s: core.sb(f"l{layer}_{n}", s, F32, lctx)
                if layer == 1:
                    hR = sb("h", [P, NT, D])
                    table_plain(core, t, "t1", hR, zeroed)
                    count_bins(core, t, order, lctx)
                    acc.S, acc.V = sb("acc_s", [64, 4, NP]), sb("acc_v", [96, 4, NP])
                    acc.halves = [[acc.S[:]], [acc.V[:]]]
                    edge_sums(core, t, "e1", acc, extra=loads, order=order)
                    scale_weights(core, "w", zeroed, scales)
                    finish_product(core, t, "f1", acc, t.w.post1, hR)
                    continue
                pre, post, fc, attrT, n_sc = ((t.w.pre0, t.w.post0, t.w.fc0, ins["attr64T"], 96) if layer == 0 else
                                              (t.w.pre2, t.w.post2, t.w.fc2, ins["attr8T"], 64))
                t.sc = sb("sc", [P, NT, n_sc + 96])
                node_tables(core, t, f"t{layer}", pre, n_sc)
                acc.A, acc.B, acc.C = sb("acc_a", [P, 3, NP]), sb("acc_b", [96, NP]), sb("acc_c", [96, NP])
                acc.halves = [[acc.A[:]], [acc.B[:], acc.C[:]]]
                if layer == 0:
                    acc.X = sb("acc_x", [96, 3, NP])
                    acc.halves[1].append(acc.X[:])
                mlp = Bundle()
                mlp.w, mlp.attrT = fc, attrT
                mlp.rin, mlp.kinds, mlp.width = (64, 3, 224) if layer == 0 else (8, 2, 192)
                mlp.scale = 1 / math.sqrt(mlp.rin)
                edge_sums(core, t, f"e{layer}", acc, mlp)
                finish_gated(core, t, f"f{layer}", acc, post, layer == 2)
        with core.semaphores(again=False):
            if layers > 3:
                flow_attention(core, t, ins, order)
            store(core, t, out)


LAYERS = 4


def kernel(**inputs):
    import concourse.bacc as _bacc
    from concourse import mybir as _mybir
    from concourse.bass_utils import run_bass_kernel_spmd as _run

    nc = _bacc.Bacc("TRN2", target_bir_lowering=False, num_devices=1)
    arrays = {k: np.asarray(v) for k, v in inputs.items() if k.startswith("L")}
    pad = ((0, EP - E), (0, 0))
    x = np.asarray(inputs["x"])
    src = np.pad(np.asarray(inputs["src"]), (0, EP - E), constant_values=N - 1)
    dst = np.pad(np.asarray(inputs["dst"]), (0, EP - E), constant_values=N - 1)
    arrays["x_pad"] = np.pad(x, ((0, NP - N), (0, 0)))
    arrays["attr_pt"] = np.pad(np.asarray(inputs["node_vec1"])[:, 0], (0, NP - N)).reshape(NT, P).T
    arrays["src_pt"], arrays["dst_pt"] = src.reshape(ET, P).T, dst.reshape(ET, P).T
    arrays["src_rows"], arrays["dst_rows"] = src.reshape(NG, GE), dst.reshape(NG, GE)
    arrays["e4_pt"] = np.pad(np.asarray(inputs["edge_attr_4"]), pad).reshape(ET, P, 4).transpose(1, 0, 2).reshape(
        P, ET * 4)
    arrays["attr64T"] = np.pad(np.asarray(inputs["edge_attr_64"]), pad).T
    arrays["attr8T"] = np.pad(np.asarray(inputs["edge_attr_8"]), pad).T
    arrays = {k: np.ascontiguousarray(v) for k, v in arrays.items()}
    ins = {k: nc.dram_tensor(f"in_{k}", v.shape, _mybir.dt.from_np(v.dtype), kind="ExternalInput").ap()
           for k, v in arrays.items()}
    out = nc.dram_tensor("result", (N, D), F32, kind="ExternalOutput").ap()
    program(nc, ins, out, LAYERS)
    r = _run(nc, [{f"in_{k}": v for k, v in arrays.items()}], core_ids=[0])
    return r.results[0]["result"]
```
